# Optimizing a Trainium2 kernel written in Bass

```python
import numpy as np
import jax
import jax.numpy as jnp

def _softmax(x, axis=-1):
    return jax.nn.softmax(x, axis=axis)

def _gelu(x):
    return jax.nn.gelu(x, approximate=True)

def _silu(x):
    return jax.nn.silu(x)

def _sigmoid(x):
    return jax.nn.sigmoid(x)

def _layernorm(x, axis=-1, eps=1e-05):
    m = jnp.mean(x, axis=axis, keepdims=True)
    v = jnp.var(x, axis=axis, keepdims=True)
    return (x - m) / jnp.sqrt(v + eps)

def _scatter_add(tgt, idx, src, axis=0):
    return tgt.at[idx].add(src)

def _segment_sum(src, seg, n):
    return jax.ops.segment_sum(src, seg, n)
kernel_name = 'mk_seq_preln_d4_jaxref_r8_807229'

def setup_inputs(seed: int=0):
    np.random.seed(seed)
    _w = jnp.asarray

    def _L0_attn_setup():
        import jax, jax.numpy as jnp
        import numpy as np
        import math
        D_MODEL = 128
        N_HEADS = 16
        HEAD_DIM = D_MODEL // N_HEADS

        def _apply_rope_full(x):
            B, S, D = x.shape
            half = D // 2
            pos = jnp.arange(S, dtype=jnp.float32)[:, None]
            freqs = 1.0 / 10000.0 ** (jnp.arange(half, dtype=jnp.float32) / half)
            ang = pos * freqs[None, :]
            sin, cos = (jnp.sin(ang), jnp.cos(ang))
            x1, x2 = (x[..., :half], x[..., half:])
            return jnp.concatenate([x1 * cos - x2 * sin, x1 * sin + x2 * cos], axis=-1)

        def _alibi_slopes(n_heads):
            return jnp.array([2.0 ** (-8.0 * (i + 1) / n_heads) for i in range(n_heads)], dtype=jnp.float32)
        key = jax.random.key(seed)
        ks = jax.random.split(key, 5)
        B, S, D = (2, 256, D_MODEL)
        scale = 1.0 / math.sqrt(D)
        return {'x': jax.random.normal(ks[0], (B, S, D), dtype=jnp.float32), 'wq': jax.random.normal(ks[1], (D, D), dtype=jnp.float32) * scale, 'wk': jax.random.normal(ks[2], (D, D), dtype=jnp.float32) * scale, 'wv': jax.random.normal(ks[3], (D, D), dtype=jnp.float32) * scale, 'out_w': jax.random.normal(ks[4], (D, D), dtype=jnp.float32) * scale, 'out_b': jnp.zeros((D,), dtype=jnp.float32)}
    _L0_attn_in = _L0_attn_setup()

    def _L0_ffn_setup():
        import jax, jax.numpy as jnp
        import numpy as np
        DIM = 128
        DEPTH = 6
        HEADS = 16
        DIM_HEAD = 64
        WINDOW = 32
        INNER = HEADS * DIM_HEAD
        DIM_INNER = int(DIM * 4 * 2 / 3)
        QK_SCALE = 8.0

        def shift_tokens(t):
            a, s = jnp.split(t, 2, -1)
            s = jnp.pad(s, ((0, 0), (1, 0), (0, 0)))[:, :-1]
            return jnp.concatenate([a, s], -1)

        def l2norm(t):
            return t / jnp.maximum(jnp.linalg.norm(t, axis=-1, keepdims=True), 1e-12)

        def rotate_half(x):
            x1, x2 = jnp.split(x, 2, -1)
            return jnp.concatenate([-x2, x1], -1)

        def rotary_tables(n):
            half = jnp.arange(0, DIM_HEAD, 2, dtype=jnp.float32)
            inv_freq = 1.0 / 10000.0 ** (half / DIM_HEAD)
            t = jnp.arange(n, dtype=jnp.float32)
            freqs = t[:, None] * inv_freq[None, :]
            freqs = jnp.concatenate([freqs, freqs], -1)
            base_scale = (half + 0.4 * DIM_HEAD) / (1.4 * DIM_HEAD)
            power = (t - n // 2) / (WINDOW // 2)
            scale = base_scale[None, :] ** power[:, None]
            scale = jnp.concatenate([scale, scale], -1)
            return (freqs, scale)

        def local_attention(q, k, v):
            b, h, n, d = q.shape
            w = WINDOW
            nw = n // w
            bq = q.reshape(b, h, nw, w, d)
            bk = k.reshape(b, h, nw, w, d)
            bv = v.reshape(b, h, nw, w, d)

            def look(t):
                p = jnp.pad(t, ((0, 0), (0, 0), (1, 0), (0, 0), (0, 0)))
                return jnp.concatenate([p[:, :, :nw], p[:, :, 1:]], axis=3)
            bk2, bv2 = (look(bk), look(bv))
            seq = jnp.arange(n).reshape(nw, w)
            seq_p = jnp.pad(seq, ((1, 0), (0, 0)), constant_values=-1)
            jt = jnp.concatenate([seq_p[:nw], seq_p[1:]], axis=1)
            it = seq[:, :, None]
            jb = jt[:, None, :]
            mask = (it < jb) | (it > jb + w) | (jb == -1)
            sim = jnp.einsum('bhwie,bhwje->bhwij', bq, bk2) * QK_SCALE
            sim = jnp.where(mask, -jnp.finfo(sim.dtype).max, sim)
            attn = jax.nn.softmax(sim, -1)
            out = jnp.einsum('bhwij,bhwje->bhwie', attn, bv2)
            return out.reshape(b, h, n, d)

        def attn_layer(x, Wqkv, qs, ksc, Wo):
            b, n, _ = x.shape
            qkv = x @ Wqkv
            q, k, v = jnp.split(qkv, 3, -1)
            sh = lambda t: t.reshape(b, n, HEADS, DIM_HEAD).transpose(0, 2, 1, 3)
            q, k, v = (sh(q), sh(k), sh(v))
            q = l2norm(q) * qs
            k = l2norm(k) * ksc
            freqs, scale = rotary_tables(n)
            cos, sin = (jnp.cos(freqs), jnp.sin(freqs))
            q = q * cos * scale + rotate_half(q) * sin * scale
            inv = 1.0 / scale
            k = k * cos * inv + rotate_half(k) * sin * inv
            out = local_attention(q, k, v)
            out = out.transpose(0, 2, 1, 3).reshape(b, n, INNER)
            return out @ Wo

        def ffn_layer(x, g, bln, W1, b1, W2, b2):
            mu = x.mean(-1, keepdims=True)
            var = ((x - mu) ** 2).mean(-1, keepdims=True)
            xn = (x - mu) / jnp.sqrt(var + 1e-05) * g + bln
            hg = xn @ W1 + b1
            a, gate = jnp.split(hg, 2, -1)
            return a * jax.nn.gelu(gate, approximate=False) @ W2 + b2
        key = jax.random.key(seed)
        ks = jax.random.split(key, 8)
        B, N = (2, 256)
        init = lambda k, shape: jax.random.normal(k, shape, jnp.float32) * 0.02
        return {'x': jax.random.normal(ks[0], (B, N, DIM), jnp.float32), 'Wqkv': init(ks[1], (DEPTH, DIM, 3 * INNER)), 'q_scale': jnp.ones((DEPTH, DIM_HEAD), jnp.float32), 'k_scale': jnp.ones((DEPTH, DIM_HEAD), jnp.float32), 'Wo': init(ks[2], (DEPTH, INNER, DIM)), 'ln_g': jnp.ones((DEPTH, DIM), jnp.float32), 'ln_b': jnp.zeros((DEPTH, DIM), jnp.float32), 'W1': init(ks[3], (DEPTH, DIM, 2 * DIM_INNER)), 'b1': jnp.zeros((DEPTH, 2 * DIM_INNER), jnp.float32), 'W2': init(ks[4], (DEPTH, DIM_INNER, DIM)), 'b2': jnp.zeros((DEPTH, DIM), jnp.float32)}
    _L0_ffn_in = _L0_ffn_setup()

    def _L1_attn_setup():
        import jax, jax.numpy as jnp
        import numpy as np
        B, S, H, D = (4, 256, 128, 128)
        key = jax.random.key(seed)
        k0, k1, k2, k3 = jax.random.split(key, 4)
        x = jax.random.normal(k0, (B, S, H), dtype=jnp.float32)
        scale = 1.0 / np.sqrt(H)
        Wq = jax.random.normal(k1, (D, H), dtype=jnp.float32) * scale
        Wk = jax.random.normal(k2, (D, H), dtype=jnp.float32) * scale
        Wv = jax.random.normal(k3, (D, H), dtype=jnp.float32) * scale
        return {'x': x, 'Wq': Wq, 'Wk': Wk, 'Wv': Wv}
    _L1_attn_in = _L1_attn_setup()

    def _L1_ffn_setup():
        import jax, jax.numpy as jnp
        import numpy as np
        B, S, D, E = (4, 512, 128, 8)
        key = jax.random.key(seed)
        k1, k2, k3, k4, k5 = jax.random.split(key, 5)
        scale = 1.0 / np.sqrt(D)
        return {'x': jax.random.normal(k1, (B, S, D), dtype=jnp.float32), 'Wg': jax.random.normal(k2, (D, D), dtype=jnp.float32) * scale, 'bg': jnp.zeros((D,), dtype=jnp.float32), 'We': jax.random.normal(k3, (E, D, D), dtype=jnp.float32) * scale, 'be': jnp.zeros((E, D), dtype=jnp.float32)}
    _L1_ffn_in = _L1_ffn_setup()

    def _L2_attn_setup():
        import jax, jax.numpy as jnp
        import numpy as np
        DT_MIN, DT_MAX = (0.001, 0.1)
        CHUNK = 64
        key = jax.random.key(seed)
        ks = jax.random.split(key, 8)
        b, L, D = (2, 512, 128)
        d_inner, d_state, nheads, K = (256, 128, 32, 4)
        conv_dim = d_inner + 2 * d_state
        d_in_proj = 2 * d_inner + 2 * d_state + nheads
        f32 = jnp.float32
        return {'x': jax.random.normal(ks[0], (b, L, D), f32), 'in_proj_w': jax.random.normal(ks[1], (d_in_proj, D), f32) * D ** (-0.5), 'conv_w': jax.random.normal(ks[2], (conv_dim, K), f32) * 0.3, 'conv_b': jnp.zeros((conv_dim,), f32), 'dt_bias': jax.random.normal(ks[3], (nheads,), f32) * 0.5, 'A_log': jnp.log(jax.random.uniform(ks[4], (nheads,), f32, 1.0, 16.0)), 'D_skip': jnp.ones((nheads,), f32), 'norm_w': jnp.ones((d_inner,), f32), 'out_proj_w': jax.random.normal(ks[5], (D, d_inner), f32) * d_inner ** (-0.5), 'ln_w': jnp.ones((D,), f32), 'ln_b': jnp.zeros((D,), f32)}
    _L2_attn_in = _L2_attn_setup()

    def _L2_ffn_setup():
        import jax, jax.numpy as jnp
        import numpy as np
        E = 8
        C = 160
        D = 128
        H = 512
        B, S = (4, 256)
        key = jax.random.key(seed)
        ks = jax.random.split(key, 12)
        sc = 0.02
        return {'input': jax.random.normal(ks[0], (B, S, D), jnp.float32), 'router_w': jax.random.normal(ks[1], (D, E), jnp.float32) * sc, 'router_b': jnp.zeros((E,), jnp.float32), 'w1': jax.random.normal(ks[2], (E, D, H), jnp.float32) * sc, 'b1': jnp.zeros((E, H), jnp.float32), 'w2': jax.random.normal(ks[3], (E, H, D), jnp.float32) * sc, 'b2': jnp.zeros((E, D), jnp.float32), 'ow1': jax.random.normal(ks[4], (D, H), jnp.float32) * sc, 'ob1': jnp.zeros((H,), jnp.float32), 'ow2': jax.random.normal(ks[5], (H, D), jnp.float32) * sc, 'ob2': jnp.zeros((D,), jnp.float32)}
    _L2_ffn_in = _L2_ffn_setup()

    def _L3_attn_setup():
        import jax, jax.numpy as jnp
        import numpy as np
        N_HEAD = 16
        NEG_INF = jnp.finfo(jnp.float32).min
        key = jax.random.key(seed)
        k1, k2, k3, k4 = jax.random.split(key, 4)
        B, T, C = (4, 256, 128)
        x = jax.random.normal(k1, (B, T, C), dtype=jnp.float32)
        w_attn = jax.random.normal(k2, (C, 3 * C), dtype=jnp.float32) * C ** (-0.5)
        w_proj = jax.random.normal(k3, (C, C), dtype=jnp.float32) * C ** (-0.5)
        decay_raw = jax.random.normal(k4, (N_HEAD,), dtype=jnp.float32)
        return {'x': x, 'w_attn': w_attn, 'w_proj': w_proj, 'decay_raw': decay_raw}
    _L3_attn_in = _L3_attn_setup()

    def _L3_ffn_setup():
        import jax, jax.numpy as jnp
        import numpy as np
        DIM = 128
        E = 16
        TOPK = 2
        G = 4
        TOPK_G = 2
        INTER = 64
        N_SHARED = 2
        ROUTE_SCALE = 1.0

        def _gate(xf, gate_w, gate_b):
            scores = xf @ gate_w.T
            scores = jax.nn.softmax(scores.astype(jnp.float32), axis=-1)
            orig = scores
            scores = scores + gate_b
            T = xf.shape[0]
            sg = scores.reshape(T, G, E // G)
            group_scores = jax.lax.top_k(sg, 2)[0].sum(-1)
            _, gidx = jax.lax.top_k(group_scores, TOPK_G)
            keep = jax.nn.one_hot(gidx, G).sum(axis=1) > 0
            sg = jnp.where(keep[:, :, None], sg, -jnp.inf)
            scores = sg.reshape(T, E)
            _, idx = jax.lax.top_k(scores, TOPK)
            weights = jnp.take_along_axis(orig, idx, axis=1)
            weights = (weights * ROUTE_SCALE).astype(xf.dtype)
            return (weights, idx)
        key = jax.random.key(seed)
        ks = jax.random.split(key, 16)
        s = lambda fan_in: 1.0 / np.sqrt(fan_in)
        inp = {'x': jax.random.normal(ks[0], (4, 128, DIM), dtype=jnp.float32), 'gate_w': jax.random.normal(ks[1], (E, DIM), dtype=jnp.float32) * s(DIM), 'gate_b': jnp.zeros((E,), dtype=jnp.float32), 'We1': jax.random.normal(ks[2], (E, DIM, INTER), dtype=jnp.float32) * s(DIM), 'be1': jnp.zeros((E, INTER), dtype=jnp.float32), 'We2': jax.random.normal(ks[3], (E, INTER, DIM), dtype=jnp.float32) * s(INTER), 'be2': jnp.zeros((E, DIM), dtype=jnp.float32), 'We3': jax.random.normal(ks[4], (E, DIM, INTER), dtype=jnp.float32) * s(DIM), 'be3': jnp.zeros((E, INTER), dtype=jnp.float32), 'ws1': jax.random.normal(ks[5], (DIM, N_SHARED * INTER), dtype=jnp.float32) * s(DIM), 'bs1': jnp.zeros((N_SHARED * INTER,), dtype=jnp.float32), 'ws2': jax.random.normal(ks[6], (N_SHARED * INTER, DIM), dtype=jnp.float32) * s(N_SHARED * INTER), 'bs2': jnp.zeros((DIM,), dtype=jnp.float32), 'ws3': jax.random.normal(ks[7], (DIM, N_SHARED * INTER), dtype=jnp.float32) * s(DIM), 'bs3': jnp.zeros((N_SHARED * INTER,), dtype=jnp.float32)}
        return inp
    _L3_ffn_in = _L3_ffn_setup()
    _d = {'L0_attn_x': _L0_attn_in['x'], 'L0_attn_wq': _L0_attn_in['wq'], 'L0_attn_wk': _L0_attn_in['wk'], 'L0_attn_wv': _L0_attn_in['wv'], 'L0_attn_out_w': _L0_attn_in['out_w'], 'L0_attn_out_b': _L0_attn_in['out_b'], 'L0_ffn_Wqkv': _L0_ffn_in['Wqkv'], 'L0_ffn_q_scale': _L0_ffn_in['q_scale'], 'L0_ffn_k_scale': _L0_ffn_in['k_scale'], 'L0_ffn_Wo': _L0_ffn_in['Wo'], 'L0_ffn_ln_g': _L0_ffn_in['ln_g'], 'L0_ffn_ln_b': _L0_ffn_in['ln_b'], 'L0_ffn_W1': _L0_ffn_in['W1'], 'L0_ffn_b1': _L0_ffn_in['b1'], 'L0_ffn_W2': _L0_ffn_in['W2'], 'L0_ffn_b2': _L0_ffn_in['b2'], 'L1_attn_Wq': _L1_attn_in['Wq'], 'L1_attn_Wk': _L1_attn_in['Wk'], 'L1_attn_Wv': _L1_attn_in['Wv'], 'L1_ffn_Wg': _L1_ffn_in['Wg'], 'L1_ffn_bg': _L1_ffn_in['bg'], 'L1_ffn_We': _L1_ffn_in['We'], 'L1_ffn_be': _L1_ffn_in['be'], 'L2_attn_in_proj_w': _L2_attn_in['in_proj_w'], 'L2_attn_conv_w': _L2_attn_in['conv_w'], 'L2_attn_conv_b': _L2_attn_in['conv_b'], 'L2_attn_dt_bias': _L2_attn_in['dt_bias'], 'L2_attn_A_log': _L2_attn_in['A_log'], 'L2_attn_D_skip': _L2_attn_in['D_skip'], 'L2_attn_norm_w': _L2_attn_in['norm_w'], 'L2_attn_out_proj_w': _L2_attn_in['out_proj_w'], 'L2_attn_ln_w': _L2_attn_in['ln_w'], 'L2_attn_ln_b': _L2_attn_in['ln_b'], 'L2_ffn_router_w': _L2_ffn_in['router_w'], 'L2_ffn_router_b': _L2_ffn_in['router_b'], 'L2_ffn_w1': _L2_ffn_in['w1'], 'L2_ffn_b1': _L2_ffn_in['b1'], 'L2_ffn_w2': _L2_ffn_in['w2'], 'L2_ffn_b2': _L2_ffn_in['b2'], 'L2_ffn_ow1': _L2_ffn_in['ow1'], 'L2_ffn_ob1': _L2_ffn_in['ob1'], 'L2_ffn_ow2': _L2_ffn_in['ow2'], 'L2_ffn_ob2': _L2_ffn_in['ob2'], 'L3_attn_w_attn': _L3_attn_in['w_attn'], 'L3_attn_w_proj': _L3_attn_in['w_proj'], 'L3_attn_decay_raw': _L3_attn_in['decay_raw'], 'L3_ffn_gate_w': _L3_ffn_in['gate_w'], 'L3_ffn_gate_b': _L3_ffn_in['gate_b'], 'L3_ffn_We1': _L3_ffn_in['We1'], 'L3_ffn_be1': _L3_ffn_in['be1'], 'L3_ffn_We2': _L3_ffn_in['We2'], 'L3_ffn_be2': _L3_ffn_in['be2'], 'L3_ffn_We3': _L3_ffn_in['We3'], 'L3_ffn_be3': _L3_ffn_in['be3'], 'L3_ffn_ws1': _L3_ffn_in['ws1'], 'L3_ffn_bs1': _L3_ffn_in['bs1'], 'L3_ffn_ws2': _L3_ffn_in['ws2'], 'L3_ffn_bs2': _L3_ffn_in['bs2'], 'L3_ffn_ws3': _L3_ffn_in['ws3'], 'L3_ffn_bs3': _L3_ffn_in['bs3']}
    _x0 = _d['L0_attn_x']
    _d['L0_attn_x'] = jax.random.normal(jax.random.fold_in(jax.random.key(seed), 1), (8, 512, 128), dtype=_x0.dtype)
    del _x0
    return _d

def reference(L0_attn_x, L0_attn_wq, L0_attn_wk, L0_attn_wv, L0_attn_out_w, L0_attn_out_b, L0_ffn_Wqkv, L0_ffn_q_scale, L0_ffn_k_scale, L0_ffn_Wo, L0_ffn_ln_g, L0_ffn_ln_b, L0_ffn_W1, L0_ffn_b1, L0_ffn_W2, L0_ffn_b2, L1_attn_Wq, L1_attn_Wk, L1_attn_Wv, L1_ffn_Wg, L1_ffn_bg, L1_ffn_We, L1_ffn_be, L2_attn_in_proj_w, L2_attn_conv_w, L2_attn_conv_b, L2_attn_dt_bias, L2_attn_A_log, L2_attn_D_skip, L2_attn_norm_w, L2_attn_out_proj_w, L2_attn_ln_w, L2_attn_ln_b, L2_ffn_router_w, L2_ffn_router_b, L2_ffn_w1, L2_ffn_b1, L2_ffn_w2, L2_ffn_b2, L2_ffn_ow1, L2_ffn_ob1, L2_ffn_ow2, L2_ffn_ob2, L3_attn_w_attn, L3_attn_w_proj, L3_attn_decay_raw, L3_ffn_gate_w, L3_ffn_gate_b, L3_ffn_We1, L3_ffn_be1, L3_ffn_We2, L3_ffn_be2, L3_ffn_We3, L3_ffn_be3, L3_ffn_ws1, L3_ffn_bs1, L3_ffn_ws2, L3_ffn_bs2, L3_ffn_ws3, L3_ffn_bs3):

    def _L0_attn_ref(x, wq, wk, wv, out_w, out_b):
        import jax, jax.numpy as jnp
        import numpy as np
        import math
        D_MODEL = 128
        N_HEADS = 16
        HEAD_DIM = D_MODEL // N_HEADS

        def _apply_rope_full(x):
            B, S, D = x.shape
            half = D // 2
            pos = jnp.arange(S, dtype=jnp.float32)[:, None]
            freqs = 1.0 / 10000.0 ** (jnp.arange(half, dtype=jnp.float32) / half)
            ang = pos * freqs[None, :]
            sin, cos = (jnp.sin(ang), jnp.cos(ang))
            x1, x2 = (x[..., :half], x[..., half:])
            return jnp.concatenate([x1 * cos - x2 * sin, x1 * sin + x2 * cos], axis=-1)

        def _alibi_slopes(n_heads):
            return jnp.array([2.0 ** (-8.0 * (i + 1) / n_heads) for i in range(n_heads)], dtype=jnp.float32)
        B, S, D = x.shape
        H, Dh = (N_HEADS, HEAD_DIM)
        q = x @ wq.T
        k = x @ wk.T
        v = x @ wv.T
        q = _apply_rope_full(q)
        k = _apply_rope_full(k)
        q = q.reshape(B, S, H, Dh).transpose(0, 2, 1, 3)
        k = k.reshape(B, S, H, Dh).transpose(0, 2, 1, 3)
        v = v.reshape(B, S, H, Dh).transpose(0, 2, 1, 3)
        scores = jnp.einsum('bhqd,bhkd->bhqk', q, k) / math.sqrt(Dh)
        pos = jnp.arange(S, dtype=jnp.float32)
        rel = pos[None, :] - pos[:, None]
        scores = scores + _alibi_slopes(H)[None, :, None, None] * rel[None, None]
        causal = jnp.triu(jnp.ones((S, S), dtype=bool), k=1)
        scores = jnp.where(causal[None, None], jnp.float32(-1000000000.0), scores)
        attn = jax.nn.softmax(scores, axis=-1)
        out = jnp.einsum('bhqk,bhkd->bhqd', attn, v)
        out = out.transpose(0, 2, 1, 3).reshape(B, S, D)
        return out @ out_w.T + out_b

    def _L0_ffn_ref(x, Wqkv, q_scale, k_scale, Wo, ln_g, ln_b, W1, b1, W2, b2):
        import jax, jax.numpy as jnp
        import numpy as np
        DIM = 128
        DEPTH = 6
        HEADS = 16
        DIM_HEAD = 64
        WINDOW = 32
        INNER = HEADS * DIM_HEAD
        DIM_INNER = int(DIM * 4 * 2 / 3)
        QK_SCALE = 8.0

        def shift_tokens(t):
            a, s = jnp.split(t, 2, -1)
            s = jnp.pad(s, ((0, 0), (1, 0), (0, 0)))[:, :-1]
            return jnp.concatenate([a, s], -1)

        def l2norm(t):
            return t / jnp.maximum(jnp.linalg.norm(t, axis=-1, keepdims=True), 1e-12)

        def rotate_half(x):
            x1, x2 = jnp.split(x, 2, -1)
            return jnp.concatenate([-x2, x1], -1)

        def rotary_tables(n):
            half = jnp.arange(0, DIM_HEAD, 2, dtype=jnp.float32)
            inv_freq = 1.0 / 10000.0 ** (half / DIM_HEAD)
            t = jnp.arange(n, dtype=jnp.float32)
            freqs = t[:, None] * inv_freq[None, :]
            freqs = jnp.concatenate([freqs, freqs], -1)
            base_scale = (half + 0.4 * DIM_HEAD) / (1.4 * DIM_HEAD)
            power = (t - n // 2) / (WINDOW // 2)
            scale = base_scale[None, :] ** power[:, None]
            scale = jnp.concatenate([scale, scale], -1)
            return (freqs, scale)

        def local_attention(q, k, v):
            b, h, n, d = q.shape
            w = WINDOW
            nw = n // w
            bq = q.reshape(b, h, nw, w, d)
            bk = k.reshape(b, h, nw, w, d)
            bv = v.reshape(b, h, nw, w, d)

            def look(t):
                p = jnp.pad(t, ((0, 0), (0, 0), (1, 0), (0, 0), (0, 0)))
                return jnp.concatenate([p[:, :, :nw], p[:, :, 1:]], axis=3)
            bk2, bv2 = (look(bk), look(bv))
            seq = jnp.arange(n).reshape(nw, w)
            seq_p = jnp.pad(seq, ((1, 0), (0, 0)), constant_values=-1)
            jt = jnp.concatenate([seq_p[:nw], seq_p[1:]], axis=1)
            it = seq[:, :, None]
            jb = jt[:, None, :]
            mask = (it < jb) | (it > jb + w) | (jb == -1)
            sim = jnp.einsum('bhwie,bhwje->bhwij', bq, bk2) * QK_SCALE
            sim = jnp.where(mask, -jnp.finfo(sim.dtype).max, sim)
            attn = jax.nn.softmax(sim, -1)
            out = jnp.einsum('bhwij,bhwje->bhwie', attn, bv2)
            return out.reshape(b, h, n, d)

        def attn_layer(x, Wqkv, qs, ksc, Wo):
            b, n, _ = x.shape
            qkv = x @ Wqkv
            q, k, v = jnp.split(qkv, 3, -1)
            sh = lambda t: t.reshape(b, n, HEADS, DIM_HEAD).transpose(0, 2, 1, 3)
            q, k, v = (sh(q), sh(k), sh(v))
            q = l2norm(q) * qs
            k = l2norm(k) * ksc
            freqs, scale = rotary_tables(n)
            cos, sin = (jnp.cos(freqs), jnp.sin(freqs))
            q = q * cos * scale + rotate_half(q) * sin * scale
            inv = 1.0 / scale
            k = k * cos * inv + rotate_half(k) * sin * inv
            out = local_attention(q, k, v)
            out = out.transpose(0, 2, 1, 3).reshape(b, n, INNER)
            return out @ Wo

        def ffn_layer(x, g, bln, W1, b1, W2, b2):
            mu = x.mean(-1, keepdims=True)
            var = ((x - mu) ** 2).mean(-1, keepdims=True)
            xn = (x - mu) / jnp.sqrt(var + 1e-05) * g + bln
            hg = xn @ W1 + b1
            a, gate = jnp.split(hg, 2, -1)
            return a * jax.nn.gelu(gate, approximate=False) @ W2 + b2
        for i in range(DEPTH):
            x = attn_layer(shift_tokens(x), Wqkv[i], q_scale[i], k_scale[i], Wo[i]) + x
            x = ffn_layer(shift_tokens(x), ln_g[i], ln_b[i], W1[i], b1[i], W2[i], b2[i]) + x
        return x

    def _L1_attn_ref(x, Wq, Wk, Wv):
        import jax, jax.numpy as jnp
        import numpy as np
        B, S, H, D = (4, 256, 128, 128)
        b, s, _ = x.shape
        d = Wq.shape[0]
        q = jnp.einsum('bsh,dh->bsd', x, Wq)
        k = jnp.einsum('bsh,dh->bsd', x, Wk)
        v = jnp.einsum('bsh,dh->bsd', x, Wv)
        kT = k.reshape(b, d, s)
        scores = jnp.matmul(q, kT) / jnp.sqrt(jnp.float32(d))
        attn = jax.nn.softmax(scores, axis=0)
        tril = jnp.tril(jnp.ones((s, s), dtype=bool))
        attn_masked = jnp.where(tril[None, :, :], attn, jnp.float32(1e-09))
        return jnp.matmul(attn_masked, v)

    def _L1_ffn_ref(x, Wg, bg, We, be):
        import jax, jax.numpy as jnp
        import numpy as np
        B, S, D, E = (4, 512, 128, 8)
        probs = jax.nn.softmax(x @ Wg + bg, axis=-1)
        idx = jnp.argmax(probs, axis=-1)
        p = jnp.take_along_axis(probs, idx[..., None], axis=-1)[..., 0]
        e_idx = idx % We.shape[0]
        h = jax.nn.relu(jnp.einsum('bsd,edf->besf', x, We) + be[None, :, None, :])
        onehot = jax.nn.one_hot(e_idx, We.shape[0], dtype=x.dtype)
        out = jnp.einsum('besf,bse->bsf', h, onehot) * p[..., None]
        return out

    def _L2_attn_ref(x, in_proj_w, conv_w, conv_b, dt_bias, A_log, D_skip, norm_w, out_proj_w, ln_w, ln_b):
        import jax, jax.numpy as jnp
        import numpy as np
        DT_MIN, DT_MAX = (0.001, 0.1)
        CHUNK = 64
        b, L, d_model = x.shape
        d_inner = norm_w.shape[0]
        nheads = A_log.shape[0]
        hd = d_inner // nheads
        conv_dim = conv_w.shape[0]
        d_state = (conv_dim - d_inner) // 2
        Q = CHUNK
        c = L // Q
        zxbcdt = jnp.einsum('bld,kd->blk', x, in_proj_w)
        z = zxbcdt[..., :d_inner]
        xBC = zxbcdt[..., d_inner:d_inner + conv_dim]
        dt_raw = zxbcdt[..., d_inner + conv_dim:]
        K = conv_w.shape[1]
        xp = jnp.pad(xBC, ((0, 0), (K - 1, 0), (0, 0)))
        conv = sum((xp[:, k:k + L, :] * conv_w[:, k] for k in range(K))) + conv_b
        xBC = jax.nn.silu(conv)
        x_ssm = xBC[..., :d_inner]
        Bm = xBC[..., d_inner:d_inner + d_state]
        Cm = xBC[..., d_inner + d_state:]
        dt = DT_MIN + (DT_MAX - DT_MIN) * jax.nn.sigmoid(dt_raw + dt_bias)
        A = -jnp.exp(A_log)
        xh = x_ssm.reshape(b, c, Q, nheads, hd)
        dtc = dt.reshape(b, c, Q, nheads)
        x_dt = xh * dtc[..., None]
        dA = jnp.einsum('bcqh,h->bhcq', dtc, A)
        Acum = jnp.cumsum(dA, axis=-1)
        Bc = Bm.reshape(b, c, Q, d_state)
        Cc = Cm.reshape(b, c, Q, d_state)
        seg = Acum[..., :, None] - Acum[..., None, :]
        mask = jnp.tril(jnp.ones((Q, Q), bool))
        Lmat = jnp.exp(jnp.where(mask, seg, -jnp.inf))
        Yd = jnp.einsum('bcqn,bcsn,bhcqs,bcshp->bcqhp', Cc, Bc, Lmat, x_dt)
        decay_states = jnp.exp(Acum[..., -1:] - Acum)
        states = jnp.einsum('bcqn,bhcq,bcqhp->bchpn', Bc, decay_states, x_dt)
        chunk_decay = jnp.exp(Acum[..., -1])

        def step(carry, inp):
            st, dec = inp
            return (dec[..., None, None] * carry + st, carry)
        _, prevs = jax.lax.scan(step, jnp.zeros((b, nheads, hd, d_state), x.dtype), (jnp.moveaxis(states, 1, 0), jnp.moveaxis(chunk_decay, 2, 0)))
        prevs = jnp.moveaxis(prevs, 0, 1)
        Yo = jnp.einsum('bcqn,bchpn,bhcq->bcqhp', Cc, prevs, jnp.exp(Acum))
        Y = (Yd + Yo).reshape(b, L, nheads, hd) + D_skip[None, None, :, None] * xh.reshape(b, L, nheads, hd)
        y = Y.reshape(b, L, d_inner)
        y = y * jax.nn.silu(z)
        y = y * jax.lax.rsqrt(jnp.mean(y * y, axis=-1, keepdims=True) + 1e-05) * norm_w
        out = jnp.einsum('bli,di->bld', y, out_proj_w)
        mu = jnp.mean(out, axis=-1, keepdims=True)
        var = jnp.mean((out - mu) ** 2, axis=-1, keepdims=True)
        ln = (out - mu) * jax.lax.rsqrt(var + 1e-05) * ln_w + ln_b
        return x + ln

    def _L2_ffn_ref(input, router_w, router_b, w1, b1, w2, b2, ow1, ob1, ow2, ob2):
        import jax, jax.numpy as jnp
        import numpy as np
        E = 8
        C = 160
        D = 128
        H = 512
        B, S = (4, 256)
        Bq, Sq, Dq = input.shape
        N = Bq * Sq
        xf = input.reshape(N, Dq)
        probs = jax.nn.softmax(xf @ router_w + router_b, axis=-1)
        eid = jnp.argmax(probs, axis=-1)
        onehot = jax.nn.one_hot(eid, E, dtype=xf.dtype)
        rank = (jnp.cumsum(onehot, axis=0)[jnp.arange(N), eid] - 1.0).astype(jnp.int32)
        valid = rank < C
        pos = jnp.where(valid, rank, 0)
        vmask = valid.astype(xf.dtype)[:, None]
        buf = jnp.zeros((E, C, Dq), xf.dtype).at[eid, pos].add(xf * vmask)
        h = jax.nn.relu(jnp.einsum('ecd,edh->ech', buf, w1) + b1[:, None, :])
        y = jnp.einsum('ech,ehd->ecd', h, w2) + b2[:, None, :]
        y_tok = y[eid, pos] * vmask
        yov = jax.nn.relu(xf @ ow1 + ob1) @ ow2 + ob2
        out = y_tok + yov * (1.0 - vmask)
        return out.reshape(Bq, Sq, Dq)

    def _L3_attn_ref(x, w_attn, w_proj, decay_raw):
        import jax, jax.numpy as jnp
        import numpy as np
        N_HEAD = 16
        NEG_INF = jnp.finfo(jnp.float32).min
        B, T, C = x.shape
        H = N_HEAD
        D = C // H
        qkv = x @ w_attn
        q, k, v = jnp.split(qkv, 3, axis=-1)
        q = q.reshape(B, T, H, D).transpose(0, 2, 1, 3)
        k = k.reshape(B, T, H, D).transpose(0, 2, 1, 3)
        v = v.reshape(B, T, H, D).transpose(0, 2, 1, 3)
        idx = jnp.arange(T)
        causal = jnp.where(idx[None, :] > idx[:, None], NEG_INF, 0.0).astype(jnp.float32)
        decay = jax.nn.softplus(decay_raw)
        dist = jnp.maximum(idx[:, None] - idx[None, :], 0).astype(jnp.float32)
        log1p_dist = jnp.log1p(dist)
        logw = -jnp.log1p(decay[:, None, None] * log1p_dist)
        attn_mask = causal[None, :, :] + logw
        scores = jnp.einsum('bhqd,bhkd->bhqk', q, k) * (1.0 / jnp.sqrt(jnp.float32(D)))
        scores = scores + attn_mask[None]
        att = jax.nn.softmax(scores, axis=-1)
        y = jnp.einsum('bhqk,bhkd->bhqd', att, v)
        y = y.transpose(0, 2, 1, 3).reshape(B, T, C)
        return y @ w_proj

    def _L3_ffn_ref(x, gate_w, gate_b, We1, be1, We2, be2, We3, be3, ws1, bs1, ws2, bs2, ws3, bs3):
        import jax, jax.numpy as jnp
        import numpy as np
        DIM = 128
        E = 16
        TOPK = 2
        G = 4
        TOPK_G = 2
        INTER = 64
        N_SHARED = 2
        ROUTE_SCALE = 1.0

        def _gate(xf, gate_w, gate_b):
            scores = xf @ gate_w.T
            scores = jax.nn.softmax(scores.astype(jnp.float32), axis=-1)
            orig = scores
            scores = scores + gate_b
            T = xf.shape[0]
            sg = scores.reshape(T, G, E // G)
            group_scores = jax.lax.top_k(sg, 2)[0].sum(-1)
            _, gidx = jax.lax.top_k(group_scores, TOPK_G)
            keep = jax.nn.one_hot(gidx, G).sum(axis=1) > 0
            sg = jnp.where(keep[:, :, None], sg, -jnp.inf)
            scores = sg.reshape(T, E)
            _, idx = jax.lax.top_k(scores, TOPK)
            weights = jnp.take_along_axis(orig, idx, axis=1)
            weights = (weights * ROUTE_SCALE).astype(xf.dtype)
            return (weights, idx)
        shape = x.shape
        xf = x.reshape(-1, DIM)
        weights, idx = _gate(xf, gate_w, gate_b)
        combine = (jax.nn.one_hot(idx, E, dtype=xf.dtype) * weights[..., None]).sum(1)
        h1 = jnp.einsum('td,edi->tei', xf, We1) + be1
        h3 = jnp.einsum('td,edi->tei', xf, We3) + be3
        h = jax.nn.silu(h1) * h3
        yo = jnp.einsum('tei,eid->ted', h, We2) + be2
        y = jnp.einsum('te,ted->td', combine, yo)
        z = jax.nn.silu(xf @ ws1 + bs1) * (xf @ ws3 + bs3) @ ws2 + bs2
        return (y + z).reshape(shape)
    x = L0_attn_x
    x = x + _L0_attn_ref(_layernorm(x, axis=-1), L0_attn_wq, L0_attn_wk, L0_attn_wv, L0_attn_out_w, L0_attn_out_b)
    x = x + _L0_ffn_ref(_layernorm(x, axis=-1), L0_ffn_Wqkv, L0_ffn_q_scale, L0_ffn_k_scale, L0_ffn_Wo, L0_ffn_ln_g, L0_ffn_ln_b, L0_ffn_W1, L0_ffn_b1, L0_ffn_W2, L0_ffn_b2)
    x = x + _L1_attn_ref(_layernorm(x, axis=-1), L1_attn_Wq, L1_attn_Wk, L1_attn_Wv)
    x = x + _L1_ffn_ref(_layernorm(x, axis=-1), L1_ffn_Wg, L1_ffn_bg, L1_ffn_We, L1_ffn_be)
    x = x + _L2_attn_ref(_layernorm(x, axis=-1), L2_attn_in_proj_w, L2_attn_conv_w, L2_attn_conv_b, L2_attn_dt_bias, L2_attn_A_log, L2_attn_D_skip, L2_attn_norm_w, L2_attn_out_proj_w, L2_attn_ln_w, L2_attn_ln_b)
    x = x + _L2_ffn_ref(_layernorm(x, axis=-1), L2_ffn_router_w, L2_ffn_router_b, L2_ffn_w1, L2_ffn_b1, L2_ffn_w2, L2_ffn_b2, L2_ffn_ow1, L2_ffn_ob1, L2_ffn_ow2, L2_ffn_ob2)
    x = x + _L3_attn_ref(_layernorm(x, axis=-1), L3_attn_w_attn, L3_attn_w_proj, L3_attn_decay_raw)
    x = x + _L3_ffn_ref(_layernorm(x, axis=-1), L3_ffn_gate_w, L3_ffn_gate_b, L3_ffn_We1, L3_ffn_be1, L3_ffn_We2, L3_ffn_be2, L3_ffn_We3, L3_ffn_be3, L3_ffn_ws1, L3_ffn_bs1, L3_ffn_ws2, L3_ffn_bs2, L3_ffn_ws3, L3_ffn_bs3)
    return x

_drawn_inputs = setup_inputs


def setup_inputs(seed=0):
    import zlib

    import numpy as np

    out = dict(_drawn_inputs(seed))
    spreads = {'L0_attn_out_b': (0.0, 0.1),
     'L0_ffn_q_scale': (1.0, 0.6),
     'L0_ffn_k_scale': (1.0, 0.6),
     'L0_ffn_ln_g': (1.0, 0.6),
     'L0_ffn_ln_b': (0.0, 0.8),
     'L0_ffn_b1': (0.0, 0.45),
     'L0_ffn_b2': (0.0, 0.1),
     'L1_ffn_bg': (0.0, 0.8),
     'L1_ffn_be': (0.0, 0.8),
     'L2_attn_conv_b': (0.0, 0.32),
     'L2_attn_D_skip': (1.0, 0.6),
     'L2_attn_norm_w': (1.0, 0.2),
     'L2_attn_ln_w': (1.0, 0.536),
     'L2_attn_ln_b': (0.0, 0.67),
     'L2_ffn_router_b': (0.0, 0.8),
     'L2_ffn_b1': (0.0, 0.8),
     'L2_ffn_b2': (0.0, 0.8),
     'L2_ffn_ob1': (0.0, 0.8),
     'L2_ffn_ob2': (0.0, 0.756),
     'L3_ffn_gate_b': (0.0, 0.512),
     'L3_ffn_be1': (0.0, 0.8),
     'L3_ffn_be2': (0.0, 2.0),
     'L3_ffn_be3': (0.0, 0.8),
     'L3_ffn_bs1': (0.0, 2.0),
     'L3_ffn_bs2': (0.0, 1.683),
     'L3_ffn_bs3': (0.0, 2.0)}
    factors = {'L0_ffn_W1': 3.912,
     'L0_ffn_W2': 2.927,
     'L1_ffn_Wg': 7.875,
     'L1_ffn_We': 8.0,
     'L2_attn_dt_bias': 8.0,
     'L2_ffn_router_w': 6.15,
     'L2_ffn_w1': 8.0,
     'L2_ffn_w2': 8.0,
     'L2_ffn_ow1': 8.0,
     'L2_ffn_ow2': 6.567,
     'L3_attn_decay_raw': 8.0,
     'L3_ffn_gate_w': 3.528,
     'L3_ffn_We1': 2.941,
     'L3_ffn_We2': 3.082,
     'L3_ffn_We3': 3.006}
    for name, (base, spread) in spreads.items():
        noise = np.random.default_rng([zlib.crc32(name.encode()), seed]).standard_normal(out[name].shape)
        drawn = base * np.exp(spread * noise) if base else spread * noise
        out[name] = jnp.asarray(drawn.astype(out[name].dtype))
    for name, factor in factors.items():
        out[name] = (out[name] * factor).astype(out[name].dtype)
    return out
```

```python
from contextlib import ExitStack

import numpy as np
import concourse.bass as bass
from concourse import mybir

P = 128
D = 128
NB = 8
S = 512
TT = S // P
NT = NB * TT
EPS = 1e-5
F32 = mybir.dt.float32
ALU = mybir.AluOpType
ACT = mybir.ActivationFunctionType
AX = mybir.AxisListType
AHEAD = 1
NEG = -1.0e30


def linker(eng, sem, start, total):
    count = [0]

    def link(ins):
        count[0] += 1
        ins.then_inc(sem, 1)
        eng.wait_ge(sem, AHEAD + start + count[0])

    def check():
        assert count[0] == total, (count[0], total)
    link.check = check
    return link


class Chip:

    def __init__(self, nc, dram, ctx):
        self.nc, self.dram = nc, dram
        self.x = ctx.enter_context(nc.sbuf_tensor("x_resid", [P, NT, D], F32))
        self.xT = ctx.enter_context(nc.sbuf_tensor("xT_all", [P, NB * S], F32))
        self.ident = ctx.enter_context(nc.sbuf_tensor("ident", [P, P], F32))
        self.ones = ctx.enter_context(nc.sbuf_tensor("ones", [P, P], F32))
        self.passed = ctx.enter_context(nc.semaphore("passed"))
        self.mhalf = ctx.enter_context(nc.sbuf_tensor("minus_half", [P, P], F32))
        self.bank = ctx.enter_context(nc.psum_tensor("bank", [P, 8, 512], F32))


def apart(eng, chip):
    eng.sem_inc(chip.passed, 1)


class Scope:

    def __init__(self, chip, tag, ctx):
        self.nc, self.tag, self.ctx = chip.nc, tag, ctx
        self.counted, self.sems = [], []
        ctx.callback(self.close)

    def close(self):
        if self.sems:
            self.nc.clear_and_free_semaphores(self.sems)
            self.nc.all_engine_barrier()

    def sb(self, name, shape, dt=F32):
        return self.ctx.enter_context(self.nc.sbuf_tensor(f"{self.tag}_{name}", shape, dt))

    def sem(self, name):
        self.counted.append(self.dma_sem(name))
        return self.counted[-1]

    def start(self, sp):
        for sem in self.counted:
            sp.sem_inc(sem, 1)

    def dma_sem(self, name):
        self.sems.append(self.nc.alloc_semaphore(f"{self.tag}_{name}"))
        return self.sems[-1]


def load_x(chip):
    nc = chip.nc
    with ExitStack() as ctx:
        m = Scope(chip, "load", ctx)
        loaded = m.dma_sem("loaded")
        block = ctx.enter_context(nc.Block())

        @block.sync
        def _(sp):
            sp.dma_start(chip.x[:, :, :], chip.dram["x"].rearrange("(n p) d -> p n d", p=P)).then_inc(loaded, 16)
            sp.dma_start(chip.ident[:, :], chip.dram["c_ident"]).then_inc(loaded, 16)
            sp.wait_ge(loaded, 32)

        @block.gpsimd
        def _(pool):
            pool.memset(chip.ones[:, :], 1.0)
            pool.memset(chip.mhalf[:, :], -0.5)


def store_x(chip):
    nc = chip.nc
    with ExitStack() as ctx:
        m = Scope(chip, "store", ctx)
        stored = m.dma_sem("stored")
        block = ctx.enter_context(nc.Block())

        @block.sync
        def _(sp):
            sp.dma_start(chip.dram["out"].rearrange("(n p) d -> p n d", p=P), chip.x[:, :, :]).then_inc(stored, 16)
            sp.wait_ge(stored, 16)


LN_LINKS = 1


class Norm:

    def __init__(self, m):
        self.stats = m.sb("ln_stats", [P, TT, 6])
        self.mv = m.sb("ln_mean_var", [P, TT, 2])
        self.rstd = m.sb("ln_rstd", [P, TT])
        self.xn = m.sb("ln_xn", [P, TT, D])
        self.stats_ready = m.sem("ln_stats_ready")
        self.var_eps = m.sem("ln_var_eps")
        self.rstd_ready = m.sem("ln_rstd_ready")

    def gpsimd(self, pool, chip, b):
        pool.wait_ge(self.stats_ready, AHEAD + b + 1)
        apart(pool, chip)
        pool.tensor_scalar(self.rstd[:, :], self.mv[:, :, 1], EPS, None, ALU.add).then_inc(self.var_eps, 1)
        pool.wait_ge(self.var_eps, AHEAD + b + 1)
        pool.tensor_tensor(self.rstd[:, :], self.rstd[:, :], chip.mhalf[:, 0:TT], ALU.pow).then_inc(self.rstd_ready, 1)

    def vector(self, dve, chip, b, link):
        for t in range(TT):
            ins = dve.bn_stats(self.stats[:, t, :], chip.x[:, b * TT + t, :])
        link(ins)
        apart(dve, chip)
        for t in range(TT):
            ins = dve.bn_aggr(self.mv[:, t, :], self.stats[:, t, :])
        ins.then_inc(self.stats_ready, 1)
        dve.wait_ge(self.rstd_ready, AHEAD + b + 1)
        for t in range(TT):
            ins = dve.tensor_scalar(self.xn[:, t, :], chip.x[:, b * TT + t, :], self.mv[:, t, 0:1],
                                    self.rstd[:, t:t + 1], ALU.subtract, ALU.mult)
        return ins


def norm_stage(chip, tag, wv=None, v_all=None, keep=None):
    nc = chip.nc
    with ExitStack() as ctx:
        m = Scope(chip, tag, ctx)
        n = Norm(m)
        xt = m.sb("xt", [P, S])
        wv_sb = m.sb("wv", [P, D])
        w_loaded = m.dma_sem("w_loaded")
        dve_step = m.sem("dve_step")
        xn_ready = m.sem("xn_ready")
        turned = m.sem("turned")
        xt_ready = m.sem("xt_ready")
        xt_kept = m.sem("xt_kept")
        xn_kept = m.sem("xn_kept")
        v_made = m.sem("v_made")
        v_kept = m.sem("v_kept")
        block = ctx.enter_context(nc.Block())

        @block.sync
        def _(sp):
            m.start(sp)
            if wv is not None:
                sp.dma_start(wv_sb[:, :], wv).then_inc(w_loaded, 16)

        @block.vector
        def _(dve):
            with dve.Fori(0, NB) as b:
                link = linker(dve, dve_step, b * LN_LINKS, LN_LINKS)
                dve.wait_ge(turned, AHEAD + b)
                if keep is not None:
                    dve.wait_ge(xn_kept, AHEAD + b)
                n.vector(dve, chip, b, link).then_inc(xn_ready, 1)
                link.check()

        @block.tensor
        def _(pe):
            if wv is not None:
                pe.wait_ge(w_loaded, 16)
            with pe.Fori(0, NB) as b:
                pe.wait_ge(xn_ready, AHEAD + b + 1)
                pe.wait_ge(xt_ready, AHEAD + b)
                for t in range(TT):
                    ins = pe.transpose(chip.bank[:, 0, t * P:(t + 1) * P], n.xn[:, t, :], chip.ident[:, :])
                ins.then_inc(turned, 1)
                if wv is not None:
                    pe.wait_ge(xt_ready, AHEAD + b + 1)
                    pe.wait_ge(v_kept, AHEAD + b)
                    for t in range(TT):
                        ins = pe.matmul(chip.bank[:, 1, t * P:(t + 1) * P], xt[:, t * P:(t + 1) * P], wv_sb[:, :],
                                        start=True, stop=True)
                    ins.then_inc(v_made, 1)

        @block.scalar
        def _(act):
            with act.Fori(0, NB) as b:
                act.wait_ge(turned, AHEAD + b + 1)
                act.wait_ge(xt_kept, AHEAD + b)
                if wv is not None:
                    act.wait_ge(v_made, AHEAD + b)
                act.activation(xt[:, :], chip.bank[:, 0, :], ACT.Copy).then_inc(xt_ready, 1)
                if wv is not None:
                    act.wait_ge(v_made, AHEAD + b + 1)
                    act.activation(v_all[:, bass.ts(b, TT), :], chip.bank[:, 1, :].rearrange("p (t d) -> p t d", d=D),
                                   ACT.Copy).then_inc(v_kept, 1)

        @block.gpsimd
        def _(pool):
            with pool.Fori(0, NB) as b:
                n.gpsimd(pool, chip, b)
                if keep is not None:
                    pool.wait_ge(xn_ready, AHEAD + b + 1)
                    pool.tensor_copy(keep[:, bass.ts(b, TT), :], n.xn[:, :, :]).then_inc(xn_kept, 1)
                pool.wait_ge(xt_ready, AHEAD + b + 1)
                pool.tensor_copy(chip.xT[:, bass.ts(b, S)], xt[:, :]).then_inc(xt_kept, 1)


NH = 16
HD = D // NH
G = 4
HPG = NH // G
ISQ = 1.0 / float(np.sqrt(np.float32(HD)))


def small_head_attention(chip, tag, wqk, wv, wo, bias_kind, rope=None, ob=None):
    nc, x = chip.nc, chip.x
    nproj = 4 if rope is not None else 2
    with ExitStack() as outer:
        mo = Scope(chip, tag, outer)
        v_all = mo.sb("v", [P, NT, D])
        o_all = mo.sb("o", [P, NT, D])
        norm_stage(chip, tag + "n", wv, v_all)
        with ExitStack() as ctx:
            m = Scope(chip, tag + "a", ctx)
            w = m.sb("w", [P, nproj, P])
            table = m.sb("table", [P, HPG, S])
            if rope is not None:
                rot = m.sb("rot", [P, 2, S])
                t1 = m.sb("t1", [P, 2, S])
                t2 = m.sb("t2", [P, 2, S])
            else:
                dist = m.sb("dist", [P, S])
                causal = m.sb("causal", [P, S])
                dec_in = m.sb("dec_in", [P, NH])
                dec = m.sb("dec", [P, NH])
                lnw = m.sb("lnw", [P, HPG, S])
                d_loaded = m.dma_sem("d_loaded")
                dec_step = m.sem("dec_step")
                lnw_ready = m.sem("lnw_ready")
            qk = m.sb("qk", [P, 2, S])
            NS = 3
            sc = m.sb("sc", [P, NS, S])
            pt = m.sb("pt", [P, 2, S])
            mx = m.sb("mx", [P, 16])
            nmx = m.sb("nmx", [P, 16])
            rs = m.sb("rs", [P, 16])
            rr = m.sb("rr", [P, 16])
            U = HPG * TT
            w_loaded = m.dma_sem("w_loaded")
            group_done = m.sem("group_done")
            table_ready = m.sem("table_ready")
            proj_made = m.sem("proj_made")
            rot_step = m.sem("rot_step")
            qk_ready = m.sem("qk_ready")
            s_made = m.sem("s_made")
            s_biased = m.sem("s_biased")
            nmx_ready = m.sem("nmx_ready")
            p_ready = m.sem("p_ready")
            p_turned = m.sem("p_turned")
            pt_ready = m.sem("pt_ready")
            pv_made = m.sem("pv_made")
            rr_ready = m.sem("rr_ready")
            o_kept = m.sem("o_kept")
            block = ctx.enter_context(nc.Block())

            @block.sync
            def _(sp):
                m.start(sp)
                if rope is None:
                    sp.dma_start(dist[:, :], chip.dram["c_log1p_dist"]).then_inc(d_loaded, 16)
                    sp.dma_start(causal[:, :], chip.dram["c_causal"]).then_inc(d_loaded, 16)
                    sp.dma_start(dec_in[:, :], chip.dram["L3_attn_decay_raw"].partition_broadcast(P)).then_inc(d_loaded, 16)
                with sp.Fori(0, G) as g:
                    sp.wait_ge(group_done, AHEAD + g)
                    sp.dma_start(w[:, :, :], wqk[g].rearrange("p (a c) -> p a c", c=P)).then_inc(w_loaded, 16)
                    if rope is not None:
                        sp.dma_start(rot[:, :, :], rope[g].rearrange("p (a c) -> p a c", c=S)).then_inc(w_loaded, 16)
                        sp.dma_start(table[:, :, :], bias_kind[g].rearrange("p (a c) -> p a c", c=S)).then_inc(w_loaded, 16)

            NLOAD = 16 * (3 if rope is not None else 1)

            @block.tensor
            def _(pe):
                with pe.Fori(0, G) as g:
                    pe.wait_ge(w_loaded, g * NLOAD + NLOAD)
                    apart(pe, chip)
                    with pe.Fori(0, NB) as b:
                        i = pe.snap(g * NB + b)
                        pe.wait_ge(s_biased, AHEAD + i * U)
                        for a in range(nproj):
                            pe.matmul(chip.bank[:, a, :], w[:, a, :], chip.xT[:, bass.ts(b, S)],
                                      start=True, stop=True).then_inc(proj_made, 1)

                        def scores(u):
                            j, t = u // TT, u % TT
                            if u == 0:
                                pe.wait_ge(qk_ready, AHEAD + i * 2 + 2)
                            if u >= 4:
                                pe.wait_ge(s_biased, AHEAD + i * U + u - 3)
                            pe.matmul(chip.bank[:, u % 4, 0:(t + 1) * P], qk[32 * j:32 * j + HD, 0, t * P:(t + 1) * P],
                                      qk[32 * j:32 * j + HD, 1, 0:(t + 1) * P], start=True, stop=True).then_inc(s_made, 1)

                        def turn(u):
                            t = u % TT
                            pe.wait_ge(p_ready, AHEAD + i * U + u + 1)
                            if u >= 2:
                                pe.wait_ge(pt_ready, AHEAD + i * U + u - 1)
                            else:
                                pe.wait_ge(pt_ready, AHEAD + i * U)
                            for k in range(t + 1):
                                ins = pe.transpose(chip.bank[:, 4 + u % 2, k * P:(k + 1) * P],
                                                   sc[:, u % NS, k * P:(k + 1) * P], chip.ident[:, :])
                            ins.then_inc(p_turned, 1)

                        def weigh(u):
                            j, t = u // TT, u % TT
                            pe.wait_ge(pt_ready, AHEAD + i * U + u + 1)
                            if u == 0:
                                pe.wait_ge(o_kept, AHEAD + i)
                            for k in range(t + 1):
                                ins = pe.matmul(chip.bank[:, 6, u * HD:(u + 1) * HD], pt[:, u % 2, k * P:(k + 1) * P],
                                                v_all[:, b * TT + k, bass.ds(g * 32 + j * HD, HD)],
                                                start=(k == 0), stop=(k == t))
                            ins.then_inc(pv_made, 1)

                        for u in range(U + 3):
                            if u < U:
                                scores(u)
                            if 0 <= u - 2 < U:
                                turn(u - 2)
                            if 0 <= u - 3 < U:
                                weigh(u - 3)

            NROT = 2 if rope is not None else 0

            @block.vector
            def _(dve):
                if rope is None:
                    dve.wait_ge(d_loaded, 48)
                    dve.wait_ge(dec_step, AHEAD + 3)
                    dve.scalar_tensor_tensor(dec[:, :], dec_in[:, :], 0.0, dec[:, :], ALU.max, ALU.add).then_inc(dec_step, 1)
                with dve.Fori(0, G) as g:
                    if rope is None:
                        dve.wait_ge(lnw_ready, AHEAD + g + 1)
                        for j in range(HPG):
                            ins = dve.scalar_tensor_tensor(table[:, j, :], lnw[:, j, :], -1.0 / ISQ, causal[:, :],
                                                           ALU.mult, ALU.add)
                        ins.then_inc(table_ready, 1)
                        dve.wait_ge(table_ready, AHEAD + g + 1)
                    else:
                        dve.wait_ge(w_loaded, g * NLOAD + NLOAD)
                    apart(dve, chip)
                    with dve.Fori(0, NB) as b:
                        i = dve.snap(g * NB + b)
                        if rope is None:
                            for a in range(2):
                                dve.wait_ge(proj_made, AHEAD + i * 2 + a + 1)
                                dve.tensor_copy(qk[:, a, :], chip.bank[:, a, :]).then_inc(qk_ready, 1)
                        else:
                            for a in range(2):
                                dve.wait_ge(proj_made, AHEAD + i * 4 + 2 * a + 2)
                                dve.tensor_tensor(t1[:, a, :], chip.bank[:, 2 * a, :], rot[:, 0, :], ALU.mult)
                                dve.tensor_tensor(t2[:, a, :], chip.bank[:, 2 * a + 1, :], rot[:, 1, :], ALU.mult)\
                                    .then_inc(rot_step, 1)
                            for a in range(2):
                                dve.wait_ge(rot_step, AHEAD + i * 2 + a + 1)
                                dve.tensor_tensor(qk[:, a, :], t1[:, a, :], t2[:, a, :], ALU.add).then_inc(qk_ready, 1)

                        for u in range(U):
                            t = u % TT
                            nk = (t + 1) * P
                            dve.wait_ge(s_made, AHEAD + i * U + u + 1)
                            if u >= NS:
                                dve.wait_ge(p_turned, AHEAD + i * U + u - NS + 1)
                            if u == 0:
                                dve.wait_ge(p_ready, AHEAD + i * U)
                            apart(dve, chip)
                            dve.tensor_tensor_reduce(sc[:, u % NS, 0:nk], chip.bank[:, u % 4, 0:nk],
                                                     table[:, u // TT, S - nk:S], 1.0, NEG * 2, ALU.add, ALU.max,
                                                     mx[:, u:u + 1]).then_inc(s_biased, 1)
                            dve.wait_ge(s_biased, AHEAD + i * U + u + 1)
                            dve.tensor_scalar(nmx[:, u:u + 1], mx[:, u:u + 1], -ISQ, None, ALU.mult).then_inc(nmx_ready, 1)
                        dve.wait_ge(p_ready, AHEAD + i * U + U)
                        dve.reciprocal(rr[:, :], rs[:, :]).then_inc(rr_ready, 1)
                        dve.wait_ge(rr_ready, AHEAD + i + 1)
                        dve.wait_ge(pv_made, AHEAD + i * U + U)
                        for t in range(TT):
                            src = chip.bank[:, 6, 0:U * HD].rearrange("p (j t d) -> p j t d", j=HPG, t=TT)[:, :, t, :]
                            rep = rr[:, :].rearrange("p (j t) -> p j t", j=HPG)[:, :, t:t + 1].to_broadcast([P, HPG, HD])
                            ins = dve.tensor_tensor(
                                o_all[:, b * TT + t, bass.ds(g * 32, 32)].rearrange("p (j d) -> p j d", d=HD),
                                src, rep, ALU.mult)
                        ins.then_inc(o_kept, 1)

            @block.scalar
            def _(act):
                if rope is None:
                    act.wait_ge(d_loaded, 48)
                    act.activation(dec[:, :], dec_in[:, :], ACT.Abs).then_inc(dec_step, 1)
                    act.wait_ge(dec_step, AHEAD + 1)
                    act.activation(dec[:, :], dec[:, :], ACT.Exp, scale=-1.0).then_inc(dec_step, 1)
                    act.wait_ge(dec_step, AHEAD + 2)
                    act.activation(dec[:, :], dec[:, :], ACT.Ln, bias=chip.ones[:, 0:1]).then_inc(dec_step, 1)
                    act.wait_ge(dec_step, AHEAD + 4)
                with act.Fori(0, G) as g:
                    if rope is None:
                        act.wait_ge(table_ready, AHEAD + g)
                        for j in range(HPG):
                            act.activation(dec_in[:, j:j + 1], dec[:, bass.ds(g * HPG + j, 1)], ACT.Copy).then_inc(dec_step, 1)
                        act.wait_ge(dec_step, AHEAD + g * HPG + 4 + HPG)
                        for j in range(HPG):
                            ins = act.activation(lnw[:, j, :], dist[:, :], ACT.Ln, bias=chip.ones[:, 0:1], scale=dec_in[:, j:j + 1])
                        ins.then_inc(lnw_ready, 1)
                    with act.Fori(0, NB) as b:
                        i = act.snap(g * NB + b)

                        def exp(u):
                            nk = (u % TT + 1) * P
                            act.wait_ge(nmx_ready, AHEAD + i * U + u + 1)
                            if u == 0:
                                act.wait_ge(rr_ready, AHEAD + i)
                            act.activation(sc[:, u % NS, 0:nk], sc[:, u % NS, 0:nk], ACT.Exp, bias=nmx[:, u:u + 1],
                                           scale=ISQ, accum_out=rs[:, u:u + 1]).then_inc(p_ready, 1)

                        def keep(u):
                            nk = (u % TT + 1) * P
                            act.wait_ge(p_turned, AHEAD + i * U + u + 1)
                            if u >= 2:
                                act.wait_ge(pv_made, AHEAD + i * U + u - 1)
                            else:
                                act.wait_ge(pv_made, AHEAD + i * U)
                            act.activation(pt[:, u % 2, 0:nk], chip.bank[:, 4 + u % 2, 0:nk], ACT.Copy).then_inc(pt_ready, 1)

                        for u in range(U + 2):
                            if u < U:
                                exp(u)
                            if 0 <= u - 2:
                                keep(u - 2)

            @block.gpsimd
            def _(pool):
                with pool.Fori(0, G) as g:
                    pool.wait_ge(o_kept, AHEAD + g * NB + NB)
                    pool.sem_inc(group_done, 1)

        out_projection(chip, tag + "o", o_all, wo, ob)


def out_projection(chip, tag, o_all, wo, ob):
    nc, x = chip.nc, chip.x
    with ExitStack() as ctx:
        m = Scope(chip, tag, ctx)
        cur = m.sb("cur", [P, TT, D])
        curT = m.sb("curT", [P, S])
        w = m.sb("w", [P, D])
        bias = m.sb("bias", [P, D])
        w_loaded = m.dma_sem("w_loaded")
        cur_ready = m.sem("cur_ready")
        turned = m.sem("turned")
        curT_ready = m.sem("curT_ready")
        made = m.sem("made")
        biased = m.sem("biased")
        added = m.sem("added")
        block = ctx.enter_context(nc.Block())

        @block.sync
        def _(sp):
            m.start(sp)
            sp.dma_start(w[:, :], wo).then_inc(w_loaded, 16)
            if ob is not None:
                sp.dma_start(bias[:, :], ob.partition_broadcast(P)).then_inc(w_loaded, 16)

        nload = 32 if ob is not None else 16

        @block.gpsimd
        def _(pool):
            with pool.Fori(0, NB) as b:
                pool.wait_ge(turned, AHEAD + b)
                pool.tensor_copy(cur[:, :, :], o_all[:, bass.ts(b, TT), :]).then_inc(cur_ready, 1)

        @block.tensor
        def _(pe):
            pe.wait_ge(w_loaded, nload)
            with pe.Fori(0, NB) as b:
                pe.wait_ge(cur_ready, AHEAD + b + 1)
                pe.wait_ge(curT_ready, AHEAD + b)
                for t in range(TT):
                    ins = pe.transpose(chip.bank[:, 0, t * P:(t + 1) * P], cur[:, t, :], chip.ident[:, :])
                ins.then_inc(turned, 1)
                pe.wait_ge(curT_ready, AHEAD + b + 1)
                pe.wait_ge(added, AHEAD + b)
                for t in range(TT):
                    ins = pe.matmul(chip.bank[:, 1, t * P:(t + 1) * P], curT[:, t * P:(t + 1) * P], w[:, :],
                                    start=True, stop=True)
                ins.then_inc(made, 1)

        @block.scalar
        def _(act):
            with act.Fori(0, NB) as b:
                act.wait_ge(turned, AHEAD + b + 1)
                act.wait_ge(made, AHEAD + b)
                act.activation(curT[:, :], chip.bank[:, 0, :], ACT.Copy).then_inc(curT_ready, 1)

        @block.vector
        def _(dve):
            dve.wait_ge(w_loaded, nload)
            with dve.Fori(0, NB) as b:
                xb = x[:, bass.ts(b, TT), :]
                if ob is not None:
                    dve.tensor_tensor(xb, xb, bias[:, :].rearrange("p (a d) -> p a d", a=1).to_broadcast([P, TT, D]), ALU.add)\
                        .then_inc(biased, 1)
                    dve.wait_ge(biased, AHEAD + b + 1)
                dve.wait_ge(made, AHEAD + b + 1)
                dve.tensor_tensor(xb, xb, chip.bank[:, 1, :].rearrange("p (t d) -> p t d", d=D), ALU.add).then_inc(added, 1)


DEPTH = 6
LH = 16
LD = 64
NG = LH * LD // P
WIN = 32
NK = P + WIN
HID = 341
HC = -(-HID // P)
QKS = 8.0
U2 = 2 * TT


def local_layers(chip):
    nc, dram, bank, yT, ident = chip.nc, chip.dram, chip.bank, chip.xT, chip.ident
    norm_stage(chip, "l0n")
    with ExitStack() as ctx:
        m = Scope(chip, "l", ctx)
        wqk = m.sb("wqk", [P, NG + 1, 4 * P])
        wv = m.sb("wv", [P, LH * LD])
        wo = m.sb("wo", [P, NG, D])
        w1 = m.sb("w1", [P, 2 * HC, P])
        w2 = m.sb("w2", [P, HC, D])
        cols = m.sb("cols", [P, 8 + 2 * HC])
        base = m.sb("base", [P, 4, S])
        rot = m.sb("rot", [P, 4, S])
        mask = m.sb("mask", [P, 2, NK])
        pair = m.sb("pair", [P, 2])
        avg = m.sb("avg", [P, P])
        xs = m.sb("xs", [P, S])
        wst = m.sb("wst", [P, 4, P])
        t1 = m.sb("t1", [P, 2, S])
        t2 = m.sb("t2", [P, 2, S])
        sq = m.sb("sq", [P, 2, S])
        ss = m.sb("ss", [P, TT, 4])
        rn = m.sb("rn", [P, TT, 4])
        rkb = m.sb("rkb", [P, TT, P])
        q_sb = m.sb("q", [P, 2, S])
        k_sb = m.sb("k", [P, 2, WIN + S])
        v_sb = m.sb("v", [P, 2, TT, P])
        nscale = m.sb("nscale", [P, 2, TT, 2])
        PAD = P - WIN
        pb = m.sb("pb", [P, U2, PAD + NK])
        NPT = 4
        pt = m.sb("pt", [P, NPT, NK])
        nm = m.sb("nm", [P, U2])
        rs = m.sb("rs", [P, U2])
        rr = m.sb("rr", [P, U2])
        ot = m.sb("ot", [P, NG, S])
        xc = m.sb("xc", [P, S])
        sqf = m.sb("sqf", [P, S])
        sv = m.sb("sv", [P, TT])
        rv = m.sb("rv", [P, TT])
        xg = m.sb("xg", [P, S])
        ge = m.sb("ge", [P, 2, S])
        hh = m.sb("hh", [P, 2, S])

        tables_in = m.dma_sem("tables_in")
        w_in = m.dma_sem("w_in")
        layer_done = m.sem("layer_done")
        zeroed = m.sem("zeroed")
        padded = m.sem("padded")
        rot_ready = m.sem("rot_ready")
        xs_ready = m.sem("xs_ready")
        wst_ready = m.sem("wst_ready")
        q_made = m.sem("q_made")
        k_made = m.sem("k_made")
        q_turned = m.sem("q_turned")
        k_turned = m.sem("k_turned")
        q_squared = m.sem("q_squared")
        k_squared = m.sem("k_squared")
        v_made = m.sem("v_made")
        v_kept = m.sem("v_kept")
        ss_made = m.sem("ss_made")
        ss_kept = m.sem("ss_kept")
        rn_ready = m.sem("rn_ready")
        rkb_ready = m.sem("rkb_ready")
        q_ready = m.sem("q_ready")
        k_added = m.sem("k_added")
        rk_spread = m.sem("rk_spread")
        k_ready = m.sem("k_ready")
        s_made = m.sem("s_made")
        s_masked = m.sem("s_masked")
        p_exp = m.sem("p_exp")
        rr_ready = m.sem("rr_ready")
        p_ready = m.sem("p_ready")
        p_turned = m.sem("p_turned")
        pt_ready = m.sem("pt_ready")
        pv_made = m.sem("pv_made")
        ot_kept = m.sem("ot_kept")
        wo_made = m.sem("wo_made")
        y_mid = m.sem("y_mid")
        mean_made = m.sem("mean_made")
        xc_ready = m.sem("xc_ready")
        sqf_ready = m.sem("sqf_ready")
        sv_made = m.sem("sv_made")
        sv_kept = m.sem("sv_kept")
        rv_ready = m.sem("rv_ready")
        rv_spread = m.sem("rv_spread")
        xcn_ready = m.sem("xcn_ready")
        xg_ready = m.sem("xg_ready")
        h_made = m.sem("h_made")
        ge_ready = m.sem("ge_ready")
        hh_ready = m.sem("hh_ready")
        w2_used = m.sem("w2_used")
        y_done = m.sem("y_done")
        block = ctx.enter_context(nc.Block())
        NW = 6 * 16

        @block.sync
        def _(sp):
            m.start(sp)
            sp.dma_start(base[:, :, :], dram["c_lrot"].rearrange("p (a c) -> p a c", c=S)).then_inc(tables_in, 16)
            sp.dma_start(mask[:, :, :], dram["c_lmask"].rearrange("p (a c) -> p a c", c=NK)).then_inc(tables_in, 16)
            sp.dma_start(pair[:, :], dram["c_pair"]).then_inc(tables_in, 16)
            with sp.Fori(0, DEPTH) as l:
                sp.wait_ge(layer_done, AHEAD + l)
                sp.dma_start(wqk[:, 0:NG, :], dram["w_l_qk"][l].rearrange("p (g c) -> p g c", c=4 * P)).then_inc(w_in, 16)
                sp.dma_start(wv[:, :], dram["w_l_v"][l]).then_inc(w_in, 16)
                sp.dma_start(wo[:, :, :], dram["w_l_o"][l].rearrange("(g p) d -> p g d", p=P)).then_inc(w_in, 16)
                sp.dma_start(w1[:, :, :], dram["w_l_1"][l].rearrange("p (a c) -> p a c", c=P)).then_inc(w_in, 16)
                sp.dma_start(w2[:, :, :], dram["w_l_2"][l].rearrange("(a p) d -> p a d", p=P)).then_inc(w_in, 16)
                sp.dma_start(cols[:, :], dram["w_l_cols"][l]).then_inc(w_in, 16)

        TURN, COPY, WEIGH, NORM = 3, 3, 5, 1
        KEEP = WEIGH - 1
        PREP_Q, PREP_K, PREP_SS, PREP_V, PREP_RK = 0, 2, 4, 5, 7
        TB = (6, 2)

        def groups(eng, steps):
            steps(-1, 1, False, False, 0)
            steps(0, 0, True, False, 1)
            with eng.Fori(0, NG // 2 - 1) as k:
                steps(k * 2 + 1, 1, True, True, k * 2 + 2)
                steps(k * 2 + 2, 0, True, True, k * 2 + 3)
            steps(NG - 1, 1, True, True, None)
            steps(NG, 0, False, True, None)

        def lagging(s, lag, par, runs, behind):
            if s >= lag:
                return (s - lag, 0, par) if runs else None
            return (s - lag + U2, 1, 1 - par) if behind else None

        @block.tensor
        def _(pe):
            pe.wait_ge(tables_in, 48)
            pe.wait_ge(zeroed, AHEAD + 1)
            pe.wait_ge(padded, AHEAD + 1)
            with pe.Fori(0, DEPTH) as l:
                pe.wait_ge(w_in, l * NW + NW)
                apart(pe, chip)
                with pe.Fori(0, NB) as b:
                    i = pe.snap(l * NB + b)

                    def steps(g, par, runs, behind, n):
                        q = i * NG + g
                        r = None if n is None else i * NG + n

                        def scores(u):
                            t, j = u // 2, u % 2
                            rows = slice(LD * j, LD * j + LD)
                            if u == 0:
                                pe.wait_ge(q_ready, AHEAD + q + 1)
                                pe.wait_ge(k_ready, AHEAD + q + 1)
                            pe.wait_ge(s_masked, AHEAD + q * U2 + u - 1 if u >= 2 else q * U2)
                            apart(pe, chip)
                            pe.matmul(bank[:, 4 + j, 0:NK], q_sb[rows, par, t * P:(t + 1) * P],
                                      k_sb[rows, par, t * P:t * P + NK], start=True, stop=True).then_inc(s_made, 1)

                        def turn(u, back, par):
                            t, j = u // 2, u % 2
                            done = (q - back) * U2 + u
                            pe.wait_ge(p_ready, AHEAD + done + 1)
                            pe.wait_ge(pt_ready, AHEAD + done - 1 if u else done)
                            apart(pe, chip)
                            ins = pe.transpose(bank[:, TB[j], 0:P], pb[:, u, P:PAD + NK], ident[:, :])
                            if t > 0:
                                ins = pe.transpose(bank[:, TB[j], P:NK], pb[0:WIN, u, 0:P], ident[0:WIN, 0:WIN])
                            ins.then_inc(p_turned, 1)

                        def weigh(u, back, par):
                            t, j = u // 2, u % 2
                            rows = slice(LD * j, LD * j + LD)
                            pe.wait_ge(pt_ready, AHEAD + (q - back) * U2 + u + 1)
                            if u == 0:
                                pe.wait_ge(ot_kept, AHEAD + q - back)
                                pe.wait_ge(v_kept, AHEAD + q - back + 1)
                            apart(pe, chip)
                            ins = pe.matmul(bank[rows, 7, t * P:(t + 1) * P], v_sb[:, par, t, rows], pt[:, u % NPT, 0:P],
                                            start=True, stop=(t == 0), skip_group_check=True)
                            if t > 0:
                                ins = pe.matmul(bank[rows, 7, t * P:t * P + WIN], v_sb[:, par, t - 1, rows],
                                                pt[:, u % NPT, P:NK], start=False, stop=True, skip_group_check=True)
                            ins.then_inc(pv_made, 1)

                        for s in range(U2):
                            if runs:
                                scores(s)
                            unit = lagging(s, TURN, par, runs, behind)
                            if unit:
                                turn(*unit)
                            unit = lagging(s, WEIGH, par, runs, behind)
                            if unit:
                                weigh(*unit)
                            if n is None:
                                continue
                            if s == PREP_Q:
                                pe.wait_ge(wst_ready, AHEAD + i * (NG + 1) + n + 1)
                                pe.wait_ge(k_turned, AHEAD + r)
                                pe.wait_ge(k_squared, AHEAD + r)
                                pe.wait_ge(xs_ready, AHEAD + i * 2 + 1)
                                apart(pe, chip)
                                pe.matmul(bank[:, 0, :], wst[:, 0, :], xs[:, :], start=True, stop=True)
                                pe.matmul(bank[:, 1, :], wst[:, 1, :], xs[:, :], start=True, stop=True).then_inc(q_made, 1)
                            if s == PREP_K:
                                pe.wait_ge(q_turned, AHEAD + r + 1)
                                pe.wait_ge(q_squared, AHEAD + r + 1)
                                apart(pe, chip)
                                pe.matmul(bank[:, 0, :], wst[:, 2, :], xs[:, :], start=True, stop=True)
                                pe.matmul(bank[:, 1, :], wst[:, 3, :], xs[:, :], start=True, stop=True).then_inc(k_made, 1)
                            if s == PREP_SS:
                                pe.wait_ge(q_squared, AHEAD + r + 1)
                                pe.wait_ge(k_squared, AHEAD + r + 1)
                                pe.wait_ge(k_ready, AHEAD + r)
                                apart(pe, chip)
                                for t in range(TT):
                                    for a in range(2):
                                        ins = pe.matmul(bank[:, 3, t * 4 + 2 * a:t * 4 + 2 * a + 2],
                                                        sq[:, a, t * P:(t + 1) * P], pair[:, :], start=True, stop=True)
                                ins.then_inc(ss_made, 1)
                            if s == PREP_V:
                                pe.wait_ge(ss_kept, AHEAD + r + 1)
                                apart(pe, chip)
                                for t in range(TT):
                                    ins = pe.matmul(bank[:, 3, t * P:(t + 1) * P], xs[:, t * P:(t + 1) * P],
                                                    wv[:, bass.ts(n, P)], start=True, stop=True)
                                ins.then_inc(v_made, 1)
                            if s == PREP_RK:
                                pe.wait_ge(rkb_ready, AHEAD + r + 1)
                                pe.wait_ge(v_kept, AHEAD + r + 1)
                                apart(pe, chip)
                                for t in range(TT):
                                    ins = pe.matmul(bank[:, 3, t * P:(t + 1) * P], rkb[:, t, :], ident[:, :],
                                                    start=True, stop=True)
                                ins.then_inc(rk_spread, 1)

                    groups(pe, steps)

                    pe.wait_ge(ot_kept, AHEAD + i * NG + NG)
                    pe.wait_ge(k_turned, AHEAD + i * NG + NG)
                    apart(pe, chip)
                    for g in range(NG):
                        ins = pe.matmul(bank[:, 0, :], wo[:, g, :], ot[:, g, :], start=(g == 0), stop=(g == NG - 1))
                    ins.then_inc(wo_made, 1)
                    pe.wait_ge(xs_ready, AHEAD + i * 2 + 2)
                    apart(pe, chip)
                    pe.matmul(bank[:, 1, :], avg[:, :], xs[:, :], start=True, stop=True).then_inc(mean_made, 1)
                    pe.wait_ge(sqf_ready, AHEAD + i + 1)
                    apart(pe, chip)
                    for t in range(TT):
                        ins = pe.matmul(bank[:, 2, t:t + 1], sqf[:, t * P:(t + 1) * P], avg[:, 0:1], start=True, stop=True)
                    ins.then_inc(sv_made, 1)
                    pe.wait_ge(rv_ready, AHEAD + i + 1)
                    apart(pe, chip)
                    for t in range(TT):
                        ins = pe.matmul(bank[:, 3, t * P:(t + 1) * P], rv[:, t:t + 1].to_broadcast([P, P]), ident[:, :],
                                        start=True, stop=True)
                    ins.then_inc(rv_spread, 1)
                    for c in range(HC + 1):
                        if c < HC:
                            if c == 0:
                                pe.wait_ge(xg_ready, AHEAD + i + 1)
                            if c >= 2:
                                pe.wait_ge(hh_ready, AHEAD + i * HC + c - 1)
                            apart(pe, chip)
                            pe.matmul(bank[:, 5 + 2 * (c % 2), :], w1[:, HC + c, :], xg[:, :], start=True, stop=True)
                            pe.matmul(bank[:, 4 + 2 * (c % 2), :], w1[:, c, :], xg[:, :], start=True, stop=True)\
                                .then_inc(h_made, 1)
                        if c >= 1:
                            pe.wait_ge(hh_ready, AHEAD + i * HC + c)
                            apart(pe, chip)
                            pe.matmul(bank[:, 1, :], w2[:, c - 1, :], hh[:, (c - 1) % 2, :], start=(c == 1), stop=(c == HC))\
                                .then_inc(w2_used, 1)

        @block.vector
        def _(dve):
            dve.memset(xs[LD:P, 0:1], 0.0)
            dve.memset(avg[:, :], 1.0 / D).then_inc(zeroed, 1)
            dve.wait_ge(tables_in, 48)
            with dve.Fori(0, DEPTH) as l:
                dve.wait_ge(w_in, l * NW + NW)
                apart(dve, chip)
                for a in range(4):
                    ins = dve.tensor_scalar(rot[:, a, :], base[:, a, :], cols[:, a:a + 1], None, ALU.mult)
                ins.then_inc(rot_ready, 1)
                dve.wait_ge(rot_ready, AHEAD + l + 1)
                apart(dve, chip)
                with dve.Fori(0, NB) as b:
                    i = dve.snap(l * NB + b)

                    def steps(g, par, runs, behind, n):
                        q = i * NG + g
                        r = None if n is None else i * NG + n

                        def masked(u):
                            t = u // 2
                            dve.wait_ge(s_made, AHEAD + q * U2 + u + 1)
                            dve.wait_ge(p_turned, AHEAD + (q - 1) * U2 + u + 1 if behind else i * NG * U2)
                            if u == 0:
                                dve.wait_ge(q_ready, AHEAD + q + 1)
                            apart(dve, chip)
                            dve.tensor_tensor_reduce(pb[:, u, PAD:PAD + NK], bank[:, 4 + u % 2, 0:NK], mask[:, min(t, 1), :],
                                                     nscale[:, par, t, u % 2:u % 2 + 1], -NEG * 2, ALU.add, ALU.min,
                                                     nm[:, u:u + 1]).then_inc(s_masked, 1)

                        def normed(u, back, par):
                            done = (q - back) * U2 + u
                            dve.wait_ge(p_exp, AHEAD + done + 1)
                            dve.reciprocal(rr[:, u:u + 1], rs[:, u:u + 1]).then_inc(rr_ready, 1)
                            dve.wait_ge(rr_ready, AHEAD + done + 1)
                            dve.tensor_scalar(pb[:, u, PAD:PAD + NK], pb[:, u, PAD:PAD + NK], rr[:, u:u + 1], None,
                                              ALU.mult).then_inc(p_ready, 1)

                        for s in range(U2):
                            if runs:
                                masked(s)
                            unit = lagging(s, NORM, par, runs, behind)
                            if unit:
                                normed(*unit)
                            if n is None:
                                continue
                            for at, a, squared, turned in ((PREP_Q + 1, 0, q_squared, q_turned), (PREP_K + 1, 1, k_squared, k_turned)):
                                if s == at:
                                    dve.wait_ge(squared, AHEAD + r + 1)
                                    dve.wait_ge((q_ready, k_ready)[a], AHEAD + r)
                                    dve.tensor_tensor(t1[:, a, :], bank[:, 0, :], rot[:, 2 * a, :], ALU.mult)
                                    dve.tensor_tensor(t2[:, a, :], bank[:, 1, :], rot[:, 2 * a + 1, :], ALU.mult)\
                                        .then_inc(turned, 1)
                            if s == PREP_SS:
                                dve.wait_ge(ss_made, AHEAD + r + 1)
                                dve.wait_ge(rn_ready, AHEAD + r)
                                apart(dve, chip)
                                dve.tensor_scalar(ss[:, :, :], bank[:, 3, 0:4 * TT].rearrange("p (t a) -> p t a", a=4),
                                                  1e-24, None, ALU.max).then_inc(ss_kept, 1)
                            if s == PREP_RK:
                                dve.wait_ge(rk_spread, AHEAD + r + 1)
                                dve.wait_ge(k_added, AHEAD + r + 1)
                                dve.tensor_tensor(k_sb[:, 1 - par, WIN:WIN + S], bank[:, 3, :], t1[:, 1, :], ALU.mult)\
                                    .then_inc(k_ready, 1)

                    groups(dve, steps)

                    yb = yT[:, bass.ts(b, S)]
                    dve.wait_ge(wo_made, AHEAD + i + 1)
                    dve.tensor_tensor(yb, yb, bank[:, 0, :], ALU.add).then_inc(y_mid, 1)
                    dve.wait_ge(mean_made, AHEAD + i + 1)
                    dve.tensor_tensor(xc[:, :], xs[:, :], bank[:, 1, :], ALU.subtract).then_inc(xc_ready, 1)
                    dve.wait_ge(sv_made, AHEAD + i + 1)
                    apart(dve, chip)
                    dve.tensor_scalar(sv[:, :], bank[:, 2, 0:TT], EPS, None, ALU.add).then_inc(sv_kept, 1)
                    dve.wait_ge(rv_spread, AHEAD + i + 1)
                    dve.tensor_tensor(xc[:, :], xc[:, :], bank[:, 3, :], ALU.mult).then_inc(xcn_ready, 1)
                    for c in range(HC):
                        dve.wait_ge(ge_ready, AHEAD + i * HC + c + 1)
                        dve.wait_ge(w2_used, AHEAD + i * HC + max(c - 1, 0))
                        dve.scalar_tensor_tensor(hh[:, c % 2, :], bank[:, 4 + 2 * (c % 2), :], cols[:, 8 + c:9 + c],
                                                 ge[:, c % 2, :], ALU.add, ALU.mult).then_inc(hh_ready, 1)
                    dve.wait_ge(w2_used, AHEAD + i * HC + HC)
                    apart(dve, chip)
                    dve.scalar_tensor_tensor(yb, bank[:, 1, :], cols[:, 6:7], yb, ALU.add, ALU.add).then_inc(y_done, 1)

        @block.scalar
        def _(act):
            with act.Fori(0, DEPTH) as l:
                with act.Fori(0, NB) as b:
                    i = act.snap(l * NB + b)

                    def shifted():
                        act.activation(xs[0:LD, :], yT[0:LD, bass.ts(b, S)], ACT.Copy)
                        act.activation(xs[LD:P, 1:S], yT[LD:P, bass.ds(b * S, S - 1)], ACT.Copy).then_inc(xs_ready, 1)

                    act.wait_ge(y_done, AHEAD + i)
                    apart(act, chip)
                    shifted()

                    def steps(g, par, runs, behind, n):
                        q = i * NG + g
                        r = None if n is None else i * NG + n
                        for s in range(U2):
                            if runs:
                                act.wait_ge(s_masked, AHEAD + q * U2 + s + 1)
                                act.activation(pb[:, s, PAD:PAD + NK], pb[:, s, PAD:PAD + NK], ACT.Exp,
                                               bias=nm[:, s:s + 1], scale=-1.0, accum_out=rs[:, s:s + 1]).then_inc(p_exp, 1)
                            unit = lagging(s, COPY, par, runs, behind)
                            if unit:
                                u, back, _ = unit
                                done = (q - back) * U2 + u
                                wide = NK if u // 2 > 0 else P
                                act.wait_ge(p_turned, AHEAD + done + 1)
                                act.wait_ge(pv_made, AHEAD + done - NPT + 1 if u >= NPT - 1 or back == 0 and behind else i * NG * U2)
                                act.activation(pt[:, u % NPT, 0:wide], bank[:, TB[u % 2], 0:wide], ACT.Copy).then_inc(pt_ready, 1)
                            if s == KEEP and behind:
                                act.wait_ge(pv_made, AHEAD + q * U2)
                                act.activation(ot[:, bass.ds(g - 1, 1), :], bank[:, 7:8, :], ACT.Copy).then_inc(ot_kept, 1)
                            if n is None:
                                continue
                            for at, a, made, squared in ((PREP_Q, 0, q_made, q_squared), (PREP_K, 1, k_made, k_squared)):
                                if s == at:
                                    act.wait_ge(made, AHEAD + r + 1)
                                    act.wait_ge(ss_made, AHEAD + r)
                                    act.activation(sq[:, a, :], bank[:, 0, :], ACT.Square).then_inc(squared, 1)
                            if s == PREP_V:
                                act.wait_ge(v_made, AHEAD + r + 1)
                                act.activation(v_sb[:, 1 - par, :, :], bank[:, 3, :].rearrange("p (t c) -> p t c", c=P),
                                               ACT.Copy).then_inc(v_kept, 1)

                    groups(act, steps)
                    act.wait_ge(y_mid, AHEAD + i + 1)
                    apart(act, chip)
                    shifted()
                    act.wait_ge(xc_ready, AHEAD + i + 1)
                    act.activation(sqf[:, :], xc[:, :], ACT.Square).then_inc(sqf_ready, 1)
                    act.wait_ge(xcn_ready, AHEAD + i + 1)
                    act.activation(xg[:, :], xc[:, :], ACT.Identity, bias=cols[:, 5:6], scale=cols[:, 4:5]).then_inc(xg_ready, 1)
                    for c in range(HC):
                        act.wait_ge(h_made, AHEAD + i * HC + c + 1)
                        act.wait_ge(hh_ready, AHEAD + i * HC + max(c - 1, 0))
                        act.activation(ge[:, c % 2, :], bank[:, 5 + 2 * (c % 2), :], ACT.Gelu,
                                       bias=cols[:, 8 + HC + c:9 + HC + c]).then_inc(ge_ready, 1)

        @block.gpsimd
        def _(pool):
            pool.memset(pb[:, :, 0:PAD], 0.0)
            pool.memset(wqk[:, NG, :], 0.0)
            pool.memset(k_sb[:, :, 0:WIN], 0.0).then_inc(padded, 1)
            with pool.Fori(0, DEPTH) as l:
                pool.wait_ge(w_in, l * NW + NW)
                apart(pool, chip)
                with pool.Fori(0, NB) as b:
                    i = pool.snap(l * NB + b)

                    def weights(n):
                        pool.tensor_copy(wst[:, :, :].rearrange("p a c -> p (a c)"),
                                         wqk[:, bass.ds(n, 1), :].rearrange("p a c -> p (a c)")).then_inc(wst_ready, 1)

                    pool.wait_ge(k_made, AHEAD + i * NG)
                    pool.wait_ge(wst_ready, AHEAD + i * (NG + 1))
                    apart(pool, chip)
                    weights(0)

                    def steps(g, par, runs, behind, n):
                        r = None if n is None else i * NG + n
                        if n is None:
                            return
                        pool.wait_ge(k_turned, AHEAD + r + 1)
                        pool.tensor_tensor(t1[:, 1, :], t1[:, 1, :], t2[:, 1, :], ALU.add).then_inc(k_added, 1)
                        pool.wait_ge(ss_kept, AHEAD + r + 1)
                        pool.wait_ge(rk_spread, AHEAD + r)
                        pool.tensor_tensor(rn[:, :, :].rearrange("p t a -> p (t a)"),
                                           ss[:, :, :].rearrange("p t a -> p (t a)"),
                                           chip.mhalf[:, 0:4 * TT], ALU.pow).then_inc(rn_ready, 1)
                        pool.wait_ge(rn_ready, AHEAD + r + 1)
                        apart(pool, chip)
                        pool.tensor_copy(
                            rkb[:, :, :].rearrange("p t (a c) -> p t a c", a=2),
                            rn[:, :, 2:4].rearrange("p t (a c) -> p t a c", c=1).to_broadcast([P, TT, 2, LD]))\
                            .then_inc(rkb_ready, 1)
                        pool.tensor_scalar(nscale[:, 1 - par, :, :], rn[:, :, 0:2], -QKS, None, ALU.mult)
                        pool.tensor_tensor(q_sb[:, 1 - par, :], t1[:, 0, :], t2[:, 0, :], ALU.add).then_inc(q_ready, 1)
                        pool.wait_ge(k_made, AHEAD + r + 1)
                        apart(pool, chip)
                        weights(n + 1)

                    groups(pool, steps)
                    pool.wait_ge(sv_kept, AHEAD + i + 1)
                    pool.tensor_tensor(rv[:, :], sv[:, :], chip.mhalf[:, 0:TT], ALU.pow).then_inc(rv_ready, 1)
                pool.wait_ge(y_done, AHEAD + l * NB + NB)
                apart(pool, chip)
                pool.sem_inc(layer_done, 1)

    with ExitStack() as ctx:
        m = Scope(chip, "lo", ctx)
        cur = m.sb("cur", [P, S])
        cur_ready = m.sem("cur_ready")
        turned = m.sem("turned")
        added = m.sem("added")
        block = ctx.enter_context(nc.Block())

        @block.sync
        def _(sp):
            m.start(sp)

        @block.gpsimd
        def _(pool):
            with pool.Fori(0, NB) as b:
                pool.wait_ge(turned, AHEAD + b)
                pool.tensor_copy(cur[:, :], yT[:, bass.ts(b, S)]).then_inc(cur_ready, 1)

        @block.tensor
        def _(pe):
            with pe.Fori(0, NB) as b:
                pe.wait_ge(cur_ready, AHEAD + b + 1)
                pe.wait_ge(added, AHEAD + b)
                for t in range(TT):
                    ins = pe.transpose(bank[:, 0, t * P:(t + 1) * P], cur[:, t * P:(t + 1) * P], ident[:, :])
                ins.then_inc(turned, 1)

        @block.vector
        def _(dve):
            with dve.Fori(0, NB) as b:
                dve.wait_ge(turned, AHEAD + b + 1)
                xb = chip.x[:, bass.ts(b, TT), :]
                dve.tensor_tensor(xb, xb, bank[:, 0, :].rearrange("p (t d) -> p t d", d=D), ALU.add).then_inc(added, 1)


def batch_softmax_attention(chip):
    nc, dram, bank = chip.nc, chip.dram, chip.bank
    sq128 = 1.0 / float(np.sqrt(np.float32(D)))
    with ExitStack() as outer:
        mo = Scope(chip, "b", outer)
        v_all = mo.sb("v", [P, NT, D])
        norm_stage(chip, "bn", dram["w_b_v"], v_all)
        qT = mo.sb("qT", [P, NB * S])
        kR = mo.sb("kR", [P, NB, S])
        with ExitStack() as ctx:
            m = Scope(chip, "bp", ctx)
            w = m.sb("w", [P, 2, D])
            cur = m.sb("cur", [P, TT, P])
            w_in = m.dma_sem("w_in")
            cur_ready = m.sem("cur_ready")
            q_made = m.sem("q_made")
            k_made = m.sem("k_made")
            q_kept = m.sem("q_kept")
            k_kept = m.sem("k_kept")
            block = ctx.enter_context(nc.Block())

            @block.sync
            def _(sp):
                m.start(sp)
                sp.dma_start(w[:, :, :], dram["w_b_qk"].rearrange("p (a c) -> p a c", c=D)).then_inc(w_in, 16)

            @block.gpsimd
            def _(pool):
                with pool.Fori(0, NB) as b:
                    pool.wait_ge(k_made, AHEAD + b)
                    pool.tensor_copy(cur[:, :, :], chip.xT[:, bass.ts(b, S)].rearrange("p (r c) -> p c r", c=TT))\
                        .then_inc(cur_ready, 1)

            @block.tensor
            def _(pe):
                pe.wait_ge(w_in, 16)
                with pe.Fori(0, NB) as b:
                    pe.wait_ge(q_kept, AHEAD + b)
                    pe.matmul(bank[:, 0, :], w[:, 0, :], chip.xT[:, bass.ts(b, S)], start=True, stop=True).then_inc(q_made, 1)
                    pe.wait_ge(cur_ready, AHEAD + b + 1)
                    pe.wait_ge(k_kept, AHEAD + b)
                    apart(pe, chip)
                    for c in range(TT):
                        ins = pe.matmul(bank[:, 1, c * P:(c + 1) * P], cur[:, c, :], w[:, 1, :], start=True, stop=True)
                    ins.then_inc(k_made, 1)

            @block.scalar
            def _(act):
                with act.Fori(0, NB) as b:
                    act.wait_ge(q_made, AHEAD + b + 1)
                    apart(act, chip)
                    act.activation(qT[:, bass.ts(b, S)], bank[:, 0, :], ACT.Copy).then_inc(q_kept, 1)

            @block.vector
            def _(dve):
                with dve.Fori(0, NB) as b:
                    dve.wait_ge(k_made, AHEAD + b + 1)
                    apart(dve, chip)
                    dve.tensor_copy(kR[:, bass.ds(b, 1), :], bank[:, 1:2, :]).then_inc(k_kept, 1)

        with ExitStack() as ctx:
            m = Scope(chip, "bs", ctx)
            mx = m.sb("mx", [P, S])
            sm = m.sb("sm", [P, S])
            e = m.sb("e", [P, NB, S])
            at = m.sb("at", [P, NB, S])
            s_made = m.sem("s_made")
            dve_step = m.sem("dve_step")
            e_in = m.sem("e_in")
            e_ready = m.sem("e_ready")
            a_ready = m.sem("a_ready")
            at_ready = m.sem("at_ready")
            o_made = m.sem("o_made")
            o_added = m.sem("o_added")
            block = ctx.enter_context(nc.Block())

            def over_batches(t):
                return t.rearrange("p b i -> p i b")

            @block.sync
            def _(sp):
                m.start(sp)

            @block.tensor
            def _(pe):
                for j in range(TT):
                    for b in range(NB):
                        pe.wait_ge(o_added, AHEAD + j * NB)
                        pe.matmul(bank[:, b, :], kR[:, b, j * P:(j + 1) * P], qT[:, b * S:(b + 1) * S],
                                  start=True, stop=True).then_inc(s_made, 1)
                    for b in range(NB):
                        pe.wait_ge(at_ready, AHEAD + j * NB + b + 1)
                        pe.wait_ge(e_in, AHEAD + (j + 1) * NB)
                        for i in range(TT):
                            ins = pe.matmul(bank[:, b, i * P:(i + 1) * P], at[:, b, i * P:(i + 1) * P],
                                            v_all[:, b * TT + j, :], start=True, stop=True)
                        ins.then_inc(o_made, 1)

            @block.vector
            def _(dve):
                for j in range(TT):
                    link = linker(dve, dve_step, j * 3, 3)
                    dve.wait_ge(s_made, AHEAD + (j + 1) * NB)
                    link(dve.tensor_reduce(mx[:, :], over_batches(bank[:, :, :]), AX.X, ALU.max))
                    for b in range(NB):
                        dve.tensor_tensor(e[:, b, :], bank[:, b, :], mx[:, :], ALU.subtract).then_inc(e_in, 1)
                    dve.wait_ge(e_ready, AHEAD + (j + 1) * NB)
                    link(dve.tensor_reduce(sm[:, :], over_batches(e[:, :, :]), AX.X, ALU.add))
                    link(dve.reciprocal(sm[:, :], sm[:, :]))
                    for b in range(NB):
                        dve.tensor_tensor(e[:, b, :], e[:, b, :], sm[:, :], ALU.mult).then_inc(a_ready, 1)
                    link.check()
                    for b in range(NB):
                        dve.wait_ge(o_made, AHEAD + j * NB + b + 1)
                        xb = chip.x[:, b * TT:(b + 1) * TT, :]
                        dve.tensor_tensor(xb, xb, bank[:, b, :].rearrange("p (t d) -> p t d", d=D), ALU.add)\
                            .then_inc(o_added, 1)
                        dve.wait_ge(o_added, AHEAD + j * NB + b + 1)

            @block.scalar
            def _(act):
                for j in range(TT):
                    for b in range(NB):
                        act.wait_ge(e_in, AHEAD + j * NB + b + 1)
                        act.activation(e[:, b, :], e[:, b, :], ACT.Exp, scale=sq128).then_inc(e_ready, 1)

            @block.gpsimd
            def _(pool):
                for j in range(TT):
                    for b in range(NB):
                        pool.wait_ge(a_ready, AHEAD + j * NB + b + 1)
                        pool.affine_select(out=at[:, b, :], in_=e[:, b, :], pattern=[[1, S]], compare_op=ALU.is_ge,
                                           fill=1e-9, base=-j * P, channel_multiplier=-1).then_inc(at_ready, 1)


NE4 = 8


def argmax_experts(chip):
    nc, dram, bank = chip.nc, chip.dram, chip.bank
    norm_stage(chip, "en")
    with ExitStack() as ctx:
        m = Scope(chip, "e", ctx)
        wg = m.sb("wg", [P, D])
        we = m.sb("we", [P, NE4 * D])
        be = m.sb("be", [1, NE4 * D])
        bg = m.sb("bg", [P, D])
        rev = m.sb("rev", [P, D])
        cur = m.sb("cur", [P, 2, S])
        lg = m.sb("lg", [P, TT, D])
        pr = m.sb("pr", [P, TT, D])
        eq = m.sb("eq", [P, TT, D])
        red = m.sb("red", [P, 4, TT])
        rcp = m.sb("rcp", [P, TT])
        oh = m.sb("oh", [P, TT, NE4])
        acc = m.sb("acc", [P, 2, D])
        w_in = m.dma_sem("w_in")
        cur_ready = m.sem("cur_ready")
        g_made = m.sem("g_made")
        g_read = m.sem("g_read")
        shifted = m.sem("shifted")
        e_ready = m.sem("e_ready")
        dve_step = m.sem("dve_step")
        h_made = m.sem("h_made")
        h_read = m.sem("h_read")
        block = ctx.enter_context(nc.Block())
        STEPS = 10 + TT * (NE4 + 1)

        @block.sync
        def _(sp):
            m.start(sp)
            sp.dma_start(wg[:, :], dram["w_e_g"]).then_inc(w_in, 16)
            sp.dma_start(we[:, :], dram["w_e_e"]).then_inc(w_in, 16)
            sp.dma_start(be[:, :], dram["w_e_be"]).then_inc(w_in, 16)
            sp.dma_start(bg[:, :], dram["w_e_bg"].partition_broadcast(P)).then_inc(w_in, 16)
            sp.dma_start(rev[:, :], dram["c_rev"]).then_inc(w_in, 16)

        @block.gpsimd
        def _(pool):
            with pool.Fori(0, NB // 2) as k:
                for r in range(2):
                    b = 2 * k + r
                    pool.wait_ge(h_made, AHEAD + 2 * k * TT)
                    pool.tensor_copy(cur[:, r, :], chip.xT[:, bass.ts(b, S)]).then_inc(cur_ready, 1)

        @block.tensor
        def _(pe):
            pe.wait_ge(w_in, 80)
            with pe.Fori(0, NB // 2) as k:
                for r in range(2):
                    b = 2 * k + r
                    pe.wait_ge(cur_ready, AHEAD + b + 1)
                    pe.wait_ge(g_read, AHEAD + b)
                    apart(pe, chip)
                    for t in range(TT):
                        ins = pe.matmul(bank[:, 0, t * P:(t + 1) * P], cur[:, r, t * P:(t + 1) * P], wg[:, :],
                                        start=True, stop=True)
                    ins.then_inc(g_made, 1)
                    for t in range(TT):
                        first = 2 + 2 * (t % 2)
                        pe.wait_ge(h_read, AHEAD + b * TT + max(t - 1, 0))
                        apart(pe, chip)
                        for half in range(2):
                            cols = slice(half * 4 * D, (half + 1) * 4 * D)
                            pe.matmul(bank[:, first + half, :], cur[:, r, t * P:(t + 1) * P], we[:, cols],
                                      start=True, stop=False)
                            ins = pe.matmul(bank[:, first + half, :], chip.ones[0:1, :], be[:, cols], start=False, stop=True)
                        ins.then_inc(h_made, 1)

        @block.scalar
        def _(act):
            with act.Fori(0, NB) as b:
                act.wait_ge(shifted, AHEAD + b + 1)
                act.activation(pr[:, :, :], lg[:, :, :], ACT.Exp).then_inc(e_ready, 1)

        @block.vector
        def _(dve):
            dve.wait_ge(w_in, 80)

            def per_tile(v):
                return v.rearrange("p (t a) -> p t a", a=1).to_broadcast([P, TT, D])

            def per_class(v):
                return v.rearrange("p (a c) -> p a c", a=1).to_broadcast([P, TT, D])

            with dve.Fori(0, NB) as b:
                link = linker(dve, dve_step, b * STEPS, STEPS)
                dve.wait_ge(g_made, AHEAD + b + 1)
                ins = dve.tensor_tensor(lg[:, :, :], bank[:, 0, :].rearrange("p (t c) -> p t c", c=D), per_class(bg[:, :]), ALU.add)
                ins.then_inc(g_read, 1)
                dve.wait_ge(g_read, AHEAD + b + 1)
                link(dve.tensor_reduce(red[:, 0, :], lg[:, :, :], AX.X, ALU.max))
                dve.tensor_tensor(lg[:, :, :], lg[:, :, :], per_tile(red[:, 0, :]), ALU.subtract).then_inc(shifted, 1)
                dve.wait_ge(e_ready, AHEAD + b + 1)
                link(dve.tensor_reduce(red[:, 1, :], pr[:, :, :], AX.X, ALU.add))
                link(dve.reciprocal(rcp[:, :], red[:, 1, :]))
                link(dve.tensor_tensor(pr[:, :, :], pr[:, :, :], per_tile(rcp[:, :]), ALU.mult))
                link(dve.tensor_reduce(red[:, 2, :], pr[:, :, :], AX.X, ALU.max))
                link(dve.tensor_tensor(eq[:, :, :], pr[:, :, :], per_tile(red[:, 2, :]), ALU.is_equal))
                link(dve.tensor_tensor(eq[:, :, :], eq[:, :, :], per_class(rev[:, :]), ALU.mult))
                link(dve.tensor_reduce(red[:, 3, :], eq[:, :, :], AX.X, ALU.max))
                link(dve.tensor_tensor(eq[:, :, :], per_class(rev[:, :]), per_tile(red[:, 3, :]), ALU.is_equal))
                link(dve.tensor_reduce(oh[:, :, :], eq[:, :, :].rearrange("p t (a e) -> p t e a", e=NE4), AX.X, ALU.max))
                for t in range(TT):
                    first = 2 + 2 * (t % 2)
                    dve.wait_ge(h_made, AHEAD + b * TT + t + 1)
                    apart(dve, chip)
                    for e in range(NE4):
                        h = bank[:, first + e // 4, (e % 4) * D:(e % 4 + 1) * D]
                        sel = oh[:, t, e:e + 1]
                        if e == 0:
                            link(dve.tensor_scalar(acc[:, t % 2, :], h, sel, None, ALU.mult))
                        else:
                            link(dve.scalar_tensor_tensor(acc[:, t % 2, :], h, sel, acc[:, t % 2, :], ALU.mult, ALU.add))
                    link(dve.tensor_scalar(acc[:, t % 2, :], acc[:, t % 2, :], 0.0, red[:, 2, t:t + 1], ALU.max, ALU.mult))
                    xt = chip.x[:, b * TT + t, :]
                    ins = dve.tensor_tensor(xt, xt, acc[:, t % 2, :], ALU.add)
                    ins.then_inc(h_read, 1)
                    dve.wait_ge(h_read, AHEAD + b * TT + t + 1)
                link.check()


DI = 256
NS5 = 128
SH5 = 32
SP5 = DI // SH5
KC = 4
XC = (DI + 2 * NS5) // P
HGRP = 4
DT_MIN, DT_MAX = 0.001, 0.1


def state_space(chip):
    nc, dram, bank, ident = chip.nc, chip.dram, chip.bank, chip.ident
    with ExitStack() as outer:
        mo = Scope(chip, "s", outer)
        xn_all = mo.sb("xn", [P, NT, D])
        norm_stage(chip, "sn", keep=xn_all)
        with ExitStack() as ctx:
            m = Scope(chip, "sx", ctx)
            w_x = m.sb("w_x", [P, XC, P])
            w_z = m.sb("w_z", [P, DI])
            w_dt = m.sb("w_dt", [P, SH5])
            w_o = m.sb("w_o", [P, 2, D])
            taps = m.sb("taps", [P, XC, KC + 1])
            rows = m.sb("rows", [P, 3 * SH5 + DI + 2 * D])
            upto = m.sb("upto", [P, P])
            pick = m.sb("pick", [SH5, SH5, P])
            acoef = m.sb("acoef", [P, SH5])
            cur = m.sb("cur", [P, S])
            cvin = m.sb("cvin", [P, XC, KC - 1 + S])
            cacc = m.sb("cacc", [P, XC, S])
            u = m.sb("u", [P, XC, S])
            sz = m.sb("sz", [P, TT, DI])
            dtr = m.sb("dtr", [P, TT, SH5])
            sg = m.sb("sg", [P, TT, SH5])
            dt = m.sb("dt", [P, TT, SH5])
            dA = m.sb("dA", [P, TT, SH5])
            xs = m.sb("xs", [P, TT, DI])
            bt = m.sb("bt", [P, TT, NS5])
            cum = m.sb("cum", [P, 2 * SH5])
            acT = m.sb("acT", [SH5, P])
            nac = m.sb("nac", [P, SH5])
            dif = m.sb("dif", [P, SH5])
            ex = m.sb("ex", [P, 3, SH5])
            xdt = m.sb("xdt", [P, DI])
            xdd = m.sb("xdd", [P, DI])
            cbm = m.sb("cbm", [P, P])
            tmin = m.sb("tmin", [P, 2, HGRP, P])
            mm = m.sb("mm", [P, 2, HGRP, P])
            state = m.sb("state", [P, DI])
            y = m.sb("y", [P, TT, DI])
            t1 = m.sb("t1", [P, DI])
            ysq = m.sb("ysq", [P, DI])
            ms = m.sb("ms", [P, TT])
            ms2 = m.sb("ms2", [P, TT])
            rms = m.sb("rms", [P, TT])
            yT = m.sb("yT", [P, 2, S])
            stats = m.sb("stats", [P, TT, 6])
            mv = m.sb("mv", [P, TT, 2])
            ve = m.sb("ve", [P, TT])
            rstd = m.sb("rstd", [P, TT])
            ln = m.sb("ln", [P, TT, D])
            w_in = m.dma_sem("w_in")
            a_exp = m.sem("a_exp")
            zeroed = m.sem("zeroed")
            cur_ready = m.sem("cur_ready")
            xbc_made = m.sem("xbc_made")
            cv_ready = m.sem("cv_ready")
            conv_done = m.sem("conv_done")
            u_ready = m.sem("u_ready")
            z_made = m.sem("z_made")
            sz_ready = m.sem("sz_ready")
            dt_made = m.sem("dt_made")
            dtr_ready = m.sem("dtr_ready")
            sg_ready = m.sem("sg_ready")
            dA_ready = m.sem("dA_ready")
            tok_made = m.sem("tok_made")
            tok_kept = m.sem("tok_kept")
            cum_made = m.sem("cum_made")
            cum_kept = m.sem("cum_kept")
            dif_ready = m.sem("dif_ready")
            ex_ready = m.sem("ex_ready")
            cb_made = m.sem("cb_made")
            cb_read = m.sem("cb_read")
            xdd_ready = m.sem("xdd_ready")
            st_made = m.sem("st_made")
            state_ready = m.sem("state_ready")
            ab_made = m.sem("ab_made")
            min_ready = m.sem("min_ready")
            seg_ready = m.sem("seg_ready")
            mm_ready = m.sem("mm_ready")
            yd_part = m.sem("yd_part")
            y_read = m.sem("y_read")
            y_gated = m.sem("y_gated")
            ms_ready = m.sem("ms_ready")
            ms2_ready = m.sem("ms2_ready")
            rms_ready = m.sem("rms_ready")
            yn_ready = m.sem("yn_ready")
            yT_made = m.sem("yT_made")
            yT_kept = m.sem("yT_kept")
            out_made = m.sem("out_made")
            ve_ready = m.sem("ve_ready")
            rstd_ready = m.sem("rstd_ready")
            x_done = m.sem("x_done")
            dve_step = m.sem("dve_step")
            block = ctx.enter_context(nc.Block())
            NHG = SH5 // HGRP

            def row(k, n):
                return rows[:, k:k + n]
            A_LOG, DT_B, D_SK = row(0, SH5), row(SH5, SH5), row(2 * SH5, SH5)
            NORM_W, LN_W, LN_B = row(3 * SH5, DI), row(3 * SH5 + DI, D), row(3 * SH5 + DI + D, D)

            @block.sync
            def _(sp):
                m.start(sp)
                sp.dma_start(w_x[:, :, :], dram["w_s_x"].rearrange("p (a c) -> p a c", c=P)).then_inc(w_in, 16)
                sp.dma_start(w_z[:, :], dram["w_s_z"]).then_inc(w_in, 16)
                sp.dma_start(w_dt[:, :], dram["w_s_dt"]).then_inc(w_in, 16)
                sp.dma_start(w_o[:, :, :], dram["w_s_o"].rearrange("(a p) d -> p a d", p=P)).then_inc(w_in, 16)
                sp.dma_start(taps[:, :, :], dram["w_s_taps"].rearrange("(a p) k -> p a k", p=P)).then_inc(w_in, 16)
                sp.dma_start(rows[:, :], dram["w_s_rows"].partition_broadcast(P)).then_inc(w_in, 16)
                sp.dma_start(upto[:, :], dram["c_upto"]).then_inc(w_in, 16)
                sp.dma_start(pick[:, :, :], dram["c_pick5"].rearrange("k (a c) -> k a c", c=P)).then_inc(w_in, 16)

            @block.gpsimd
            def _(pool):
                pool.memset(cvin[:, :, 0:KC - 1], 0.0).then_inc(zeroed, 1)
                with pool.Fori(0, NB) as b:
                    pool.wait_ge(out_made, AHEAD + b)
                    pool.tensor_copy(cur[:, :], chip.xT[:, bass.ts(b, S)]).then_inc(cur_ready, 1)
                    pool.wait_ge(ms2_ready, AHEAD + b + 1)
                    pool.tensor_tensor(rms[:, :], ms2[:, :], chip.mhalf[:, 0:TT], ALU.pow).then_inc(rms_ready, 1)
                    pool.wait_ge(ve_ready, AHEAD + b + 1)
                    pool.tensor_tensor(rstd[:, :], ve[:, :], chip.mhalf[:, 0:TT], ALU.pow).then_inc(rstd_ready, 1)

            @block.tensor
            def _(pe):
                pe.wait_ge(w_in, 128)
                with pe.Fori(0, NB) as b:
                    pe.wait_ge(cur_ready, AHEAD + b + 1)
                    pe.wait_ge(x_done, AHEAD + b)
                    for c in range(XC):
                        if c >= 2:
                            pe.wait_ge(cv_ready, AHEAD + b * XC + c - 1)
                        apart(pe, chip)
                        pe.matmul(bank[:, c % 2, :], w_x[:, c, :], cur[:, :], start=True, stop=True).then_inc(xbc_made, 1)
                    for t in range(TT):
                        ins = pe.matmul(bank[:, 2 + t // 2, (t % 2) * DI:(t % 2 + 1) * DI], cur[:, t * P:(t + 1) * P], w_z[:, :],
                                        start=True, stop=True)
                    ins.then_inc(z_made, 1)
                    for t in range(TT):
                        ins = pe.matmul(bank[:, 4, t * SH5:(t + 1) * SH5], cur[:, t * P:(t + 1) * P], w_dt[:, :],
                                        start=True, stop=True)
                    ins.then_inc(dt_made, 1)
                    pe.wait_ge(u_ready, AHEAD + b * XC + 3)
                    apart(pe, chip)
                    for t in range(TT):
                        for c in range(2):
                            pe.transpose(bank[:, 5 + t // 2, (t % 2) * DI + c * P:(t % 2) * DI + (c + 1) * P],
                                         u[:, c, t * P:(t + 1) * P], ident[:, :])
                    for t in range(TT):
                        ins = pe.transpose(bank[:, 7, t * P:(t + 1) * P], u[:, 2, t * P:(t + 1) * P], ident[:, :])
                    ins.then_inc(tok_made, 1)
                    pe.wait_ge(u_ready, AHEAD + b * XC + XC)
                    pe.wait_ge(dA_ready, AHEAD + b + 1)
                    pe.wait_ge(tok_kept, AHEAD + b + 1)
                    apart(pe, chip)
                    for t in range(TT):
                        i = b * TT + t
                        tile = slice(t * P, (t + 1) * P)
                        pe.wait_ge(y_read, AHEAD + i)
                        apart(pe, chip)
                        pe.matmul(bank[:, 4, 0:SH5], upto[:, :], dA[:, t, :], start=True, stop=True)
                        pe.matmul(bank[:, 4, SH5:2 * SH5], chip.ones[:, :], dA[:, t, :], start=True, stop=True)
                        pe.matmul(bank[0:SH5, 4, 2 * SH5:2 * SH5 + P], dA[:, t, :], upto[:, :], start=True, stop=True)\
                            .then_inc(cum_made, 1)
                        pe.matmul(bank[:, 5, 0:P], u[:, 2, tile], u[:, 3, tile], start=True, stop=True).then_inc(cb_made, 1)
                        for g in range(NHG + 2):
                            if g < NHG:
                                if g == 0:
                                    pe.wait_ge(cum_kept, AHEAD + i + 1)
                                pe.wait_ge(min_ready, AHEAD + i * NHG + max(g - 1, 0))
                                apart(pe, chip)
                                for k in range(HGRP):
                                    ins = pe.matmul(bank[:, g % 2, k * P:(k + 1) * P], pick[:, g * HGRP + k, :], acT[:, :],
                                                    start=True, stop=True)
                                ins.then_inc(ab_made, 1)
                            if g == 1:
                                pe.wait_ge(xdd_ready, AHEAD + i + 1)
                                pe.wait_ge(state_ready, AHEAD + b * (TT + 1) + t + 1)
                                apart(pe, chip)
                                pe.matmul(bank[:, 6, 0:DI], bt[:, t, :], xdd[:, :], start=True, stop=True)
                                pe.matmul(bank[:, 6, DI:2 * DI], u[:, 3, tile], state[:, :], start=True, stop=True)\
                                    .then_inc(st_made, 1)
                            if g >= 2:
                                pe.wait_ge(mm_ready, AHEAD + i * NHG + g - 1)
                                apart(pe, chip)
                                for k in range(HGRP):
                                    h = (g - 2) * HGRP + k
                                    ins = pe.matmul(bank[:, 7, h * SP5:(h + 1) * SP5], mm[:, g % 2, k, :],
                                                    xdt[:, h * SP5:(h + 1) * SP5], start=True, stop=True)
                                ins.then_inc(yd_part, 1)
                    pe.wait_ge(yn_ready, AHEAD + b + 1)
                    apart(pe, chip)
                    for t in range(TT):
                        for c in range(2):
                            ins = pe.transpose(bank[:, 2 + c, t * P:(t + 1) * P], y[:, t, c * P:(c + 1) * P], ident[:, :])
                    ins.then_inc(yT_made, 1)
                    pe.wait_ge(yT_kept, AHEAD + b + 1)
                    apart(pe, chip)
                    for t in range(TT):
                        for c in range(2):
                            ins = pe.matmul(bank[:, 5, t * D:(t + 1) * D], yT[:, c, t * P:(t + 1) * P], w_o[:, c, :],
                                            start=(c == 0), stop=(c == 1))
                    ins.then_inc(out_made, 1)

            @block.scalar
            def _(act):
                act.wait_ge(w_in, 128)
                act.activation(acoef[:, :], A_LOG, ACT.Exp).then_inc(a_exp, 1)
                with act.Fori(0, NB) as b:
                    for c in range(XC):
                        act.wait_ge(xbc_made, AHEAD + b * XC + c + 1)
                        act.wait_ge(conv_done, AHEAD + b * XC)
                        act.activation(cvin[:, c, KC - 1:], bank[:, c % 2, :], ACT.Copy).then_inc(cv_ready, 1)
                    act.wait_ge(z_made, AHEAD + b + 1)
                    act.activation(sz[:, 0:2, :], bank[:, 2, :].rearrange("p (t c) -> p t c", c=DI), ACT.Silu)
                    act.activation(sz[:, 2:4, :], bank[:, 3, :].rearrange("p (t c) -> p t c", c=DI), ACT.Silu).then_inc(sz_ready, 1)
                    for c in range(XC):
                        act.wait_ge(conv_done, AHEAD + b * XC + c + 1)
                        act.activation(u[:, c, :], cacc[:, c, :], ACT.Silu).then_inc(u_ready, 1)
                    act.wait_ge(dtr_ready, AHEAD + b + 1)
                    act.activation(sg[:, :, :], dtr[:, :, :], ACT.Sigmoid).then_inc(sg_ready, 1)
                    act.wait_ge(tok_made, AHEAD + b + 1)
                    act.activation(xs[:, 0:2, :], bank[:, 5, :].rearrange("p (t c) -> p t c", c=DI), ACT.Copy)
                    act.activation(xs[:, 2:4, :], bank[:, 6, :].rearrange("p (t c) -> p t c", c=DI), ACT.Copy)
                    act.activation(bt[:, :, :], bank[:, 7, :].rearrange("p (t c) -> p t c", c=NS5), ACT.Copy).then_inc(tok_kept, 1)
                    for t in range(TT):
                        i = b * TT + t
                        act.wait_ge(cum_made, AHEAD + i + 1)
                        act.activation(cum[:, :], bank[:, 4, 0:2 * SH5], ACT.Copy)
                        act.activation(acT[:, :], bank[0:SH5, 4, 2 * SH5:2 * SH5 + P], ACT.Copy).then_inc(cum_kept, 1)
                        act.wait_ge(dif_ready, AHEAD + i + 1)
                        act.activation(ex[:, 0:2, :], cum[:, :].rearrange("p (a h) -> p a h", a=2), ACT.Exp)
                        act.activation(ex[:, 2, :], dif[:, :], ACT.Exp).then_inc(ex_ready, 1)
                        for g in range(NHG):
                            act.wait_ge(min_ready, AHEAD + i * NHG + g + 1)
                            for k in range(HGRP):
                                h = g * HGRP + k
                                ins = act.activation(tmin[:, g % 2, k, :], tmin[:, g % 2, k, :], ACT.Exp, bias=nac[:, h:h + 1])
                            ins.then_inc(seg_ready, 1)
                    for t in range(TT):
                        act.wait_ge(y_gated, AHEAD + b * TT + t + 1)
                        act.activation(ysq[:, :], y[:, t, :], ACT.Square, accum_out=ms[:, t:t + 1]).then_inc(ms_ready, 1)
                        act.wait_ge(ms_ready, AHEAD + b * TT + t + 1)
                    act.wait_ge(yT_made, AHEAD + b + 1)
                    act.activation(yT[:, 0, :], bank[:, 2, :], ACT.Copy)
                    act.activation(yT[:, 1, :], bank[:, 3, :], ACT.Copy).then_inc(yT_kept, 1)

            STEPS = SS_STEPS

            @block.vector
            def _(dve):
                dve.wait_ge(w_in, 128)
                dve.wait_ge(a_exp, AHEAD + 1)
                dve.tensor_scalar(acoef[:, :], acoef[:, :], -1.0, None, ALU.mult).then_inc(a_exp, 1)
                dve.wait_ge(a_exp, AHEAD + 2)
                dve.wait_ge(zeroed, AHEAD + 1)

                def heads(v):
                    return v.rearrange("p (h a) -> p h a", a=1).to_broadcast([P, SH5, SP5])

                def by_head(v):
                    return v.rearrange("p (h c) -> p h c", c=SP5)

                with dve.Fori(0, NB) as b:
                    link = linker(dve, dve_step, b * STEPS, STEPS)
                    for c in range(XC):
                        dve.wait_ge(cv_ready, AHEAD + b * XC + c + 1)
                        dve.wait_ge(u_ready, AHEAD + b * XC)
                        apart(dve, chip)
                        link(dve.tensor_scalar(cacc[:, c, :], cvin[:, c, 0:S], taps[:, c, 0:1], None, ALU.mult))
                        for k in range(1, KC):
                            link(dve.scalar_tensor_tensor(cacc[:, c, :], cvin[:, c, k:k + S], taps[:, c, k:k + 1],
                                                          cacc[:, c, :], ALU.mult, ALU.add))
                        dve.tensor_scalar(cacc[:, c, :], cacc[:, c, :], taps[:, c, KC:KC + 1], None, ALU.add)\
                            .then_inc(conv_done, 1)
                    dve.wait_ge(dt_made, AHEAD + b + 1)
                    dve.tensor_tensor(dtr[:, :, :], bank[:, 4, 0:TT * SH5].rearrange("p (t h) -> p t h", h=SH5),
                                      DT_B.rearrange("p (a h) -> p a h", a=1).to_broadcast([P, TT, SH5]), ALU.add)\
                        .then_inc(dtr_ready, 1)
                    link(dve.memset(state[:, :], 0.0))
                    dve.sem_inc(state_ready, 1)
                    dve.wait_ge(sg_ready, AHEAD + b + 1)
                    apart(dve, chip)
                    link(dve.tensor_scalar(dt[:, :, :], sg[:, :, :], DT_MAX - DT_MIN, DT_MIN, ALU.mult, ALU.add))
                    dve.tensor_tensor(dA[:, :, :], dt[:, :, :],
                                      acoef[:, :].rearrange("p (a h) -> p a h", a=1).to_broadcast([P, TT, SH5]), ALU.mult)\
                        .then_inc(dA_ready, 1)
                    dve.wait_ge(tok_kept, AHEAD + b + 1)
                    for t in range(TT):
                        i = b * TT + t
                        link(dve.tensor_tensor(by_head(xdt[:, :]), by_head(xs[:, t, :]), heads(dt[:, t, :]), ALU.mult))
                        dve.wait_ge(cum_kept, AHEAD + i + 1)
                        apart(dve, chip)
                        dve.tensor_scalar(nac[:, :], cum[:, 0:SH5], -1.0, None, ALU.mult)
                        dve.tensor_tensor(dif[:, :], cum[:, SH5:], cum[:, 0:SH5], ALU.subtract).then_inc(dif_ready, 1)
                        dve.wait_ge(cb_made, AHEAD + i + 1)
                        link(dve.tensor_tensor(cbm[:, :], bank[:, 5, 0:P], upto[:, :], ALU.mult))
                        dve.wait_ge(ex_ready, AHEAD + i + 1)
                        dve.tensor_tensor(by_head(xdd[:, :]), by_head(xdt[:, :]), heads(ex[:, 2, :]), ALU.mult)\
                            .then_inc(xdd_ready, 1)
                        for g in range(NHG + 1):
                            if g < NHG:
                                dve.wait_ge(ab_made, AHEAD + i * NHG + g + 1)
                                dve.wait_ge(mm_ready, AHEAD + i * NHG + max(g - 1, 0))
                                own = cum[:, g * HGRP:(g + 1) * HGRP].rearrange("p (h a) -> p h a", a=1).to_broadcast([P, HGRP, P])
                                dve.tensor_tensor(tmin[:, g % 2, :, :], bank[:, g % 2, :].rearrange("p (h q) -> p h q", q=P),
                                                  own, ALU.min).then_inc(min_ready, 1)
                            if g >= 1:
                                dve.wait_ge(seg_ready, AHEAD + i * NHG + g)
                                dve.wait_ge(yd_part, AHEAD + i * NHG + max(g - 2, 0))
                                dve.tensor_tensor(mm[:, (g - 1) % 2, :, :], tmin[:, (g - 1) % 2, :, :],
                                                  cbm[:, :].rearrange("p (a q) -> p a q", a=1).to_broadcast([P, HGRP, P]),
                                                  ALU.mult).then_inc(mm_ready, 1)
                        dve.wait_ge(st_made, AHEAD + i + 1)
                        link(dve.tensor_tensor(by_head(y[:, t, :]), by_head(bank[:, 6, DI:2 * DI]), heads(ex[:, 0, :]), ALU.mult))
                        link(dve.tensor_tensor(by_head(t1[:, :]), by_head(xs[:, t, :]), heads(D_SK), ALU.mult))
                        link(dve.tensor_tensor(y[:, t, :], y[:, t, :], t1[:, :], ALU.add))
                        link(dve.tensor_tensor(by_head(state[:, :]), by_head(state[:, :]), heads(ex[:, 1, :]), ALU.mult))
                        link(dve.tensor_tensor(state[:, :], state[:, :], bank[:, 6, 0:DI], ALU.add))
                        dve.sem_inc(state_ready, 1)
                        dve.wait_ge(yd_part, AHEAD + (i + 1) * NHG)
                        dve.tensor_tensor(y[:, t, :], y[:, t, :], bank[:, 7, 0:DI], ALU.add).then_inc(y_read, 1)
                        dve.wait_ge(y_read, AHEAD + i + 1)
                        dve.wait_ge(sz_ready, AHEAD + b + 1)
                        dve.tensor_tensor(y[:, t, :], y[:, t, :], sz[:, t, :], ALU.mult).then_inc(y_gated, 1)
                    dve.wait_ge(ms_ready, AHEAD + (b + 1) * TT)
                    apart(dve, chip)
                    dve.tensor_scalar(ms2[:, :], ms[:, :], 1.0 / DI, EPS, ALU.mult, ALU.add).then_inc(ms2_ready, 1)
                    dve.wait_ge(rms_ready, AHEAD + b + 1)
                    apart(dve, chip)
                    for t in range(TT):
                        ins = dve.scalar_tensor_tensor(y[:, t, :], y[:, t, :], rms[:, t:t + 1], NORM_W, ALU.mult, ALU.mult)
                    ins.then_inc(yn_ready, 1)
                    dve.wait_ge(out_made, AHEAD + b + 1)
                    apart(dve, chip)
                    for t in range(TT):
                        ins = dve.bn_stats(stats[:, t, :], bank[:, 5, t * D:(t + 1) * D])
                    link(ins)
                    apart(dve, chip)
                    for t in range(TT):
                        ins = dve.bn_aggr(mv[:, t, :], stats[:, t, :])
                    link(ins)
                    apart(dve, chip)
                    dve.tensor_scalar(ve[:, :], mv[:, :, 1], EPS, None, ALU.add).then_inc(ve_ready, 1)
                    dve.wait_ge(rstd_ready, AHEAD + b + 1)
                    apart(dve, chip)
                    for t in range(TT):
                        ins = dve.tensor_scalar(ln[:, t, :], bank[:, 5, t * D:(t + 1) * D], mv[:, t, 0:1], rstd[:, t:t + 1],
                                                ALU.subtract, ALU.mult)
                    link(ins)
                    wide = lambda v: v.rearrange("p (a d) -> p a d", a=1).to_broadcast([P, TT, D])
                    link(dve.tensor_tensor(ln[:, :, :], ln[:, :, :], wide(LN_W), ALU.mult))
                    link(dve.tensor_tensor(ln[:, :, :], ln[:, :, :], wide(LN_B), ALU.add))
                    link(dve.tensor_tensor(ln[:, :, :], ln[:, :, :], xn_all[:, bass.ts(b, TT), :], ALU.add))
                    xb = chip.x[:, bass.ts(b, TT), :]
                    dve.tensor_tensor(xb, xb, ln[:, :, :], ALU.add).then_inc(x_done, 1)
                    link.check()


SS_STEPS = XC * KC + 2 + TT * 7 + 6


def first_of_top(dve, link, src, top, rev, tmp, top_rev, onehot, shape):
    def along(v):
        return v.rearrange("p (t a) -> p t a", a=1).to_broadcast(shape)

    def across(v):
        return v.rearrange("p (a c) -> p a c", a=1).to_broadcast(shape)

    link(dve.tensor_reduce(top, src, AX.X, ALU.max))
    link(dve.tensor_tensor(tmp, src, along(top), ALU.is_equal))
    link(dve.tensor_tensor(tmp, tmp, across(rev), ALU.mult))
    link(dve.tensor_reduce(top_rev, tmp, AX.X, ALU.max))
    link(dve.tensor_tensor(onehot, across(rev), along(top_rev), ALU.is_equal))


NE6 = 8
CAP = 160
H6 = 512
HC6 = H6 // P
K6 = NE6 + 1


def capacity_experts(chip):
    nc, dram, bank, ident = chip.nc, chip.dram, chip.bank, chip.ident
    norm_stage(chip, "cn")
    with ExitStack() as outer:
        mo = Scope(chip, "c", outer)
        selT = mo.sb("selT", [K6, NB * S])
        with ExitStack() as ctx:
            m = Scope(chip, "cr", ctx)
            rw = m.sb("rw", [P, NE6])
            rb = m.sb("rb", [P, NE6])
            rev = m.sb("rev", [P, D])
            upto = m.sb("upto", [P, P])
            lg = m.sb("lg", [P, NT, NE6])
            pr = m.sb("pr", [P, NT, NE6])
            tmp = m.sb("tmp", [P, NT, NE6])
            oh = m.sb("oh", [P, NT, NE6])
            tot = m.sb("tot", [P, 2, NT, NE6])
            sel = m.sb("sel", [P, NT, K6])
            red = m.sb("red", [P, 4, NT])
            w_in = m.dma_sem("w_in")
            made = m.sem("made")
            dve_step = m.sem("dve_step")
            shifted = m.sem("shifted")
            e_ready = m.sem("e_ready")
            oh_ready = m.sem("oh_ready")
            counted = m.sem("counted")
            sel_ready = m.sem("sel_ready")
            turned = m.sem("turned")
            kept = m.sem("kept")
            block = ctx.enter_context(nc.Block())
            SH = [P, NT, NE6]

            @block.sync
            def _(sp):
                m.start(sp)
                sp.dma_start(rw[:, :], dram["w_c_r"]).then_inc(w_in, 16)
                sp.dma_start(rb[:, :], dram["w_c_rb"].partition_broadcast(P)).then_inc(w_in, 16)
                sp.dma_start(rev[:, :], dram["c_rev"]).then_inc(w_in, 16)
                sp.dma_start(upto[:, :], dram["c_upto"]).then_inc(w_in, 16)

            @block.tensor
            def _(pe):
                pe.wait_ge(w_in, 64)
                for n in range(NT):
                    ins = pe.matmul(bank[:, 0, n * NE6:(n + 1) * NE6], chip.xT[:, n * P:(n + 1) * P], rw[:, :],
                                    start=True, stop=True)
                ins.then_inc(made, 1)
                pe.wait_ge(oh_ready, AHEAD + 1)
                flat = oh[:, :, :].rearrange("p t e -> p (t e)")
                pe.matmul(bank[:, 1, 0:NT * NE6], upto[:, :], flat, start=True, stop=True)
                pe.matmul(bank[:, 2, 0:NT * NE6], chip.ones[:, :], flat, start=True, stop=True).then_inc(counted, 1)
                pe.wait_ge(sel_ready, AHEAD + 1)
                for b in range(NB):
                    if b >= 2:
                        pe.wait_ge(kept, AHEAD + b - 1)
                    for t in range(TT):
                        ins = pe.transpose(bank[0:K6, 3 + b % 2, t * P:(t + 1) * P], sel[:, b * TT + t, :], ident[:, :])
                    ins.then_inc(turned, 1)

            @block.scalar
            def _(act):
                act.wait_ge(shifted, AHEAD + 1)
                act.activation(pr[:, :, :], lg[:, :, :], ACT.Exp).then_inc(e_ready, 1)
                for b in range(NB):
                    act.wait_ge(turned, AHEAD + b + 1)
                    act.activation(selT[:, b * S:(b + 1) * S], bank[0:K6, 3 + b % 2, :], ACT.Copy).then_inc(kept, 1)

            @block.vector
            def _(dve):
                dve.wait_ge(w_in, 64)
                link = linker(dve, dve_step, 0, 19)
                dve.wait_ge(made, AHEAD + 1)
                link(dve.tensor_tensor(lg[:, :, :], bank[:, 0, 0:NT * NE6].rearrange("p (t e) -> p t e", e=NE6),
                                       rb[:, :].rearrange("p (a e) -> p a e", a=1).to_broadcast(SH), ALU.add))
                link(dve.tensor_reduce(red[:, 0, :], lg[:, :, :], AX.X, ALU.max))
                dve.tensor_tensor(lg[:, :, :], lg[:, :, :],
                                  red[:, 0, :].rearrange("p (t a) -> p t a", a=1).to_broadcast(SH), ALU.subtract)\
                    .then_inc(shifted, 1)
                dve.wait_ge(e_ready, AHEAD + 1)
                link(dve.tensor_reduce(red[:, 1, :], pr[:, :, :], AX.X, ALU.add))
                link(dve.reciprocal(red[:, 1, :], red[:, 1, :]))
                link(dve.tensor_tensor(pr[:, :, :], pr[:, :, :],
                                       red[:, 1, :].rearrange("p (t a) -> p t a", a=1).to_broadcast(SH), ALU.mult))
                first_of_top(dve, link, pr[:, :, :], red[:, 2, :], rev[:, 0:NE6], tmp[:, :, :], red[:, 3, :], oh[:, :, :], SH)
                dve.sem_inc(oh_ready, 1)
                dve.wait_ge(counted, AHEAD + 1)
                link(dve.tensor_copy(tot[:, 0, :, :], bank[:, 2, 0:NT * NE6].rearrange("p (t e) -> p t e", e=NE6)))
                src = 0
                step = 1
                while step < NT:
                    dve.tensor_tensor(tot[:, 1 - src, step:, :], tot[:, src, step:, :], tot[:, src, 0:NT - step, :], ALU.add)
                    link(dve.tensor_copy(tot[:, 1 - src, 0:step, :], tot[:, src, 0:step, :]))
                    src, step = 1 - src, 2 * step
                rank = tmp
                dve.tensor_copy(rank[:, 0, :], bank[:, 1, 0:NE6])
                link(dve.tensor_tensor(rank[:, 1:, :], bank[:, 1, NE6:NT * NE6].rearrange("p (t e) -> p t e", e=NE6),
                                       tot[:, src, 0:NT - 1, :], ALU.add))
                link(dve.scalar_tensor_tensor(sel[:, :, 0:NE6], rank[:, :, :], float(CAP), oh[:, :, :], ALU.is_le, ALU.mult))
                link(dve.tensor_reduce(red[:, 0, :], sel[:, :, 0:NE6], AX.X, ALU.add))
                dve.tensor_scalar(sel[:, :, NE6], red[:, 0, :], -1.0, 1.0, ALU.mult, ALU.add).then_inc(sel_ready, 1)
                link.check()

        with ExitStack() as ctx:
            m = Scope(chip, "cx", ctx)
            w1 = m.sb("w1", [P, K6 * HC6, P])
            w2 = m.sb("w2", [P, K6 * HC6, D])
            b1 = m.sb("b1", [P, K6 * HC6])
            b2 = m.sb("b2", [K6, D])
            pick = m.sb("pick", [K6, K6, P])
            rl = m.sb("rl", [P, 2, S])
            hm = m.sb("hm", [P, 2, S])
            w_in = m.dma_sem("w_in")
            spread = m.sem("spread")
            h_made = m.sem("h_made")
            rl_ready = m.sem("rl_ready")
            hm_ready = m.sem("hm_ready")
            used = m.sem("used")
            tail = Tail(m)
            block = ctx.enter_context(nc.Block())
            N = K6 * HC6

            @block.sync
            def _(sp):
                m.start(sp)
                sp.dma_start(w1[:, :, :], dram["w_c_1"].rearrange("p (a c) -> p a c", c=P)).then_inc(w_in, 16)
                sp.dma_start(w2[:, :, :], dram["w_c_2"].rearrange("(a p) d -> p a d", p=P)).then_inc(w_in, 16)
                sp.dma_start(b1[:, :], dram["w_c_b1"]).then_inc(w_in, 16)
                sp.dma_start(b2[:, :], dram["w_c_b2"]).then_inc(w_in, 16)
                sp.dma_start(pick[:, :, :], dram["c_pick6"].rearrange("k (a c) -> k a c", c=P)).then_inc(w_in, 16)

            @block.tensor
            def _(pe):
                pe.wait_ge(w_in, 80)
                with pe.Fori(0, NB) as b:
                    sT = selT[:, bass.ts(b, S)]
                    for n in range(N + 1):
                        e = n // HC6
                        if n < N:
                            if n % HC6 == 0:
                                pe.wait_ge(hm_ready, AHEAD + b * N + max(n - HC6, 0))
                                apart(pe, chip)
                                pe.matmul(bank[:, 4 + e % 2, :], pick[:, e, :], sT, start=True, stop=True).then_inc(spread, 1)
                            pe.wait_ge(rl_ready, AHEAD + b * N + max(n - 1, 0))
                            apart(pe, chip)
                            pe.matmul(bank[:, n % 2, :], w1[:, n, :], chip.xT[:, bass.ts(b, S)], start=True, stop=True)\
                                .then_inc(h_made, 1)
                        if n == 0:
                            pe.wait_ge(tail.yT_ready, AHEAD + b)
                            apart(pe, chip)
                            pe.matmul(bank[:, 7, :], b2[:, :], sT, start=True, stop=False)
                        if n >= 1:
                            pe.wait_ge(hm_ready, AHEAD + b * N + n)
                            apart(pe, chip)
                            pe.matmul(bank[:, 7, :], w2[:, n - 1, :], hm[:, (n - 1) % 2, :], start=False, stop=(n == N))\
                                .then_inc(used, 1)
                    tail.tensor(pe, chip, b)

            @block.scalar
            def _(act):
                with act.Fori(0, NB) as b:
                    for n in range(N):
                        act.wait_ge(h_made, AHEAD + b * N + n + 1)
                        act.wait_ge(hm_ready, AHEAD + b * N + max(n - 1, 0))
                        act.activation(rl[:, n % 2, :], bank[:, n % 2, :], ACT.Relu, bias=b1[:, n:n + 1]).then_inc(rl_ready, 1)
                    act.wait_ge(used, AHEAD + b * N + N)
                    tail.scalar(act, chip, b)

            @block.vector
            def _(dve):
                with dve.Fori(0, NB) as b:
                    for n in range(N):
                        e = n // HC6
                        dve.wait_ge(rl_ready, AHEAD + b * N + n + 1)
                        dve.wait_ge(used, AHEAD + b * N + max(n - 1, 0))
                        dve.wait_ge(spread, AHEAD + b * K6 + e + 1)
                        dve.tensor_tensor(hm[:, n % 2, :], rl[:, n % 2, :], bank[:, 4 + e % 2, :], ALU.mult).then_inc(hm_ready, 1)
                    tail.vector(dve, chip, b)


class Tail:

    def __init__(self, m):
        self.yT = m.sb("yT", [P, S])
        self.yT_ready = m.sem("yT_ready")
        self.y_turned = m.sem("y_turned")
        self.y_added = m.sem("y_added")

    def scalar(self, act, chip, b, bias=None):
        act.wait_ge(self.y_turned, AHEAD + b)
        if bias is None:
            act.activation(self.yT[:, :], chip.bank[:, 7, :], ACT.Copy).then_inc(self.yT_ready, 1)
        else:
            act.activation(self.yT[:, :], chip.bank[:, 7, :], ACT.Identity, bias=bias).then_inc(self.yT_ready, 1)

    def tensor(self, pe, chip, b):
        pe.wait_ge(self.yT_ready, AHEAD + b + 1)
        pe.wait_ge(self.y_added, AHEAD + b)
        apart(pe, chip)
        for t in range(TT):
            ins = pe.transpose(chip.bank[:, 6, t * P:(t + 1) * P], self.yT[:, t * P:(t + 1) * P], chip.ident[:, :])
        ins.then_inc(self.y_turned, 1)

    def vector(self, dve, chip, b):
        dve.wait_ge(self.y_turned, AHEAD + b + 1)
        xb = chip.x[:, bass.ts(b, TT), :]
        dve.tensor_tensor(xb, xb, chip.bank[:, 6, :].rearrange("p (t d) -> p t d", d=D), ALU.add).then_inc(self.y_added, 1)


NE8 = 16
G8 = 4
EG = NE8 // G8
NP8 = NE8 // 2


def grouped_experts(chip):
    nc, dram, bank, ident = chip.nc, chip.dram, chip.bank, chip.ident
    norm_stage(chip, "gn")
    with ExitStack() as outer:
        mo = Scope(chip, "g", outer)
        combT = mo.sb("combT", [NE8, NB * S])
        with ExitStack() as ctx:
            m = Scope(chip, "gr", ctx)
            gw = m.sb("gw", [P, NE8])
            gb = m.sb("gb", [P, NE8])
            rev = m.sb("rev", [P, D])
            SH = [P, NT, NE8]
            lg = m.sb("lg", SH)
            pr = m.sb("pr", SH)
            tmp = m.sb("tmp", SH)
            oh = m.sb("oh", SH)
            oh2 = m.sb("oh2", SH)
            duo = m.sb("duo", [P, NT * G8, 6])
            gs = m.sb("gs", [P, NT, G8])
            gt = m.sb("gt", [P, NT, G8])
            g1 = m.sb("g1", [P, NT, G8])
            g2 = m.sb("g2", [P, NT, G8])
            comb = m.sb("comb", SH)
            red = m.sb("red", [P, 4, NT])
            w_in = m.dma_sem("w_in")
            made = m.sem("made")
            dve_step = m.sem("dve_step")
            shifted = m.sem("shifted")
            e_ready = m.sem("e_ready")
            comb_ready = m.sem("comb_ready")
            turned = m.sem("turned")
            kept = m.sem("kept")
            block = ctx.enter_context(nc.Block())

            @block.sync
            def _(sp):
                m.start(sp)
                sp.dma_start(gw[:, :], dram["w_g_g"]).then_inc(w_in, 16)
                sp.dma_start(gb[:, :], dram["w_g_gb"].partition_broadcast(P)).then_inc(w_in, 16)
                sp.dma_start(rev[:, :], dram["c_rev"]).then_inc(w_in, 16)

            @block.tensor
            def _(pe):
                pe.wait_ge(w_in, 48)
                for n in range(NT):
                    ins = pe.matmul(bank[:, 0, n * NE8:(n + 1) * NE8], chip.xT[:, n * P:(n + 1) * P], gw[:, :],
                                    start=True, stop=True)
                ins.then_inc(made, 1)
                pe.wait_ge(comb_ready, AHEAD + 1)
                for b in range(NB):
                    if b >= 2:
                        pe.wait_ge(kept, AHEAD + b - 1)
                    for t in range(TT):
                        ins = pe.transpose(bank[0:NE8, 3 + b % 2, t * P:(t + 1) * P], comb[:, b * TT + t, :], ident[:, :])
                    ins.then_inc(turned, 1)

            @block.scalar
            def _(act):
                act.wait_ge(shifted, AHEAD + 1)
                act.activation(pr[:, :, :], lg[:, :, :], ACT.Exp).then_inc(e_ready, 1)
                for b in range(NB):
                    act.wait_ge(turned, AHEAD + b + 1)
                    act.activation(combT[:, b * S:(b + 1) * S], bank[0:NE8, 3 + b % 2, :], ACT.Copy).then_inc(kept, 1)

            @block.vector
            def _(dve):
                dve.wait_ge(w_in, 48)
                link = linker(dve, dve_step, 0, 33)

                def along(v, n=NE8):
                    return v.rearrange("p (t a) -> p t a", a=1).to_broadcast([P, NT, n])

                dve.wait_ge(made, AHEAD + 1)
                link(dve.tensor_reduce(red[:, 0, :], bank[:, 0, :].rearrange("p (t e) -> p t e", e=NE8), AX.X, ALU.max))
                dve.tensor_tensor(lg[:, :, :], bank[:, 0, :].rearrange("p (t e) -> p t e", e=NE8), along(red[:, 0, :]),
                                  ALU.subtract).then_inc(shifted, 1)
                dve.wait_ge(e_ready, AHEAD + 1)
                link(dve.tensor_reduce(red[:, 1, :], pr[:, :, :], AX.X, ALU.add))
                link(dve.reciprocal(red[:, 1, :], red[:, 1, :]))
                link(dve.tensor_tensor(pr[:, :, :], pr[:, :, :], along(red[:, 1, :]), ALU.mult))
                link(dve.tensor_tensor(lg[:, :, :], pr[:, :, :],
                                       gb[:, :].rearrange("p (a e) -> p a e", a=1).to_broadcast(SH), ALU.add))
                four = lg[:, :, :].rearrange("p t (g e) -> p (t g) e", e=EG)
                dve.tensor_tensor(duo[:, :, 0:3], four[:, :, 0:3], four[:, :, 1:4], ALU.add)
                dve.tensor_tensor(duo[:, :, 3:5], four[:, :, 0:2], four[:, :, 2:4], ALU.add)
                link(dve.tensor_tensor(duo[:, :, 5:6], four[:, :, 0:1], four[:, :, 3:4], ALU.add))
                link(dve.tensor_reduce(gs[:, :, :].rearrange("p t g -> p (t g)"), duo[:, :, :], AX.X, ALU.max))
                GS = [P, NT, G8]
                first_of_top(dve, link, gs[:, :, :], red[:, 0, :], rev[:, 0:G8], gt[:, :, :], red[:, 1, :], g1[:, :, :], GS)
                link(dve.scalar_tensor_tensor(gs[:, :, :], g1[:, :, :], NEG, gs[:, :, :], ALU.mult, ALU.add))
                first_of_top(dve, link, gs[:, :, :], red[:, 0, :], rev[:, 0:G8], gt[:, :, :], red[:, 1, :], g2[:, :, :], GS)
                link(dve.tensor_tensor(g1[:, :, :], g1[:, :, :], g2[:, :, :], ALU.add))
                link(dve.tensor_scalar(gt[:, :, :], g1[:, :, :], -1.0, -NEG, ALU.add, ALU.mult))

                def over_experts(v):
                    return v.rearrange("p t (g a) -> p (t g) a", a=1).to_broadcast([P, NT * G8, EG])

                link(dve.tensor_tensor(four, four, over_experts(gt[:, :, :]), ALU.add))
                first_of_top(dve, link, lg[:, :, :], red[:, 0, :], rev[:, 0:NE8], tmp[:, :, :], red[:, 1, :], oh[:, :, :], SH)
                link(dve.scalar_tensor_tensor(lg[:, :, :], oh[:, :, :], 2 * NEG, lg[:, :, :], ALU.mult, ALU.add))
                first_of_top(dve, link, lg[:, :, :], red[:, 0, :], rev[:, 0:NE8], tmp[:, :, :], red[:, 1, :], oh2[:, :, :], SH)
                link(dve.tensor_tensor(oh[:, :, :], oh[:, :, :], oh2[:, :, :], ALU.add))
                dve.tensor_tensor(comb[:, :, :], oh[:, :, :], pr[:, :, :], ALU.mult).then_inc(comb_ready, 1)
                link.check()

        with ExitStack() as ctx:
            m = Scope(chip, "gx", ctx)
            N = NP8 + 1
            w1 = m.sb("w1", [P, N, P])
            w3 = m.sb("w3", [P, N, P])
            w2 = m.sb("w2", [P, N, D])
            cols = m.sb("cols", [P, 2 * N + 1])
            b2 = m.sb("b2", [NE8, D])
            pick = m.sb("pick", [NE8, NP8, P])
            si = m.sb("si", [P, 2, S])
            hm = m.sb("hm", [P, 2, S])
            w_in = m.dma_sem("w_in")
            h_made = m.sem("h_made")
            si_ready = m.sem("si_ready")
            dve_step = m.sem("dve_step")
            hm_ready = m.sem("hm_ready")
            used = m.sem("used")
            tail = Tail(m)
            block = ctx.enter_context(nc.Block())

            @block.sync
            def _(sp):
                m.start(sp)
                sp.dma_start(w1[:, :, :], dram["w_g_1"].rearrange("p (a c) -> p a c", c=P)).then_inc(w_in, 16)
                sp.dma_start(w3[:, :, :], dram["w_g_3"].rearrange("p (a c) -> p a c", c=P)).then_inc(w_in, 16)
                sp.dma_start(w2[:, :, :], dram["w_g_2"].rearrange("(a p) d -> p a d", p=P)).then_inc(w_in, 16)
                sp.dma_start(cols[:, :], dram["w_g_cols"]).then_inc(w_in, 16)
                sp.dma_start(b2[:, :], dram["w_g_b2"]).then_inc(w_in, 16)
                sp.dma_start(pick[:, :, :], dram["c_pick8"].rearrange("k (a c) -> k a c", c=P)).then_inc(w_in, 16)

            @block.tensor
            def _(pe):
                pe.wait_ge(w_in, 96)
                with pe.Fori(0, NB) as b:
                    cT = combT[:, bass.ts(b, S)]
                    xb = chip.xT[:, bass.ts(b, S)]
                    for n in range(N + 1):
                        if n < N:
                            o = 3 * (n % 2)
                            pe.wait_ge(hm_ready, AHEAD + b * N + max(n - 1, 0))
                            apart(pe, chip)
                            ins = pe.matmul(bank[:, o, :], w1[:, n, :], xb, start=True, stop=True)
                            ins = pe.matmul(bank[:, o + 1, :], w3[:, n, :], xb, start=True, stop=True)
                            if n < NP8:
                                ins = pe.matmul(bank[:, o + 2, :], pick[:, n, :], cT, start=True, stop=True)
                            ins.then_inc(h_made, 1)
                        if n == 0:
                            pe.wait_ge(tail.yT_ready, AHEAD + b)
                            apart(pe, chip)
                            pe.matmul(bank[:, 7, :], b2[:, :], cT, start=True, stop=False)
                        if n >= 1:
                            pe.wait_ge(hm_ready, AHEAD + b * N + n)
                            apart(pe, chip)
                            pe.matmul(bank[:, 7, :], w2[:, n - 1, :], hm[:, (n - 1) % 2, :], start=False, stop=(n == N))\
                                .then_inc(used, 1)
                    tail.tensor(pe, chip, b)

            @block.scalar
            def _(act):
                with act.Fori(0, NB) as b:
                    for n in range(N):
                        act.wait_ge(h_made, AHEAD + b * N + n + 1)
                        act.wait_ge(hm_ready, AHEAD + b * N + max(n - 1, 0))
                        act.activation(si[:, n % 2, :], bank[:, 3 * (n % 2), :], ACT.Silu, bias=cols[:, n:n + 1]).then_inc(si_ready, 1)
                    act.wait_ge(used, AHEAD + b * N + N)
                    tail.scalar(act, chip, b, bias=cols[:, 2 * N:2 * N + 1])

            @block.vector
            def _(dve):
                with dve.Fori(0, NB) as b:
                    for n in range(N):
                        o = 3 * (n % 2)
                        dve.wait_ge(si_ready, AHEAD + b * N + n + 1)
                        dve.wait_ge(used, AHEAD + b * N + max(n - 1, 0))
                        ins = dve.scalar_tensor_tensor(hm[:, n % 2, :], bank[:, o + 1, :], cols[:, N + n:N + n + 1],
                                                       si[:, n % 2, :], ALU.add, ALU.mult)
                        if n < NP8:
                            ins.then_inc(dve_step, 1)
                            dve.wait_ge(dve_step, AHEAD + b * NP8 + n + 1)
                            ins = dve.tensor_tensor(hm[:, n % 2, :], hm[:, n % 2, :], bank[:, o + 2, :], ALU.mult)
                        ins.then_inc(hm_ready, 1)
                    tail.vector(dve, chip, b)


def program(nc, dram):
    with ExitStack() as ctx:
        chip = Chip(nc, dram, ctx)
        load_x(chip)
        small_head_attention(chip, "m0", dram["w_m0_qk"], dram["w_m0_v"], dram["w_m0_o"], dram["c_alibi"],
                           rope=dram["c_rope"], ob=dram["L0_attn_out_b"])
        local_layers(chip)
        batch_softmax_attention(chip)
        argmax_experts(chip)
        state_space(chip)
        capacity_experts(chip)
        small_head_attention(chip, "m3", dram["w_m3_qk"], dram["w_m3_v"], dram["w_m3_o"], None)
        grouped_experts(chip)
        store_x(chip)


def shape_constants():
    f = np.float32
    c = {}
    c["c_ident"] = np.eye(P, dtype=f)
    p = np.arange(P, dtype=f)[:, None]
    y = np.arange(S, dtype=f)[None, :]
    dist = p + (S - P) - y
    slopes = np.array([2.0 ** (-8.0 * (h + 1) / NH) for h in range(NH)], f)
    al = np.where(dist[None] < 0, f(NEG), -slopes[:, None, None] * dist[None] / f(ISQ)).astype(f)
    c["c_alibi"] = np.ascontiguousarray(al.reshape(G, HPG, P, S).transpose(0, 2, 1, 3)).reshape(G, P, HPG * S)
    half = D // 2
    freqs = (1.0 / f(10000.0) ** (np.arange(half, dtype=f) / f(half))).astype(f)
    ang = (np.arange(S, dtype=f)[None, :] * freqs[:, None]).astype(f)
    cos = np.concatenate([np.cos(ang), np.cos(ang)]).astype(f)
    sin = np.concatenate([-np.sin(ang), np.sin(ang)]).astype(f)
    rope = np.zeros((G, P, 2, S), f)
    for g in range(G):
        for j in range(HPG):
            for a, tab in enumerate((cos, sin)):
                rope[g, 32 * j:32 * j + HD, a] = tab[(g * HPG + j) * HD:(g * HPG + j + 1) * HD]
    c["c_rope"] = rope.reshape(G, P, 2 * S)
    c["c_log1p_dist"] = np.log1p(np.maximum(dist, 0)).astype(f)
    c["c_causal"] = np.where(dist < 0, f(NEG), f(0)).astype(f)
    ch = np.arange(0, LD, 2, dtype=f)
    inv_freq = (1.0 / f(10000.0) ** (ch / f(LD))).astype(f)
    t = np.arange(S, dtype=f)
    fr = (t[:, None] * inv_freq[None, :]).astype(f)
    bs = ((ch + f(0.4 * LD)) / f(1.4 * LD)).astype(f)
    power = ((t - S // 2) / f(WIN // 2)).astype(f)
    sc = (bs[None, :] ** power[:, None]).astype(f)
    two = lambda a: np.concatenate([a, a], 1)
    sgn = np.concatenate([-np.ones(LD // 2, f), np.ones(LD // 2, f)])[None, :]
    co, si, sc = two(np.cos(fr)), two(np.sin(fr)) * sgn, two(sc)
    inv = (f(1) / sc).astype(f)
    c["c_lrot"] = np.concatenate([np.concatenate([a.T, a.T]) for a in (co * sc, si * sc, co * inv, si * inv)], 1).astype(f)
    i_, y_ = np.arange(P)[:, None], np.arange(NK)[None, :]
    back = i_ - (y_ - WIN)
    ok = (back >= 0) & (back <= WIN)
    c["c_lmask"] = np.concatenate([np.where(ok & (y_ >= WIN), 0, NEG), np.where(ok, 0, NEG)], 1).astype(f)
    c["c_pair"] = np.repeat(np.eye(2, dtype=f), LD, 0)
    c["c_rev"] = np.repeat((D - np.arange(D, dtype=f))[None, :], P, 0)
    k_, q_ = np.arange(P)[:, None], np.arange(P)[None, :]
    c["c_upto"] = (k_ <= q_).astype(f)
    c["c_pick6"] = np.repeat(np.eye(K6, dtype=f), P, 1)
    c["c_pick8"] = np.repeat(np.eye(NE8, dtype=f), P // 2, 1)
    c["c_pick5"] = np.repeat(np.eye(SH5, dtype=f), P, 1)
    return c


def padded_heads(w):
    out = np.zeros((G, D, P), w.dtype)
    for g in range(G):
        for j in range(HPG):
            h = g * HPG + j
            out[g, :, 32 * j:32 * j + HD] = w[:, h * HD:(h + 1) * HD]
    return out


def lay_out(inp):
    a = {}
    a["x"] = inp["L0_attn_x"].reshape(NB * S, D)
    half = np.concatenate([np.arange(D // 2, D), np.arange(0, D // 2)])
    wq, wk = inp["L0_attn_wq"].T, inp["L0_attn_wk"].T
    a["w_m0_qk"] = np.concatenate([padded_heads(wq), padded_heads(wq[:, half]),
                                   padded_heads(wk), padded_heads(wk[:, half])], axis=2)
    a["w_m0_v"] = inp["L0_attn_wv"].T
    a["w_m0_o"] = inp["L0_attn_out_w"].T
    a["L0_attn_out_b"] = inp["L0_attn_out_b"]
    W = inp["L0_ffn_Wqkv"]
    inner = LH * LD
    sw = np.concatenate([np.arange(LD // 2, LD), np.arange(0, LD // 2)])
    swap = (np.arange(LH)[:, None] * LD + sw[None, :]).reshape(-1)
    q, k, v = W[:, :, :inner], W[:, :, inner:2 * inner], W[:, :, 2 * inner:]
    grp = lambda w: w.reshape(DEPTH, D, NG, P)
    a["w_l_qk"] = np.stack([grp(q), grp(q[:, :, swap]), grp(k), grp(k[:, :, swap])], 3).reshape(DEPTH, D, NG * 4 * P)
    a["w_l_v"] = v
    a["w_l_o"] = inp["L0_ffn_Wo"]
    pad = HC * P - HID
    halves = lambda w: np.concatenate([np.pad(w[..., :HID], [(0, 0)] * (w.ndim - 1) + [(0, pad)]),
                                       np.pad(w[..., HID:], [(0, 0)] * (w.ndim - 1) + [(0, pad)])], -1)
    a["w_l_1"] = halves(inp["L0_ffn_W1"])
    a["w_l_2"] = np.pad(inp["L0_ffn_W2"], ((0, 0), (0, pad), (0, 0)))
    qs, ks = inp["L0_ffn_q_scale"], inp["L0_ffn_k_scale"]
    col = lambda w: w.reshape(DEPTH, -1, P).transpose(0, 2, 1)
    dup = lambda w: np.concatenate([w, w], 1)
    a["w_l_cols"] = np.concatenate([col(dup(qs)), col(dup(qs[:, sw])), col(dup(ks)), col(dup(ks[:, sw])),
                                    col(inp["L0_ffn_ln_g"]), col(inp["L0_ffn_ln_b"]), col(inp["L0_ffn_b2"]),
                                    col(inp["L0_ffn_b2"]), col(halves(inp["L0_ffn_b1"]))], 2)
    a["w_b_v"] = inp["L1_attn_Wv"].T
    a["w_b_qk"] = np.concatenate([inp["L1_attn_Wq"].T, inp["L1_attn_Wk"].T], 1)
    a["w_e_g"] = inp["L1_ffn_Wg"]
    a["w_e_e"] = inp["L1_ffn_We"].transpose(1, 0, 2).reshape(D, -1)
    a["w_e_be"] = inp["L1_ffn_be"].reshape(1, -1)
    a["w_e_bg"] = inp["L1_ffn_bg"]
    wa = inp["L3_attn_w_attn"]
    a["w_m3_qk"] = np.concatenate([padded_heads(wa[:, :D]), padded_heads(wa[:, D:2 * D])], axis=2)
    a["w_m3_v"] = wa[:, 2 * D:]
    a["w_m3_o"] = inp["L3_attn_w_proj"]
    a["L3_attn_decay_raw"] = inp["L3_attn_decay_raw"]
    w1 = np.concatenate([inp["L2_ffn_w1"], inp["L2_ffn_ow1"][None]])
    w2 = np.concatenate([inp["L2_ffn_w2"], inp["L2_ffn_ow2"][None]])
    a["w_c_1"] = w1.transpose(1, 0, 2).reshape(D, K6 * H6)
    a["w_c_2"] = w2.reshape(K6 * H6, D)
    a["w_c_b1"] = np.concatenate([inp["L2_ffn_b1"], inp["L2_ffn_ob1"][None]]).reshape(K6 * HC6, P).T
    a["w_c_b2"] = np.concatenate([inp["L2_ffn_b2"], inp["L2_ffn_ob2"][None]])
    a["w_c_r"] = inp["L2_ffn_router_w"]
    a["w_c_rb"] = inp["L2_ffn_router_b"]
    pairs = lambda w, s: np.concatenate([w.transpose(1, 0, 2).reshape(D, NE8 * (P // 2)), s], 1)
    a["w_g_1"] = pairs(inp["L3_ffn_We1"], inp["L3_ffn_ws1"])
    a["w_g_3"] = pairs(inp["L3_ffn_We3"], inp["L3_ffn_ws3"])
    a["w_g_2"] = np.concatenate([inp["L3_ffn_We2"].reshape(-1, D), inp["L3_ffn_ws2"]])
    rows = lambda e, s: np.concatenate([e.reshape(-1), s]).reshape(-1, P).T
    a["w_g_cols"] = np.concatenate([rows(inp["L3_ffn_be1"], inp["L3_ffn_bs1"]), rows(inp["L3_ffn_be3"], inp["L3_ffn_bs3"]),
                                    inp["L3_ffn_bs2"][:, None]], 1)
    a["w_g_b2"] = inp["L3_ffn_be2"]
    a["w_g_g"] = inp["L3_ffn_gate_w"].T
    a["w_g_gb"] = inp["L3_ffn_gate_b"]
    wi = inp["L2_attn_in_proj_w"].T
    a["w_s_z"] = wi[:, :DI]
    a["w_s_x"] = wi[:, DI:DI + XC * P]
    a["w_s_dt"] = wi[:, DI + XC * P:]
    a["w_s_o"] = inp["L2_attn_out_proj_w"].T
    a["w_s_taps"] = np.concatenate([inp["L2_attn_conv_w"], inp["L2_attn_conv_b"][:, None]], 1)
    a["w_s_rows"] = np.concatenate([inp["L2_attn_" + n] for n in ("A_log", "dt_bias", "D_skip", "norm_w", "ln_w", "ln_b")])
    return a


def kernel(**inputs):
    import concourse.bacc as _bacc
    from concourse.bass_utils import run_bass_kernel_spmd as _run

    nc = _bacc.Bacc("TRN2", target_bir_lowering=False, num_devices=1)
    arrays, dram = {}, {}
    inputs = {k: np.asarray(v) for k, v in inputs.items()}
    for name, a in {**lay_out(inputs), **shape_constants()}.items():
        a = np.ascontiguousarray(a)
        arrays[f"in_{name}"] = a
        dram[name] = nc.dram_tensor(f"in_{name}", a.shape, mybir.dt.from_np(a.dtype), kind="ExternalInput").ap()
    dram["out"] = nc.dram_tensor("out_x", (NB * S, D), F32, kind="ExternalOutput").ap()
    program(nc, dram)
    r = _run(nc, [arrays], core_ids=[0])
    return r.results[0]["out_x"].reshape(NB, S, D)
```

```python
from contextlib import ExitStack

import numpy as np
import concourse.bass as bass
from concourse import mybir

P = 128
D = 128
NB = 8
S = 512
TT = S // P
NT = NB * TT
EPS = 1e-5
F32 = mybir.dt.float32
ALU = mybir.AluOpType
ACT = mybir.ActivationFunctionType
AX = mybir.AxisListType
AHEAD = 1
NEG = -1.0e30


def linker(eng, sem, start, total):
    count = [0]

    def link(ins):
        count[0] += 1
        ins.then_inc(sem, 1)
        eng.wait_ge(sem, AHEAD + start + count[0])

    def check():
        assert count[0] == total, (count[0], total)
    link.check = check
    return link


class Chip:

    def __init__(self, nc, dram, ctx):
        self.nc, self.dram = nc, dram
        self.x = ctx.enter_context(nc.sbuf_tensor("x_resid", [P, NT, D], F32))
        self.xT = ctx.enter_context(nc.sbuf_tensor("xT_all", [P, NB * S], F32))
        self.ident = ctx.enter_context(nc.sbuf_tensor("ident", [P, P], F32))
        self.ones = ctx.enter_context(nc.sbuf_tensor("ones", [P, P], F32))
        self.passed = ctx.enter_context(nc.semaphore("passed"))
        self.mhalf = ctx.enter_context(nc.sbuf_tensor("minus_half", [P, P], F32))
        self.bank = ctx.enter_context(nc.psum_tensor("bank", [P, 8, 512], F32))


def apart(eng, chip):
    eng.sem_inc(chip.passed, 1)


class Scope:

    def __init__(self, chip, tag, ctx):
        self.nc, self.tag, self.ctx = chip.nc, tag, ctx
        self.counted, self.sems = [], []
        ctx.callback(self.close)

    def close(self):
        if self.sems:
            self.nc.clear_and_free_semaphores(self.sems)
            self.nc.all_engine_barrier()

    def sb(self, name, shape, dt=F32):
        return self.ctx.enter_context(self.nc.sbuf_tensor(f"{self.tag}_{name}", shape, dt))

    def sem(self, name):
        self.counted.append(self.dma_sem(name))
        return self.counted[-1]

    def start(self, sp):
        for sem in self.counted:
            sp.sem_inc(sem, 1)

    def dma_sem(self, name):
        self.sems.append(self.nc.alloc_semaphore(f"{self.tag}_{name}"))
        return self.sems[-1]


def load_x(chip):
    nc = chip.nc
    with ExitStack() as ctx:
        m = Scope(chip, "load", ctx)
        loaded = m.dma_sem("loaded")
        block = ctx.enter_context(nc.Block())

        @block.sync
        def _(sp):
            sp.dma_start(chip.x[:, :, :], chip.dram["x"].rearrange("(n p) d -> p n d", p=P)).then_inc(loaded, 16)
            sp.dma_start(chip.ident[:, :], chip.dram["c_ident"]).then_inc(loaded, 16)
            sp.wait_ge(loaded, 32)

        @block.gpsimd
        def _(pool):
            pool.memset(chip.ones[:, :], 1.0)
            pool.memset(chip.mhalf[:, :], -0.5)


def store_x(chip):
    nc = chip.nc
    with ExitStack() as ctx:
        m = Scope(chip, "store", ctx)
        stored = m.dma_sem("stored")
        block = ctx.enter_context(nc.Block())

        @block.sync
        def _(sp):
            sp.dma_start(chip.dram["out"].rearrange("(n p) d -> p n d", p=P), chip.x[:, :, :]).then_inc(stored, 16)
            sp.wait_ge(stored, 16)


def norm_stage(chip, tag, wv=None, v_all=None, keep=None):
    nc = chip.nc
    with ExitStack() as ctx:
        m = Scope(chip, tag, ctx)
        stats = m.sb("stats", [P, 2, TT, 6])
        mv = m.sb("mean_var", [P, 2, TT, 2])
        rstd = m.sb("rstd", [P, 2, TT])
        xn = m.sb("xn", [P, 2, TT, D])
        xt = m.sb("xt", [P, 2, S])
        wv_sb = m.sb("wv", [P, D])
        w_loaded = m.dma_sem("w_loaded")
        stats_made = m.sem("stats_made")
        mv_ready = m.sem("mv_ready")
        var_eps = m.sem("var_eps")
        rstd_ready = m.sem("rstd_ready")
        xn_ready = m.sem("xn_ready")
        turned = m.sem("turned")
        xt_ready = m.sem("xt_ready")
        xt_kept = m.sem("xt_kept")
        xn_kept = m.sem("xn_kept")
        v_made = m.sem("v_made")
        v_kept = m.sem("v_kept")
        block = ctx.enter_context(nc.Block())

        def batches(eng, step):
            step(0, 0)
            step(1, 1)
            with eng.Fori(1, NB // 2) as k:
                for half in range(2):
                    step(k * 2 + half, half)

        @block.sync
        def _(sp):
            m.start(sp)
            if wv is not None:
                sp.dma_start(wv_sb[:, :], wv).then_inc(w_loaded, 16)

        @block.vector
        def _(dve):
            def statistics(b, half, first=False):
                if not first:
                    dve.wait_ge(xn_ready, AHEAD + b - 1)
                apart(dve, chip)
                for t in range(TT):
                    ins = dve.bn_stats(stats[:, half, t, :], chip.x[:, b * TT + t, :])
                ins.then_inc(stats_made, 1)
                dve.wait_ge(stats_made, AHEAD + b + 1)
                apart(dve, chip)
                for t in range(TT):
                    ins = dve.bn_aggr(mv[:, half, t, :], stats[:, half, t, :])
                ins.then_inc(mv_ready, 1)

            def step(b, half):
                dve.wait_ge(rstd_ready, AHEAD + b + 1)
                dve.wait_ge(turned, AHEAD + (b - 1 if half == 1 else b))
                if keep is not None:
                    dve.wait_ge(xn_kept, AHEAD + (b - 1 if half == 1 else b))
                apart(dve, chip)
                for t in range(TT):
                    ins = dve.tensor_scalar(xn[:, half, t, :], chip.x[:, b * TT + t, :], mv[:, half, t, 0:1],
                                            rstd[:, half, t:t + 1], ALU.subtract, ALU.mult)
                ins.then_inc(xn_ready, 1)

            statistics(0, 0, first=True)
            with dve.Fori(0, NB // 2 - 1) as k:
                for half in range(2):
                    statistics(k * 2 + half + 1, 1 - half)
                    step(k * 2 + half, half)
            statistics(NB - 1, 1)
            step(NB - 2, 0)
            step(NB - 1, 1)

        @block.tensor
        def _(pe):
            if wv is not None:
                pe.wait_ge(w_loaded, 16)

            def product(b, half):
                pe.wait_ge(xt_ready, AHEAD + b + 1)
                pe.wait_ge(v_kept, AHEAD + (b - 1 if half == 1 else b))
                for t in range(TT):
                    ins = pe.matmul(chip.bank[:, 2 + half, t * P:(t + 1) * P], xt[:, half, t * P:(t + 1) * P], wv_sb[:, :],
                                    start=True, stop=True)
                ins.then_inc(v_made, 1)

            def step(b, half):
                pe.wait_ge(xn_ready, AHEAD + b + 1)
                pe.wait_ge(xt_ready, AHEAD + (b - 1 if half == 1 else b))
                for t in range(TT):
                    ins = pe.transpose(chip.bank[:, half, t * P:(t + 1) * P], xn[:, half, t, :], chip.ident[:, :])
                ins.then_inc(turned, 1)
                if wv is not None:
                    product(b, half)

            batches(pe, step)

        @block.scalar
        def _(act):
            def step(b, half):
                act.wait_ge(turned, AHEAD + b + 1)
                if wv is None:
                    apart(act, chip)
                    act.activation(chip.xT[:, bass.ts(b, S)], chip.bank[:, half, :], ACT.Copy).then_inc(xt_ready, 1)
                    return
                act.wait_ge(xt_kept, AHEAD + (b - 1 if half == 1 else b))
                act.wait_ge(v_made, AHEAD + b)
                act.activation(xt[:, half, :], chip.bank[:, half, :], ACT.Copy).then_inc(xt_ready, 1)
                act.wait_ge(v_made, AHEAD + b + 1)
                apart(act, chip)
                act.activation(v_all[:, bass.ts(b, TT), :], chip.bank[:, 2 + half, :].rearrange("p (t d) -> p t d", d=D),
                               ACT.Copy).then_inc(v_kept, 1)

            batches(act, step)

        @block.gpsimd
        def _(pool):
            def scales(b, half):
                pool.wait_ge(mv_ready, AHEAD + b + 1)
                apart(pool, chip)
                pool.tensor_scalar(rstd[:, half, :], mv[:, half, :, 1], EPS, None, ALU.add).then_inc(var_eps, 1)
                pool.wait_ge(var_eps, AHEAD + b + 1)
                apart(pool, chip)
                pool.tensor_tensor(rstd[:, half, :], rstd[:, half, :], chip.mhalf[:, 0:TT], ALU.pow).then_inc(rstd_ready, 1)

            def step(b, half):
                if keep is not None:
                    pool.wait_ge(xn_ready, AHEAD + b + 1)
                    apart(pool, chip)
                    pool.tensor_copy(keep[:, bass.ts(b, TT), :], xn[:, half, :, :]).then_inc(xn_kept, 1)
                if wv is not None:
                    pool.wait_ge(xt_ready, AHEAD + b + 1)
                    apart(pool, chip)
                    pool.tensor_copy(chip.xT[:, bass.ts(b, S)], xt[:, half, :]).then_inc(xt_kept, 1)

            scales(0, 0)
            with pool.Fori(0, NB // 2 - 1) as k:
                for half in range(2):
                    scales(k * 2 + half + 1, 1 - half)
                    step(k * 2 + half, half)
            scales(NB - 1, 1)
            step(NB - 2, 0)
            step(NB - 1, 1)


NH = 16
HD = D // NH
G = 4
HPG = NH // G
ISQ = 1.0 / float(np.sqrt(np.float32(HD)))


def small_head_attention(chip, tag, wqk, wv, wo, bias_kind, rope=None, ob=None):
    nc, x = chip.nc, chip.x
    nproj = 4 if rope is not None else 2
    with ExitStack() as outer:
        mo = Scope(chip, tag, outer)
        v_all = mo.sb("v", [P, NT, D])
        o_all = mo.sb("o", [P, NT, D])
        norm_stage(chip, tag + "n", wv, v_all)
        with ExitStack() as ctx:
            m = Scope(chip, tag + "a", ctx)
            w = m.sb("w", [P, nproj, P])
            table = m.sb("table", [P, HPG, S])
            if rope is not None:
                rot = m.sb("rot", [P, 2, S])
                t1 = m.sb("t1", [P, 2, S])
                t2 = m.sb("t2", [P, 2, S])
            else:
                dist = m.sb("dist", [P, S])
                causal = m.sb("causal", [P, S])
                dec_in = m.sb("dec_in", [P, NH])
                dec = m.sb("dec", [P, NH])
                lnw = m.sb("lnw", [P, HPG, S])
                d_loaded = m.dma_sem("d_loaded")
                dec_step = m.sem("dec_step")
                lnw_ready = m.sem("lnw_ready")
            qk = m.sb("qk", [P, 2, 2, S])
            NS, NPT = 8, 4
            sc = m.sb("sc", [P, NS, S])
            pt = m.sb("pt", [P, NPT, S])
            nmx = m.sb("nmx", [P, 16])
            rs = m.sb("rs", [P, 2, 16])
            rr = m.sb("rr", [P, 16])
            v_st = m.sb("v_st", [P, 2, TT, 32 + 32 - HD])
            ot = m.sb("ot", [P, S])
            U = HPG * TT
            w_loaded = m.dma_sem("w_loaded")
            group_done = m.sem("group_done")
            table_ready = m.sem("table_ready")
            proj_made = m.sem("proj_made")
            rot_step = m.sem("rot_step")
            qk_ready = m.sem("qk_ready")
            s_made = m.sem("s_made")
            s_biased = m.sem("s_biased")
            p_ready = m.sem("p_ready")
            p_turned = m.sem("p_turned")
            pt_ready = m.sem("pt_ready")
            pv_made = m.sem("pv_made")
            v_zeroed = m.sem("v_zeroed")
            v_staged = m.sem("v_staged")
            ot_ready = m.sem("ot_ready")
            o_turned = m.sem("o_turned")
            rr_ready = m.sem("rr_ready")
            o_kept = m.sem("o_kept")
            block = ctx.enter_context(nc.Block())

            @block.sync
            def _(sp):
                m.start(sp)
                if rope is None:
                    sp.dma_start(dist[:, :], chip.dram["c_log1p_dist"]).then_inc(d_loaded, 16)
                    sp.dma_start(causal[:, :], chip.dram["c_causal"]).then_inc(d_loaded, 16)
                    sp.dma_start(dec_in[:, :], chip.dram["L3_attn_decay_raw"].partition_broadcast(P)).then_inc(d_loaded, 16)
                with sp.Fori(0, G) as g:
                    sp.wait_ge(group_done, AHEAD + g)
                    sp.dma_start(w[:, :, :], wqk[g].rearrange("p (a c) -> p a c", c=P)).then_inc(w_loaded, 16)
                    if rope is not None:
                        sp.dma_start(rot[:, :, :], rope[g].rearrange("p (a c) -> p a c", c=S)).then_inc(w_loaded, 16)
                        sp.dma_start(table[:, :, :], bias_kind[g].rearrange("p (a c) -> p a c", c=S)).then_inc(w_loaded, 16)

            NLOAD = 16 * (3 if rope is not None else 1)

            TURN, WEIGH = 3, 5
            TURN_BACK = 9
            PREP = (1, 6)
            NQK = 2 if rope is not None else 1
            bank_read = rot_step if rope is not None else qk_ready

            def passes(eng, steps):
                steps(-1, 1, False, False, 0)
                steps(0, 0, True, False, 1)
                with eng.Fori(0, NB // 2 - 1) as k:
                    steps(k * 2 + 1, 1, True, True, k * 2 + 2)
                    steps(k * 2 + 2, 0, True, True, k * 2 + 3)
                steps(NB - 1, 1, True, True, None)
                steps(NB, 0, False, True, None)

            def lagging(s, lag, par, runs, behind):
                if s >= lag:
                    return (s - lag, 0, par) if runs else None
                return (s - lag + U, 1, 1 - par) if behind else None

            @block.tensor
            def _(pe):
                with pe.Fori(0, G) as g:
                    pe.wait_ge(w_loaded, g * NLOAD + NLOAD)
                    apart(pe, chip)
                    pe.wait_ge(o_kept, AHEAD + g * NB)

                    def steps(b, par, runs, behind, n):
                        i = g * NB + b
                        r = None if n is None else g * NB + n

                        def scores(u):
                            j, t = u // TT, u % TT
                            if u == 0:
                                pe.wait_ge(qk_ready, AHEAD + i * NQK + NQK)
                            pe.wait_ge(s_biased, AHEAD + (i * U + u - 1 if u >= 2 else i * U))
                            pe.matmul(chip.bank[:, u % 2, 0:(t + 1) * P], qk[32 * j:32 * j + HD, par, 0, t * P:(t + 1) * P],
                                      qk[32 * j:32 * j + HD, par, 1, 0:(t + 1) * P], start=True, stop=True).then_inc(s_made, 1)

                        def turn(u, back, par):
                            t = u % TT
                            done = (i - back) * U + u
                            pe.wait_ge(p_ready, AHEAD + done + 1)
                            pe.wait_ge(pt_ready, AHEAD + (done - 1 if u else done))
                            for k in range(t + 1):
                                ins = pe.transpose(chip.bank[:, 4 + u % 2, k * P:(k + 1) * P],
                                                   sc[:, u % NS, k * P:(k + 1) * P], chip.ident[:, :])
                            ins.then_inc(p_turned, 1)

                        def weigh(u, back, par):
                            j, t = u // TT, u % TT
                            pe.wait_ge(pt_ready, AHEAD + (i - back) * U + u + 1)
                            if u == 0:
                                pe.wait_ge(o_kept, AHEAD + (i - 1 if behind else i))
                                pe.wait_ge(v_staged, AHEAD + i + 1)
                            for k in range(t + 1):
                                ins = pe.matmul(chip.bank[32 * j:32 * j + 32, 6 + par, t * P:(t + 1) * P],
                                                v_st[:, par, k, j * HD:j * HD + 32], pt[:, u % NPT, k * P:(k + 1) * P],
                                                start=(k == 0), stop=(k == t), skip_group_check=True)
                            ins.then_inc(pv_made, 1)

                        for s in range(U):
                            if runs:
                                scores(s)
                            unit = lagging(s, TURN, par, runs, behind)
                            if unit:
                                turn(*unit)
                            unit = lagging(s, WEIGH, par, runs, behind)
                            if unit:
                                weigh(*unit)
                            if s == TURN_BACK and behind:
                                pe.wait_ge(ot_ready, AHEAD + i)
                                for t in range(TT):
                                    ins = pe.transpose(chip.bank[:, 7 - par, t * P:(t + 1) * P],
                                                       ot[:, t * P:(t + 1) * P], chip.ident[:, :])
                                ins.then_inc(o_turned, 1)
                            if n is None:
                                continue
                            for a in range(nproj // 2):
                                if s == PREP[a]:
                                    pe.wait_ge(bank_read, AHEAD + r * (nproj // 2) + a)
                                    for c in range(2):
                                        ins = pe.matmul(chip.bank[:, 2 + c, :], w[:, 2 * a + c, :], chip.xT[:, bass.ts(n, S)],
                                                        start=True, stop=True)
                                    ins.then_inc(proj_made, 1)

                    passes(pe, steps)

            @block.vector
            def _(dve):
                if rope is None:
                    dve.wait_ge(d_loaded, 48)
                    dve.wait_ge(dec_step, AHEAD + 3)
                    dve.scalar_tensor_tensor(dec[:, :], dec_in[:, :], 0.0, dec[:, :], ALU.max, ALU.add).then_inc(dec_step, 1)
                with dve.Fori(0, G) as g:
                    if rope is None:
                        dve.wait_ge(lnw_ready, AHEAD + g + 1)
                        for j in range(HPG):
                            ins = dve.scalar_tensor_tensor(table[:, j, :], lnw[:, j, :], -1.0 / ISQ, causal[:, :],
                                                           ALU.mult, ALU.add)
                        ins.then_inc(table_ready, 1)
                        dve.wait_ge(table_ready, AHEAD + g + 1)
                    else:
                        dve.wait_ge(w_loaded, g * NLOAD + NLOAD)
                    apart(dve, chip)

                    def steps(b, par, runs, behind, n):
                        i = g * NB + b
                        r = None if n is None else g * NB + n
                        for s in range(U):
                            if runs:
                                nk = (s % TT + 1) * P
                                dve.wait_ge(s_made, AHEAD + i * U + s + 1)
                                dve.wait_ge(p_turned, AHEAD + (i * U + s - NS + 1 if s >= NS or behind else i * U))
                                apart(dve, chip)
                                dve.tensor_tensor_reduce(sc[:, s % NS, 0:nk], chip.bank[:, s % 2, 0:nk],
                                                         table[:, s // TT, S - nk:S], -ISQ, -NEG * 2, ALU.add, ALU.min,
                                                         nmx[:, s:s + 1]).then_inc(s_biased, 1)
                            if s == WEIGH + 1 and behind:
                                dve.wait_ge(p_ready, AHEAD + i * U)
                                dve.reciprocal(rr[:, :], rs[:, 1 - par, :]).then_inc(rr_ready, 1)
                                dve.wait_ge(pv_made, AHEAD + i * U)
                                dve.tensor_copy(ot[:, :], chip.bank[:, 7 - par, :]).then_inc(ot_ready, 1)
                            if s == TURN_BACK + 1 and behind:
                                dve.wait_ge(rr_ready, AHEAD + i)
                                dve.wait_ge(o_turned, AHEAD + i)
                                apart(dve, chip)
                                for t in range(TT):
                                    src = chip.bank[:, 7 - par, t * P:(t + 1) * P].rearrange("p (j d) -> p j d", j=HPG)[:, :, 0:HD]
                                    rep = rr[:, :].rearrange("p (j t) -> p j t", j=HPG)[:, :, t:t + 1].to_broadcast([P, HPG, HD])
                                    ins = dve.tensor_tensor(
                                        o_all[:, (b - 1) * TT + t, bass.ds(g * 32, 32)].rearrange("p (j d) -> p j d", d=HD),
                                        src, rep, ALU.mult)
                                ins.then_inc(o_kept, 1)
                            if n is None:
                                continue
                            if rope is None and s == PREP[0] + 1:
                                dve.wait_ge(proj_made, AHEAD + r + 1)
                                dve.tensor_copy(qk[:, 1 - par, :, :], chip.bank[:, 2:4, :]).then_inc(qk_ready, 1)
                            for a in range(2):
                                if rope is not None and s == PREP[a] + 1:
                                    dve.wait_ge(proj_made, AHEAD + r * 2 + a + 1)
                                    dve.wait_ge(qk_ready, AHEAD + r * 2)
                                    dve.tensor_tensor(t1[:, a, :], chip.bank[:, 2, :], rot[:, 0, :], ALU.mult)
                                    dve.tensor_tensor(t2[:, a, :], chip.bank[:, 3, :], rot[:, 1, :], ALU.mult)\
                                        .then_inc(rot_step, 1)

                    passes(dve, steps)

            @block.scalar
            def _(act):
                if rope is None:
                    act.wait_ge(d_loaded, 48)
                    act.activation(dec[:, :], dec_in[:, :], ACT.Abs).then_inc(dec_step, 1)
                    act.wait_ge(dec_step, AHEAD + 1)
                    act.activation(dec[:, :], dec[:, :], ACT.Exp, scale=-1.0).then_inc(dec_step, 1)
                    act.wait_ge(dec_step, AHEAD + 2)
                    act.activation(dec[:, :], dec[:, :], ACT.Ln, bias=chip.ones[:, 0:1]).then_inc(dec_step, 1)
                    act.wait_ge(dec_step, AHEAD + 4)
                with act.Fori(0, G) as g:
                    if rope is None:
                        act.wait_ge(table_ready, AHEAD + g)
                        for j in range(HPG):
                            act.activation(dec_in[:, j:j + 1], dec[:, bass.ds(g * HPG + j, 1)], ACT.Copy).then_inc(dec_step, 1)
                        act.wait_ge(dec_step, AHEAD + g * HPG + 4 + HPG)
                        for j in range(HPG):
                            ins = act.activation(lnw[:, j, :], dist[:, :], ACT.Ln, bias=chip.ones[:, 0:1], scale=dec_in[:, j:j + 1])
                        ins.then_inc(lnw_ready, 1)

                    def steps(b, par, runs, behind, n):
                        i = g * NB + b
                        for s in range(U):
                            if runs:
                                nk = (s % TT + 1) * P
                                act.wait_ge(s_biased, AHEAD + i * U + s + 1)
                                act.activation(sc[:, s % NS, 0:nk], sc[:, s % NS, 0:nk], ACT.Exp, bias=nmx[:, s:s + 1],
                                               scale=-1.0, accum_out=rs[:, par, s:s + 1]).then_inc(p_ready, 1)
                            unit = lagging(s, TURN, par, runs, behind)
                            if unit:
                                u, back, _ = unit
                                nk = (u % TT + 1) * P
                                done = (i - back) * U + u
                                act.wait_ge(p_turned, AHEAD + done + 1)
                                act.wait_ge(pv_made, AHEAD + (done - NPT + 1 if u >= NPT - 1 or back == 0 and behind else i * U))
                                act.activation(pt[:, u % NPT, 0:nk], chip.bank[:, 4 + u % 2, 0:nk], ACT.Copy).then_inc(pt_ready, 1)

                    passes(act, steps)

            @block.gpsimd
            def _(pool):
                pool.memset(v_st[:, :, :, :], 0.0).then_inc(v_zeroed, 1)
                pool.wait_ge(v_zeroed, AHEAD + 1)
                with pool.Fori(0, G) as g:
                    with pool.Fori(0, NB // 2) as k:
                        for half in range(2):
                            b = k * 2 + half
                            r = g * NB + b
                            if rope is not None:
                                for a in range(2):
                                    pool.wait_ge(rot_step, AHEAD + r * 2 + a + 1)
                                    pool.tensor_tensor(qk[:, half, a, :], t1[:, a, :], t2[:, a, :], ALU.add).then_inc(qk_ready, 1)
                            pool.wait_ge(s_made, AHEAD + r * U + 1)
                            apart(pool, chip)
                            pool.tensor_copy(v_st[:, half, :, 0:32], v_all[:, bass.ds(b * TT, TT), bass.ds(g * 32, 32)])\
                                .then_inc(v_staged, 1)
                    pool.wait_ge(o_kept, AHEAD + g * NB + NB)
                    pool.sem_inc(group_done, 1)

        out_projection(chip, tag + "o", o_all, wo, ob)


def out_projection(chip, tag, o_all, wo, ob):
    nc, x = chip.nc, chip.x
    with ExitStack() as ctx:
        m = Scope(chip, tag, ctx)
        cur = m.sb("cur", [P, TT, D])
        curT = m.sb("curT", [P, S])
        w = m.sb("w", [P, D])
        bias = m.sb("bias", [P, D])
        w_loaded = m.dma_sem("w_loaded")
        cur_ready = m.sem("cur_ready")
        turned = m.sem("turned")
        curT_ready = m.sem("curT_ready")
        made = m.sem("made")
        biased = m.sem("biased")
        added = m.sem("added")
        block = ctx.enter_context(nc.Block())

        @block.sync
        def _(sp):
            m.start(sp)
            sp.dma_start(w[:, :], wo).then_inc(w_loaded, 16)
            if ob is not None:
                sp.dma_start(bias[:, :], ob.partition_broadcast(P)).then_inc(w_loaded, 16)

        nload = 32 if ob is not None else 16

        @block.gpsimd
        def _(pool):
            with pool.Fori(0, NB) as b:
                pool.wait_ge(turned, AHEAD + b)
                pool.tensor_copy(cur[:, :, :], o_all[:, bass.ts(b, TT), :]).then_inc(cur_ready, 1)

        @block.tensor
        def _(pe):
            pe.wait_ge(w_loaded, nload)
            with pe.Fori(0, NB) as b:
                pe.wait_ge(cur_ready, AHEAD + b + 1)
                pe.wait_ge(curT_ready, AHEAD + b)
                for t in range(TT):
                    ins = pe.transpose(chip.bank[:, 0, t * P:(t + 1) * P], cur[:, t, :], chip.ident[:, :])
                ins.then_inc(turned, 1)
                pe.wait_ge(curT_ready, AHEAD + b + 1)
                pe.wait_ge(added, AHEAD + b)
                for t in range(TT):
                    ins = pe.matmul(chip.bank[:, 1, t * P:(t + 1) * P], curT[:, t * P:(t + 1) * P], w[:, :],
                                    start=True, stop=True)
                ins.then_inc(made, 1)

        @block.scalar
        def _(act):
            with act.Fori(0, NB) as b:
                act.wait_ge(turned, AHEAD + b + 1)
                act.wait_ge(made, AHEAD + b)
                act.activation(curT[:, :], chip.bank[:, 0, :], ACT.Copy).then_inc(curT_ready, 1)

        @block.vector
        def _(dve):
            dve.wait_ge(w_loaded, nload)
            with dve.Fori(0, NB) as b:
                xb = x[:, bass.ts(b, TT), :]
                if ob is not None:
                    dve.tensor_tensor(xb, xb, bias[:, :].rearrange("p (a d) -> p a d", a=1).to_broadcast([P, TT, D]), ALU.add)\
                        .then_inc(biased, 1)
                    dve.wait_ge(biased, AHEAD + b + 1)
                dve.wait_ge(made, AHEAD + b + 1)
                dve.tensor_tensor(xb, xb, chip.bank[:, 1, :].rearrange("p (t d) -> p t d", d=D), ALU.add).then_inc(added, 1)


DEPTH = 6
LH = 16
LD = 64
NG = LH * LD // P
WIN = 32
NK = P + WIN
HID = 341
HC = -(-HID // P)
QKS = 8.0
U2 = 2 * TT


def local_layers(chip):
    nc, dram, bank, yT, ident = chip.nc, chip.dram, chip.bank, chip.xT, chip.ident
    norm_stage(chip, "l0n")
    with ExitStack() as ctx:
        m = Scope(chip, "l", ctx)
        wqk = m.sb("wqk", [P, NG + 1, 4 * P])
        wv = m.sb("wv", [P, LH * LD])
        wo = m.sb("wo", [P, NG, D])
        w1 = m.sb("w1", [P, 2 * HC, P])
        w2 = m.sb("w2", [P, HC, D])
        cols = m.sb("cols", [P, 8 + 2 * HC])
        base = m.sb("base", [P, 4, S])
        rot = m.sb("rot", [P, 4, S])
        mask = m.sb("mask", [P, 2, NK])
        pair = m.sb("pair", [P, 2])
        avg = m.sb("avg", [P, P])
        xa = m.sb("xa", [P, S])
        xs = m.sb("xs", [P, S])
        wst = m.sb("wst", [P, 4, P])
        t1 = m.sb("t1", [P, 2, S])
        t2 = m.sb("t2", [P, 2, S])
        sq = m.sb("sq", [P, 2, S])
        ssk = m.sb("ssk", [P, TT, 2])
        ssq = m.sb("ssq", [P, TT, 2])
        rk = m.sb("rk", [P, TT, 2])
        rq = m.sb("rq", [P, TT, 2])
        rkb = m.sb("rkb", [P, TT, P])
        q_sb = m.sb("q", [P, 2, S])
        k_sb = m.sb("k", [P, 2, WIN + S])
        v_sb = m.sb("v", [P, 2, TT, P])
        nscale = m.sb("nscale", [P, 2, TT, 2])
        PAD = P - WIN
        pb = m.sb("pb", [P, U2, PAD + NK])
        NPT = 4
        pt = m.sb("pt", [P, NPT, NK])
        nm = m.sb("nm", [P, U2])
        rs = m.sb("rs", [P, U2])
        rr = m.sb("rr", [P, U2])
        ot = m.sb("ot", [P, NG, S])
        xc = m.sb("xc", [P, S])
        sqf = m.sb("sqf", [P, S])
        sv = m.sb("sv", [P, TT])
        rv = m.sb("rv", [P, TT])
        xg = m.sb("xg", [P, S])
        ge = m.sb("ge", [P, 2, S])
        hh = m.sb("hh", [P, 2, S])
        early = m.sb("early", [P, 2])

        tables_in = m.dma_sem("tables_in")
        w_in = m.dma_sem("w_in")
        layer_done = m.sem("layer_done")
        zeroed = m.sem("zeroed")
        padded = m.sem("padded")
        rot_ready = m.sem("rot_ready")
        xa_ready = m.sem("xa_ready")
        xs_ready = m.sem("xs_ready")
        wst_ready = m.sem("wst_ready")
        q_made = m.sem("q_made")
        k_made = m.sem("k_made")
        q_turned = m.sem("q_turned")
        k_turned = m.sem("k_turned")
        q_squared = m.sem("q_squared")
        k_squared = m.sem("k_squared")
        v_made = m.sem("v_made")
        v_kept = m.sem("v_kept")
        ssk_made = m.sem("ssk_made")
        ssk_kept = m.sem("ssk_kept")
        ssq_made = m.sem("ssq_made")
        ssq_kept = m.sem("ssq_kept")
        rk_ready = m.sem("rk_ready")
        rq_ready = m.sem("rq_ready")
        nscale_ready = m.sem("nscale_ready")
        rkb_ready = m.sem("rkb_ready")
        q_ready = m.sem("q_ready")
        k_added = m.sem("k_added")
        rk_spread = m.sem("rk_spread")
        k_ready = m.sem("k_ready")
        s_made = m.sem("s_made")
        s_masked = m.sem("s_masked")
        p_exp = m.sem("p_exp")
        rr_ready = m.sem("rr_ready")
        p_ready = m.sem("p_ready")
        p_turned = m.sem("p_turned")
        pt_ready = m.sem("pt_ready")
        pv_made = m.sem("pv_made")
        ot_kept = m.sem("ot_kept")
        wo_made = m.sem("wo_made")
        y_mid = m.sem("y_mid")
        mean_made = m.sem("mean_made")
        xc_ready = m.sem("xc_ready")
        sqf_ready = m.sem("sqf_ready")
        sv_made = m.sem("sv_made")
        sv_kept = m.sem("sv_kept")
        rv_ready = m.sem("rv_ready")
        rv_spread = m.sem("rv_spread")
        xcn_ready = m.sem("xcn_ready")
        xg_ready = m.sem("xg_ready")
        h_made = m.sem("h_made")
        ge_ready = m.sem("ge_ready")
        hh_ready = m.sem("hh_ready")
        w2_used = m.sem("w2_used")
        y_done = m.sem("y_done")
        block = ctx.enter_context(nc.Block())
        NW = 6 * 16

        @block.sync
        def _(sp):
            m.start(sp)
            sp.dma_start(base[:, :, :], dram["c_lrot"].rearrange("p (a c) -> p a c", c=S)).then_inc(tables_in, 16)
            sp.dma_start(mask[:, :, :], dram["c_lmask"].rearrange("p (a c) -> p a c", c=NK)).then_inc(tables_in, 16)
            sp.dma_start(pair[:, :], dram["c_pair"]).then_inc(tables_in, 16)
            with sp.Fori(0, DEPTH) as l:
                sp.wait_ge(layer_done, AHEAD + l)
                sp.dma_start(wqk[:, 0:NG, :], dram["w_l_qk"][l].rearrange("p (g c) -> p g c", c=4 * P)).then_inc(w_in, 16)
                sp.dma_start(wv[:, :], dram["w_l_v"][l]).then_inc(w_in, 16)
                sp.dma_start(wo[:, :, :], dram["w_l_o"][l].rearrange("(g p) d -> p g d", p=P)).then_inc(w_in, 16)
                sp.dma_start(w1[:, :, :], dram["w_l_1"][l].rearrange("p (a c) -> p a c", c=P)).then_inc(w_in, 16)
                sp.dma_start(w2[:, :, :], dram["w_l_2"][l].rearrange("(a p) d -> p a d", p=P)).then_inc(w_in, 16)
                sp.dma_start(cols[:, :], dram["w_l_cols"][l]).then_inc(w_in, 16)

        TURN, COPY, WEIGH, NORM = 3, 3, 5, 1
        KEEP = WEIGH - 1
        PREP_K, PREP_Q, PREP_SQ, PREP_RK, PREP_V = 0, 2, 4, 6, 7
        TB = (6, 2)

        def groups(eng, steps, i):
            steps(0, 0, True, False, 1, i)
            with eng.Fori(0, NG // 2 - 1) as k:
                steps(k * 2 + 1, 1, True, True, k * 2 + 2, i)
                steps(k * 2 + 2, 0, True, True, k * 2 + 3, i)
            steps(NG - 1, 1, True, True, None, i)
            steps(NG, 0, False, True, None, i)

        def batches(eng, l, batch):
            with eng.Fori(0, NB - 1) as b:
                batch(b, eng.snap(l * NB + b), True)
            batch(NB - 1, l * NB + (NB - 1), False)

        def prepare(steps, i, span):
            steps(-1, 1, False, False, 0, i, span)

        def lagging(s, lag, par, runs, behind):
            if s >= lag:
                return (s - lag, 0, par) if runs else None
            return (s - lag + U2, 1, 1 - par) if behind else None

        @block.tensor
        def _(pe):
            pe.wait_ge(tables_in, 48)
            pe.wait_ge(zeroed, AHEAD + 1)
            pe.wait_ge(padded, AHEAD + 1)
            with pe.Fori(0, DEPTH) as l:
                pe.wait_ge(w_in, l * NW + NW)
                apart(pe, chip)
                def project(g):
                    return pe.matmul(bank[:, 0, :], wo[:, g, :], ot[:, g, :], start=(g == 0), stop=(g == NG - 1))

                def steps(g, par, runs, behind, n, i, span=range(U2)):
                    q = i * NG + g
                    r = None if n is None else i * NG + n

                    def scores(u):
                        t, j = u // 2, u % 2
                        rows = slice(LD * j, LD * j + LD)
                        if u == 0:
                            pe.wait_ge(q_ready, AHEAD + q + 1)
                            pe.wait_ge(k_ready, AHEAD + q + 1)
                        pe.wait_ge(s_masked, AHEAD + (q * U2 + u - 1 if u >= 2 else q * U2))
                        apart(pe, chip)
                        pe.matmul(bank[:, 4 + j, 0:NK], q_sb[rows, par, t * P:(t + 1) * P],
                                  k_sb[rows, par, t * P:t * P + NK], start=True, stop=True).then_inc(s_made, 1)

                    def turn(u, back, par):
                        t, j = u // 2, u % 2
                        done = (q - back) * U2 + u
                        pe.wait_ge(p_ready, AHEAD + done + 1)
                        pe.wait_ge(pt_ready, AHEAD + (done - 1 if u else done))
                        if u == 1 and not behind:
                            pe.wait_ge(y_done, AHEAD + i)
                        apart(pe, chip)
                        ins = pe.transpose(bank[:, TB[j], 0:P], pb[:, u, P:PAD + NK], ident[:, :])
                        if t > 0:
                            ins = pe.transpose(bank[:, TB[j], P:NK], pb[0:WIN, u, 0:P], ident[0:WIN, 0:WIN])
                        ins.then_inc(p_turned, 1)

                    def weigh(u, back, par):
                        t, j = u // 2, u % 2
                        rows = slice(LD * j, LD * j + LD)
                        pe.wait_ge(pt_ready, AHEAD + (q - back) * U2 + u + 1)
                        if u == 0:
                            pe.wait_ge(ot_kept, AHEAD + q - back)
                            pe.wait_ge(v_kept, AHEAD + q - back + 1)
                        apart(pe, chip)
                        ins = pe.matmul(bank[rows, 7, t * P:(t + 1) * P], v_sb[:, par, t, rows], pt[:, u % NPT, 0:P],
                                        start=True, stop=(t == 0), skip_group_check=True)
                        if t > 0:
                            ins = pe.matmul(bank[rows, 7, t * P:t * P + WIN], v_sb[:, par, t - 1, rows],
                                            pt[:, u % NPT, P:NK], start=False, stop=True, skip_group_check=True)
                        ins.then_inc(pv_made, 1)

                    for s in span:
                        if runs:
                            scores(s)
                        unit = lagging(s, TURN, par, runs, behind)
                        if unit:
                            turn(*unit)
                        unit = lagging(s, WEIGH, par, runs, behind)
                        if unit:
                            weigh(*unit)
                        if n is None and runs and s >= WEIGH:
                            if s == WEIGH:
                                pe.wait_ge(q_turned, AHEAD + i * NG + NG)
                                pe.wait_ge(ot_kept, AHEAD + i * NG + NG - 1)
                                apart(pe, chip)
                            project(2 * (s - WEIGH))
                            project(2 * (s - WEIGH) + 1)
                        if n is None and not runs and s == 1:
                            project(NG - 2)
                        if n is None:
                            continue
                        def squares(a, col, made):
                            apart(pe, chip)
                            for t in range(TT):
                                ins = pe.matmul(bank[:, 3, col + 2 * t:col + 2 * t + 2],
                                                sq[:, a, t * P:(t + 1) * P], pair[:, :], start=True, stop=True)
                            ins.then_inc(made, 1)

                        if s == PREP_K:
                            pe.wait_ge(wst_ready, AHEAD + i * (NG + 1) + n + 1)
                            pe.wait_ge(q_turned, AHEAD + r)
                            pe.wait_ge(q_squared, AHEAD + r)
                            pe.wait_ge(xa_ready, AHEAD + i + 1)
                            apart(pe, chip)
                            pe.matmul(bank[:, 0, :], wst[:, 2, :], xa[:, :], start=True, stop=True)
                            pe.matmul(bank[:, 1, :], wst[:, 3, :], xa[:, :], start=True, stop=True).then_inc(k_made, 1)
                        if s == PREP_Q:
                            pe.wait_ge(k_squared, AHEAD + r + 1)
                            pe.wait_ge(v_kept, AHEAD + r)
                            squares(1, 0, ssk_made)
                            pe.wait_ge(k_turned, AHEAD + r + 1)
                            apart(pe, chip)
                            pe.matmul(bank[:, 0, :], wst[:, 0, :], xa[:, :], start=True, stop=True)
                            pe.matmul(bank[:, 1, :], wst[:, 1, :], xa[:, :], start=True, stop=True).then_inc(q_made, 1)
                        if s == PREP_SQ:
                            pe.wait_ge(q_squared, AHEAD + r + 1)
                            pe.wait_ge(ssk_kept, AHEAD + r + 1)
                            squares(0, 0, ssq_made)
                        if s == PREP_RK:
                            pe.wait_ge(rkb_ready, AHEAD + r + 1)
                            pe.wait_ge(ssq_kept, AHEAD + r + 1)
                            apart(pe, chip)
                            for t in range(TT):
                                ins = pe.matmul(bank[:, 3, t * P:(t + 1) * P], rkb[:, t, :], ident[:, :],
                                                start=True, stop=True)
                            ins.then_inc(rk_spread, 1)
                        if s == PREP_V:
                            pe.wait_ge(k_ready, AHEAD + r + 1)
                            apart(pe, chip)
                            for t in range(TT):
                                ins = pe.matmul(bank[:, 3, t * P:(t + 1) * P], xa[:, t * P:(t + 1) * P],
                                                wv[:, bass.ts(n, P)], start=True, stop=True)
                            ins.then_inc(v_made, 1)

                def batch(b, i, more):
                    groups(pe, steps, i)

                    pe.wait_ge(ot_kept, AHEAD + i * NG + NG)
                    apart(pe, chip)
                    project(NG - 1).then_inc(wo_made, 1)
                    if more:
                        pe.wait_ge(y_mid, AHEAD + i + 1)
                        prepare(steps, i + 1, (PREP_K,))
                    pe.wait_ge(xs_ready, AHEAD + i + 1)
                    apart(pe, chip)
                    pe.matmul(bank[:, 2, :], avg[:, :], xs[:, :], start=True, stop=True).then_inc(mean_made, 1)
                    if more:
                        prepare(steps, i + 1, (PREP_Q,))
                    pe.wait_ge(sqf_ready, AHEAD + i + 1)
                    apart(pe, chip)
                    for t in range(TT):
                        ins = pe.matmul(bank[:, 4, t:t + 1], sqf[:, t * P:(t + 1) * P], avg[:, 0:1], start=True, stop=True)
                    ins.then_inc(sv_made, 1)
                    if more:
                        prepare(steps, i + 1, (PREP_SQ,))
                    pe.wait_ge(rv_ready, AHEAD + i + 1)
                    apart(pe, chip)
                    for t in range(TT):
                        ins = pe.matmul(bank[:, 6, t * P:(t + 1) * P], rv[:, t:t + 1].to_broadcast([P, P]), ident[:, :],
                                        start=True, stop=True)
                    ins.then_inc(rv_spread, 1)
                    if more:
                        prepare(steps, i + 1, (PREP_RK,))
                    for c in range(HC + 1):
                        if c < HC:
                            if c == 0:
                                pe.wait_ge(xg_ready, AHEAD + i + 1)
                            if c >= 2:
                                pe.wait_ge(hh_ready, AHEAD + i * HC + c - 1)
                            apart(pe, chip)
                            pe.matmul(bank[:, 5 + 2 * (c % 2), :], w1[:, HC + c, :], xg[:, :], start=True, stop=True)
                            pe.matmul(bank[:, 4 + 2 * (c % 2), :], w1[:, c, :], xg[:, :], start=True, stop=True)\
                                .then_inc(h_made, 1)
                        if more and c == 0:
                            prepare(steps, i + 1, (PREP_V,))
                        if c >= 1:
                            pe.wait_ge(hh_ready, AHEAD + i * HC + c)
                            apart(pe, chip)
                            pe.matmul(bank[:, 2, :], w2[:, c - 1, :], hh[:, (c - 1) % 2, :], start=(c == 1), stop=(c == HC))\
                                .then_inc(w2_used, 1)

                prepare(steps, l * NB, range(U2))
                batches(pe, l, batch)

        @block.vector
        def _(dve):
            dve.memset(xs[LD:P, 0:1], 0.0)
            dve.memset(xa[LD:P, 0:1], 0.0)
            dve.memset(avg[:, :], 1.0 / D).then_inc(zeroed, 1)
            dve.wait_ge(tables_in, 48)
            with dve.Fori(0, DEPTH) as l:
                dve.wait_ge(w_in, l * NW + NW)
                apart(dve, chip)
                for a in range(4):
                    ins = dve.tensor_scalar(rot[:, a, :], base[:, a, :], cols[:, a:a + 1], None, ALU.mult)
                ins.then_inc(rot_ready, 1)
                dve.wait_ge(rot_ready, AHEAD + l + 1)
                apart(dve, chip)
                def weights(n):
                    dve.tensor_copy(wst[:, :, :].rearrange("p a c -> p (a c)"),
                                    wqk[:, bass.ds(n, 1), :].rearrange("p a c -> p (a c)")).then_inc(wst_ready, 1)

                def weights_0(i):
                    dve.wait_ge(q_made, AHEAD + i * NG)
                    dve.wait_ge(wst_ready, AHEAD + i * (NG + 1))
                    apart(dve, chip)
                    weights(0)

                def steps(g, par, runs, behind, n, i, span=range(U2)):
                    q = i * NG + g
                    r = None if n is None else i * NG + n

                    def masked(u):
                        t = u // 2
                        dve.wait_ge(s_made, AHEAD + q * U2 + u + 1)
                        dve.wait_ge(p_turned, AHEAD + ((q - 1) * U2 + u + 1 if behind else i * NG * U2))
                        if u == 0:
                            dve.wait_ge(nscale_ready, AHEAD + q + 1)
                        apart(dve, chip)
                        dve.tensor_tensor_reduce(pb[:, u, PAD:PAD + NK], bank[:, 4 + u % 2, 0:NK], mask[:, min(t, 1), :],
                                                 nscale[:, par, t, u % 2:u % 2 + 1], -NEG * 2, ALU.add, ALU.min,
                                                 nm[:, u:u + 1]).then_inc(s_masked, 1)

                    def normed(u, back, par):
                        done = (q - back) * U2 + u
                        dve.wait_ge(p_exp, AHEAD + done + 1)
                        dve.reciprocal(rr[:, u:u + 1], rs[:, u:u + 1]).then_inc(rr_ready, 1)
                        dve.wait_ge(rr_ready, AHEAD + done + 1)
                        dve.tensor_scalar(pb[:, u, PAD:PAD + NK], pb[:, u, PAD:PAD + NK], rr[:, u:u + 1], None,
                                          ALU.mult).then_inc(p_ready, 1)

                    for s in span:
                        if runs:
                            masked(s)
                        unit = lagging(s, NORM, par, runs, behind)
                        if unit:
                            normed(*unit)
                        if n is None:
                            continue
                        for at, a, squared, turned in ((PREP_K + 1, 1, k_squared, k_turned), (PREP_Q + 1, 0, q_squared, q_turned)):
                            if s == at:
                                dve.wait_ge(squared, AHEAD + r + 1)
                                dve.wait_ge((q_ready, k_ready)[a], AHEAD + r)
                                dve.tensor_tensor(t1[:, a, :], bank[:, 0, :], rot[:, 2 * a, :], ALU.mult)
                                dve.tensor_tensor(t2[:, a, :], bank[:, 1, :], rot[:, 2 * a + 1, :], ALU.mult)\
                                    .then_inc(turned, 1)
                        if s == PREP_SQ:
                            dve.wait_ge(rk_ready, AHEAD + r + 1)
                            dve.wait_ge(rk_spread, AHEAD + r)
                            apart(dve, chip)
                            dve.tensor_copy(
                                rkb[:, :, :].rearrange("p t (a c) -> p t a c", a=2),
                                rk[:, :, :].rearrange("p t (a c) -> p t a c", c=1).to_broadcast([P, TT, 2, LD]))\
                                .then_inc(rkb_ready, 1)
                        for at, ss, made, kept, used in ((PREP_Q, ssk, ssk_made, ssk_kept, rk_ready),
                                                         (PREP_SQ, ssq, ssq_made, ssq_kept, rq_ready)):
                            if s == at:
                                dve.wait_ge(made, AHEAD + r + 1)
                                dve.wait_ge(used, AHEAD + r)
                                apart(dve, chip)
                                dve.tensor_scalar(ss[:, :, :], bank[:, 3, 0:2 * TT].rearrange("p (t a) -> p t a", a=2),
                                                  1e-24, None, ALU.max).then_inc(kept, 1)
                        if s == PREP_RK + 1:
                            dve.wait_ge(q_made, AHEAD + r + 1)
                            apart(dve, chip)
                            weights(n + 1)
                        if s == PREP_RK:
                            dve.wait_ge(rk_spread, AHEAD + r + 1)
                            dve.wait_ge(k_added, AHEAD + r + 1)
                            dve.tensor_tensor(k_sb[:, 1 - par, WIN:WIN + S], bank[:, 3, :], t1[:, 1, :], ALU.mult)\
                                .then_inc(k_ready, 1)
                        if s == U2 - 1:
                            dve.wait_ge(rq_ready, AHEAD + r + 1)
                            apart(dve, chip)
                            dve.tensor_scalar(nscale[:, 1 - par, :, :], rq[:, :, :], -QKS, None, ALU.mult)\
                                .then_inc(nscale_ready, 1)

                def batch(b, i, more):
                    groups(dve, steps, i)

                    if more:
                        weights_0(i + 1)
                    yb = yT[:, bass.ts(b, S)]
                    dve.wait_ge(wo_made, AHEAD + i + 1)
                    dve.tensor_tensor(yb, yb, bank[:, 0, :], ALU.add).then_inc(y_mid, 1)
                    if more:
                        prepare(steps, i + 1, (PREP_K, PREP_K + 1))
                    dve.wait_ge(mean_made, AHEAD + i + 1)
                    dve.tensor_tensor(xc[:, :], xs[:, :], bank[:, 2, :], ALU.subtract).then_inc(xc_ready, 1)
                    if more:
                        prepare(steps, i + 1, (PREP_Q, PREP_Q + 1))
                    dve.wait_ge(sv_made, AHEAD + i + 1)
                    apart(dve, chip)
                    dve.tensor_scalar(sv[:, :], bank[:, 4, 0:TT], EPS, None, ALU.add).then_inc(sv_kept, 1)
                    if more:
                        prepare(steps, i + 1, (PREP_SQ,))
                    dve.wait_ge(rv_spread, AHEAD + i + 1)
                    dve.tensor_tensor(xc[:, :], xc[:, :], bank[:, 6, :], ALU.mult).then_inc(xcn_ready, 1)
                    if more:
                        prepare(steps, i + 1, range(PREP_RK, U2))
                    for c in range(HC):
                        dve.wait_ge(ge_ready, AHEAD + i * HC + c + 1)
                        dve.wait_ge(w2_used, AHEAD + i * HC + max(c - 1, 0))
                        dve.scalar_tensor_tensor(hh[:, c % 2, :], bank[:, 4 + 2 * (c % 2), :], cols[:, 8 + c:9 + c],
                                                 ge[:, c % 2, :], ALU.add, ALU.mult).then_inc(hh_ready, 1)
                    dve.wait_ge(w2_used, AHEAD + i * HC + HC)
                    apart(dve, chip)
                    dve.scalar_tensor_tensor(yb, bank[:, 2, :], cols[:, 6:7], yb, ALU.add, ALU.add).then_inc(y_done, 1)

                weights_0(l * NB)
                prepare(steps, l * NB, range(U2))
                batches(dve, l, batch)

        @block.scalar
        def _(act):
            with act.Fori(0, DEPTH) as l:
                def shifted(to, b, ready):
                    act.activation(to[0:LD, :], yT[0:LD, bass.ts(b, S)], ACT.Copy)
                    act.activation(to[LD:P, 1:S], yT[LD:P, bass.ds(b * S, S - 1)], ACT.Copy).then_inc(ready, 1)

                def steps(g, par, runs, behind, n, i, span=range(U2)):
                    q = i * NG + g
                    r = None if n is None else i * NG + n
                    for s in span:
                        if s == KEEP and behind:
                            act.wait_ge(pv_made, AHEAD + q * U2)
                            act.activation(ot[:, bass.ds(g - 1, 1), :], bank[:, 7:8, :], ACT.Copy).then_inc(ot_kept, 1)
                        if runs:
                            act.wait_ge(s_masked, AHEAD + q * U2 + s + 1)
                            act.activation(pb[:, s, PAD:PAD + NK], pb[:, s, PAD:PAD + NK], ACT.Exp,
                                           bias=nm[:, s:s + 1], scale=-1.0, accum_out=rs[:, s:s + 1]).then_inc(p_exp, 1)
                        unit = lagging(s, COPY, par, runs, behind)
                        if unit:
                            u, back, _ = unit
                            done = (q - back) * U2 + u
                            wide = NK if u // 2 > 0 else P
                            act.wait_ge(p_turned, AHEAD + done + 1)
                            act.wait_ge(pv_made, AHEAD + (done - NPT + 1 if u >= NPT - 1 or back == 0 and behind else i * NG * U2))
                            act.activation(pt[:, u % NPT, 0:wide], bank[:, TB[u % 2], 0:wide], ACT.Copy).then_inc(pt_ready, 1)
                        if n is None:
                            continue
                        for at, a, made, squared in ((PREP_K, 1, k_made, k_squared), (PREP_Q, 0, q_made, q_squared)):
                            if s == at:
                                act.wait_ge(made, AHEAD + r + 1)
                                act.wait_ge((ssq_made, ssk_made)[a], AHEAD + r)
                                act.activation(sq[:, a, :], bank[:, 0, :], ACT.Square).then_inc(squared, 1)
                        if s == PREP_V:
                            act.wait_ge(v_made, AHEAD + r + 1)
                            act.activation(v_sb[:, 1 - par, :, :], bank[:, 3, :].rearrange("p (t c) -> p t c", c=P),
                                           ACT.Copy).then_inc(v_kept, 1)

                def batch(b, i, more):
                    groups(act, steps, i)
                    if more:
                        act.wait_ge(v_made, AHEAD + i * NG + NG)
                        apart(act, chip)
                        shifted(xa, b + 1, xa_ready)
                    act.activation(early[:, 0:1], chip.ones[:, 0:1], ACT.Gelu)
                    act.wait_ge(y_mid, AHEAD + i + 1)
                    apart(act, chip)
                    shifted(xs, b, xs_ready)
                    if more:
                        prepare(steps, i + 1, (PREP_K,))
                    act.wait_ge(xc_ready, AHEAD + i + 1)
                    act.activation(sqf[:, :], xc[:, :], ACT.Square).then_inc(sqf_ready, 1)
                    if more:
                        prepare(steps, i + 1, (PREP_Q,))
                    act.wait_ge(xcn_ready, AHEAD + i + 1)
                    act.activation(xg[:, :], xc[:, :], ACT.Identity, bias=cols[:, 5:6], scale=cols[:, 4:5]).then_inc(xg_ready, 1)
                    if more:
                        prepare(steps, i + 1, (PREP_V,))
                    for c in range(HC):
                        act.wait_ge(h_made, AHEAD + i * HC + c + 1)
                        act.wait_ge(hh_ready, AHEAD + i * HC + max(c - 1, 0))
                        act.activation(ge[:, c % 2, :], bank[:, 5 + 2 * (c % 2), :], ACT.Gelu,
                                       bias=cols[:, 8 + HC + c:9 + HC + c]).then_inc(ge_ready, 1)
                    act.activation(early[:, 1:2], chip.ones[:, 0:1], ACT.Exp)

                act.wait_ge(y_done, AHEAD + l * NB)
                apart(act, chip)
                shifted(xa, 0, xa_ready)
                prepare(steps, l * NB, range(U2))
                batches(act, l, batch)

        @block.gpsimd
        def _(pool):
            pool.memset(pb[:, :, 0:PAD], 0.0)
            pool.memset(wqk[:, NG, :], 0.0)
            pool.memset(k_sb[:, :, 0:WIN], 0.0).then_inc(padded, 1)
            with pool.Fori(0, DEPTH) as l:
                pool.wait_ge(w_in, l * NW + NW)
                apart(pool, chip)
                def steps(g, par, runs, behind, n, i, span=range(U2)):
                    r = None if n is None else i * NG + n
                    if n is None:
                        return
                    for a, kept, ss, rn, norm_ready, used in ((1, ssk_kept, ssk, rk, rk_ready, rkb_ready),
                                                              (0, ssq_kept, ssq, rq, rq_ready, nscale_ready)):
                        if (PREP_K, PREP_Q)[1 - a] not in span:
                            continue
                        if a == 0:
                            pool.wait_ge(q_turned, AHEAD + r + 1)
                            pool.tensor_tensor(q_sb[:, 1 - par, :], t1[:, 0, :], t2[:, 0, :], ALU.add).then_inc(q_ready, 1)
                        pool.wait_ge(kept, AHEAD + r + 1)
                        pool.wait_ge(used, AHEAD + r)
                        pool.tensor_tensor(rn[:, :, :].rearrange("p t a -> p (t a)"),
                                           ss[:, :, :].rearrange("p t a -> p (t a)"),
                                           chip.mhalf[:, 0:2 * TT], ALU.pow).then_inc(norm_ready, 1)
                        if a == 1:
                            pool.wait_ge(k_turned, AHEAD + r + 1)
                            pool.tensor_tensor(t1[:, 1, :], t1[:, 1, :], t2[:, 1, :], ALU.add).then_inc(k_added, 1)

                def batch(b, i, more):
                    groups(pool, steps, i)
                    if more:
                        prepare(steps, i + 1, (PREP_K,))
                    pool.wait_ge(sv_kept, AHEAD + i + 1)
                    pool.tensor_tensor(rv[:, :], sv[:, :], chip.mhalf[:, 0:TT], ALU.pow).then_inc(rv_ready, 1)
                    if more:
                        prepare(steps, i + 1, (PREP_Q,))

                prepare(steps, l * NB, range(U2))
                batches(pool, l, batch)
                pool.wait_ge(y_done, AHEAD + l * NB + NB)
                apart(pool, chip)
                pool.sem_inc(layer_done, 1)

    with ExitStack() as ctx:
        m = Scope(chip, "lo", ctx)
        cur = m.sb("cur", [P, S])
        cur_ready = m.sem("cur_ready")
        turned = m.sem("turned")
        added = m.sem("added")
        block = ctx.enter_context(nc.Block())

        @block.sync
        def _(sp):
            m.start(sp)

        @block.gpsimd
        def _(pool):
            with pool.Fori(0, NB) as b:
                pool.wait_ge(turned, AHEAD + b)
                pool.tensor_copy(cur[:, :], yT[:, bass.ts(b, S)]).then_inc(cur_ready, 1)

        @block.tensor
        def _(pe):
            with pe.Fori(0, NB) as b:
                pe.wait_ge(cur_ready, AHEAD + b + 1)
                pe.wait_ge(added, AHEAD + b)
                for t in range(TT):
                    ins = pe.transpose(bank[:, 0, t * P:(t + 1) * P], cur[:, t * P:(t + 1) * P], ident[:, :])
                ins.then_inc(turned, 1)

        @block.vector
        def _(dve):
            with dve.Fori(0, NB) as b:
                dve.wait_ge(turned, AHEAD + b + 1)
                xb = chip.x[:, bass.ts(b, TT), :]
                dve.tensor_tensor(xb, xb, bank[:, 0, :].rearrange("p (t d) -> p t d", d=D), ALU.add).then_inc(added, 1)


def batch_softmax_attention(chip):
    nc, dram, bank = chip.nc, chip.dram, chip.bank
    sq128 = 1.0 / float(np.sqrt(np.float32(D)))
    with ExitStack() as outer:
        mo = Scope(chip, "b", outer)
        v_all = mo.sb("v", [P, NT, D])
        norm_stage(chip, "bn", dram["w_b_v"], v_all)
        qT = mo.sb("qT", [P, NB * S])
        kR = mo.sb("kR", [P, NB, S])
        with ExitStack() as ctx:
            m = Scope(chip, "bp", ctx)
            w = m.sb("w", [P, 2, D])
            cur = m.sb("cur", [P, TT, P])
            w_in = m.dma_sem("w_in")
            cur_ready = m.sem("cur_ready")
            q_made = m.sem("q_made")
            k_made = m.sem("k_made")
            q_kept = m.sem("q_kept")
            k_kept = m.sem("k_kept")
            block = ctx.enter_context(nc.Block())

            @block.sync
            def _(sp):
                m.start(sp)
                sp.dma_start(w[:, :, :], dram["w_b_qk"].rearrange("p (a c) -> p a c", c=D)).then_inc(w_in, 16)

            @block.gpsimd
            def _(pool):
                with pool.Fori(0, NB) as b:
                    pool.wait_ge(k_made, AHEAD + b)
                    pool.tensor_copy(cur[:, :, :], chip.xT[:, bass.ts(b, S)].rearrange("p (r c) -> p c r", c=TT))\
                        .then_inc(cur_ready, 1)

            @block.tensor
            def _(pe):
                pe.wait_ge(w_in, 16)
                with pe.Fori(0, NB) as b:
                    pe.wait_ge(q_kept, AHEAD + b)
                    pe.matmul(bank[:, 0, :], w[:, 0, :], chip.xT[:, bass.ts(b, S)], start=True, stop=True).then_inc(q_made, 1)
                    pe.wait_ge(cur_ready, AHEAD + b + 1)
                    pe.wait_ge(k_kept, AHEAD + b)
                    apart(pe, chip)
                    for c in range(TT):
                        ins = pe.matmul(bank[:, 1, c * P:(c + 1) * P], cur[:, c, :], w[:, 1, :], start=True, stop=True)
                    ins.then_inc(k_made, 1)

            @block.scalar
            def _(act):
                with act.Fori(0, NB) as b:
                    act.wait_ge(q_made, AHEAD + b + 1)
                    apart(act, chip)
                    act.activation(qT[:, bass.ts(b, S)], bank[:, 0, :], ACT.Copy).then_inc(q_kept, 1)

            @block.vector
            def _(dve):
                with dve.Fori(0, NB) as b:
                    dve.wait_ge(k_made, AHEAD + b + 1)
                    apart(dve, chip)
                    dve.tensor_copy(kR[:, bass.ds(b, 1), :], bank[:, 1:2, :]).then_inc(k_kept, 1)

        with ExitStack() as ctx:
            m = Scope(chip, "bs", ctx)
            mx = m.sb("mx", [P, S])
            sm = m.sb("sm", [P, S])
            e = m.sb("e", [P, NB, S])
            at = m.sb("at", [P, NB, S])
            s_made = m.sem("s_made")
            dve_step = m.sem("dve_step")
            e_in = m.sem("e_in")
            e_ready = m.sem("e_ready")
            a_ready = m.sem("a_ready")
            at_ready = m.sem("at_ready")
            o_made = m.sem("o_made")
            o_added = m.sem("o_added")
            block = ctx.enter_context(nc.Block())

            def over_batches(t):
                return t.rearrange("p b i -> p i b")

            @block.sync
            def _(sp):
                m.start(sp)

            @block.tensor
            def _(pe):
                for j in range(TT):
                    for b in range(NB):
                        pe.wait_ge(o_added, AHEAD + j * NB)
                        pe.matmul(bank[:, b, :], kR[:, b, j * P:(j + 1) * P], qT[:, b * S:(b + 1) * S],
                                  start=True, stop=True).then_inc(s_made, 1)
                    for b in range(NB):
                        pe.wait_ge(at_ready, AHEAD + j * NB + b + 1)
                        pe.wait_ge(e_in, AHEAD + (j + 1) * NB)
                        for i in range(TT):
                            ins = pe.matmul(bank[:, b, i * P:(i + 1) * P], at[:, b, i * P:(i + 1) * P],
                                            v_all[:, b * TT + j, :], start=True, stop=True)
                        ins.then_inc(o_made, 1)

            @block.vector
            def _(dve):
                for j in range(TT):
                    link = linker(dve, dve_step, j * 3, 3)
                    dve.wait_ge(s_made, AHEAD + (j + 1) * NB)
                    link(dve.tensor_reduce(mx[:, :], over_batches(bank[:, :, :]), AX.X, ALU.max))
                    for b in range(NB):
                        dve.tensor_tensor(e[:, b, :], bank[:, b, :], mx[:, :], ALU.subtract).then_inc(e_in, 1)
                    dve.wait_ge(e_ready, AHEAD + (j + 1) * NB)
                    link(dve.tensor_reduce(sm[:, :], over_batches(e[:, :, :]), AX.X, ALU.add))
                    link(dve.reciprocal(sm[:, :], sm[:, :]))
                    for b in range(NB):
                        dve.tensor_tensor(e[:, b, :], e[:, b, :], sm[:, :], ALU.mult).then_inc(a_ready, 1)
                    link.check()
                    for b in range(NB):
                        dve.wait_ge(o_made, AHEAD + j * NB + b + 1)
                        xb = chip.x[:, b * TT:(b + 1) * TT, :]
                        dve.tensor_tensor(xb, xb, bank[:, b, :].rearrange("p (t d) -> p t d", d=D), ALU.add)\
                            .then_inc(o_added, 1)
                        dve.wait_ge(o_added, AHEAD + j * NB + b + 1)

            @block.scalar
            def _(act):
                for j in range(TT):
                    for b in range(NB):
                        act.wait_ge(e_in, AHEAD + j * NB + b + 1)
                        act.activation(e[:, b, :], e[:, b, :], ACT.Exp, scale=sq128).then_inc(e_ready, 1)

            @block.gpsimd
            def _(pool):
                for j in range(TT):
                    for b in range(NB):
                        pool.wait_ge(a_ready, AHEAD + j * NB + b + 1)
                        pool.affine_select(out=at[:, b, :], in_=e[:, b, :], pattern=[[1, S]], compare_op=ALU.is_ge,
                                           fill=1e-9, base=-j * P, channel_multiplier=-1).then_inc(at_ready, 1)


NE4 = 8


def argmax_experts(chip):
    nc, dram, bank = chip.nc, chip.dram, chip.bank
    norm_stage(chip, "en")
    with ExitStack() as ctx:
        m = Scope(chip, "e", ctx)
        wg = m.sb("wg", [P, D])
        we = m.sb("we", [P, NE4 * D])
        be = m.sb("be", [1, NE4 * D])
        bg = m.sb("bg", [P, D])
        rev = m.sb("rev", [P, D])
        cur = m.sb("cur", [P, 2, S])
        lg = m.sb("lg", [P, TT, D])
        pr = m.sb("pr", [P, TT, D])
        eq = m.sb("eq", [P, TT, D])
        red = m.sb("red", [P, 4, TT])
        rcp = m.sb("rcp", [P, TT])
        oh = m.sb("oh", [P, TT, NE4])
        acc = m.sb("acc", [P, 2, D])
        w_in = m.dma_sem("w_in")
        cur_ready = m.sem("cur_ready")
        g_made = m.sem("g_made")
        g_read = m.sem("g_read")
        shifted = m.sem("shifted")
        e_ready = m.sem("e_ready")
        dve_step = m.sem("dve_step")
        h_made = m.sem("h_made")
        h_read = m.sem("h_read")
        block = ctx.enter_context(nc.Block())
        STEPS = 10 + TT * (NE4 + 1)

        @block.sync
        def _(sp):
            m.start(sp)
            sp.dma_start(wg[:, :], dram["w_e_g"]).then_inc(w_in, 16)
            sp.dma_start(we[:, :], dram["w_e_e"]).then_inc(w_in, 16)
            sp.dma_start(be[:, :], dram["w_e_be"]).then_inc(w_in, 16)
            sp.dma_start(bg[:, :], dram["w_e_bg"].partition_broadcast(P)).then_inc(w_in, 16)
            sp.dma_start(rev[:, :], dram["c_rev"]).then_inc(w_in, 16)

        @block.gpsimd
        def _(pool):
            with pool.Fori(0, NB // 2) as k:
                for r in range(2):
                    b = 2 * k + r
                    pool.wait_ge(h_made, AHEAD + 2 * k * TT)
                    pool.tensor_copy(cur[:, r, :], chip.xT[:, bass.ts(b, S)]).then_inc(cur_ready, 1)

        @block.tensor
        def _(pe):
            pe.wait_ge(w_in, 80)
            with pe.Fori(0, NB // 2) as k:
                for r in range(2):
                    b = 2 * k + r
                    pe.wait_ge(cur_ready, AHEAD + b + 1)
                    pe.wait_ge(g_read, AHEAD + b)
                    apart(pe, chip)
                    for t in range(TT):
                        ins = pe.matmul(bank[:, 0, t * P:(t + 1) * P], cur[:, r, t * P:(t + 1) * P], wg[:, :],
                                        start=True, stop=True)
                    ins.then_inc(g_made, 1)
                    for t in range(TT):
                        first = 2 + 2 * (t % 2)
                        pe.wait_ge(h_read, AHEAD + b * TT + max(t - 1, 0))
                        apart(pe, chip)
                        for half in range(2):
                            cols = slice(half * 4 * D, (half + 1) * 4 * D)
                            pe.matmul(bank[:, first + half, :], cur[:, r, t * P:(t + 1) * P], we[:, cols],
                                      start=True, stop=False)
                            ins = pe.matmul(bank[:, first + half, :], chip.ones[0:1, :], be[:, cols], start=False, stop=True)
                        ins.then_inc(h_made, 1)

        @block.scalar
        def _(act):
            with act.Fori(0, NB) as b:
                act.wait_ge(shifted, AHEAD + b + 1)
                act.activation(pr[:, :, :], lg[:, :, :], ACT.Exp).then_inc(e_ready, 1)

        @block.vector
        def _(dve):
            dve.wait_ge(w_in, 80)

            def per_tile(v):
                return v.rearrange("p (t a) -> p t a", a=1).to_broadcast([P, TT, D])

            def per_class(v):
                return v.rearrange("p (a c) -> p a c", a=1).to_broadcast([P, TT, D])

            with dve.Fori(0, NB) as b:
                link = linker(dve, dve_step, b * STEPS, STEPS)
                dve.wait_ge(g_made, AHEAD + b + 1)
                ins = dve.tensor_tensor(lg[:, :, :], bank[:, 0, :].rearrange("p (t c) -> p t c", c=D), per_class(bg[:, :]), ALU.add)
                ins.then_inc(g_read, 1)
                dve.wait_ge(g_read, AHEAD + b + 1)
                link(dve.tensor_reduce(red[:, 0, :], lg[:, :, :], AX.X, ALU.max))
                dve.tensor_tensor(lg[:, :, :], lg[:, :, :], per_tile(red[:, 0, :]), ALU.subtract).then_inc(shifted, 1)
                dve.wait_ge(e_ready, AHEAD + b + 1)
                link(dve.tensor_reduce(red[:, 1, :], pr[:, :, :], AX.X, ALU.add))
                link(dve.reciprocal(rcp[:, :], red[:, 1, :]))
                link(dve.tensor_tensor(pr[:, :, :], pr[:, :, :], per_tile(rcp[:, :]), ALU.mult))
                link(dve.tensor_reduce(red[:, 2, :], pr[:, :, :], AX.X, ALU.max))
                link(dve.tensor_tensor(eq[:, :, :], pr[:, :, :], per_tile(red[:, 2, :]), ALU.is_equal))
                link(dve.tensor_tensor(eq[:, :, :], eq[:, :, :], per_class(rev[:, :]), ALU.mult))
                link(dve.tensor_reduce(red[:, 3, :], eq[:, :, :], AX.X, ALU.max))
                link(dve.tensor_tensor(eq[:, :, :], per_class(rev[:, :]), per_tile(red[:, 3, :]), ALU.is_equal))
                link(dve.tensor_reduce(oh[:, :, :], eq[:, :, :].rearrange("p t (a e) -> p t e a", e=NE4), AX.X, ALU.max))
                for t in range(TT):
                    first = 2 + 2 * (t % 2)
                    dve.wait_ge(h_made, AHEAD + b * TT + t + 1)
                    apart(dve, chip)
                    for e in range(NE4):
                        h = bank[:, first + e // 4, (e % 4) * D:(e % 4 + 1) * D]
                        sel = oh[:, t, e:e + 1]
                        if e == 0:
                            link(dve.tensor_scalar(acc[:, t % 2, :], h, sel, None, ALU.mult))
                        else:
                            link(dve.scalar_tensor_tensor(acc[:, t % 2, :], h, sel, acc[:, t % 2, :], ALU.mult, ALU.add))
                    link(dve.tensor_scalar(acc[:, t % 2, :], acc[:, t % 2, :], 0.0, red[:, 2, t:t + 1], ALU.max, ALU.mult))
                    xt = chip.x[:, b * TT + t, :]
                    ins = dve.tensor_tensor(xt, xt, acc[:, t % 2, :], ALU.add)
                    ins.then_inc(h_read, 1)
                    dve.wait_ge(h_read, AHEAD + b * TT + t + 1)
                link.check()


DI = 256
NS5 = 128
SH5 = 32
SP5 = DI // SH5
KC = 4
XC = (DI + 2 * NS5) // P
HGRP = 4
DT_MIN, DT_MAX = 0.001, 0.1


def state_space(chip):
    nc, dram, bank, ident = chip.nc, chip.dram, chip.bank, chip.ident
    with ExitStack() as outer:
        mo = Scope(chip, "s", outer)
        xn_all = mo.sb("xn", [P, NT, D])
        norm_stage(chip, "sn", keep=xn_all)
        with ExitStack() as ctx:
            m = Scope(chip, "sx", ctx)
            w_x = m.sb("w_x", [P, XC, P])
            w_z = m.sb("w_z", [P, DI])
            w_dt = m.sb("w_dt", [P, SH5])
            w_o = m.sb("w_o", [P, 2, D])
            taps = m.sb("taps", [P, XC, KC + 1])
            rows = m.sb("rows", [P, 3 * SH5 + DI + 2 * D])
            upto = m.sb("upto", [P, P])
            pick = m.sb("pick", [SH5, SH5, P])
            acoef = m.sb("acoef", [P, SH5])
            cur = m.sb("cur", [P, S])
            cvin = m.sb("cvin", [P, XC, KC - 1 + S])
            cacc = m.sb("cacc", [P, XC, S])
            u = m.sb("u", [P, XC, S])
            sz = m.sb("sz", [P, TT, DI])
            dtr = m.sb("dtr", [P, TT, SH5])
            sg = m.sb("sg", [P, TT, SH5])
            dt = m.sb("dt", [P, TT, SH5])
            dA = m.sb("dA", [P, TT, SH5])
            xs = m.sb("xs", [P, TT, DI])
            bt = m.sb("bt", [P, TT, NS5])
            cum = m.sb("cum", [P, 2 * SH5])
            acT = m.sb("acT", [SH5, P])
            nac = m.sb("nac", [P, SH5])
            dif = m.sb("dif", [P, SH5])
            ex = m.sb("ex", [P, 3, SH5])
            xdt = m.sb("xdt", [P, DI])
            xdd = m.sb("xdd", [P, DI])
            cbm = m.sb("cbm", [P, P])
            tmin = m.sb("tmin", [P, 2, HGRP, P])
            mm = m.sb("mm", [P, 2, HGRP, P])
            state = m.sb("state", [P, DI])
            y = m.sb("y", [P, TT, DI])
            t1 = m.sb("t1", [P, DI])
            ysq = m.sb("ysq", [P, DI])
            ms = m.sb("ms", [P, TT])
            ms2 = m.sb("ms2", [P, TT])
            rms = m.sb("rms", [P, TT])
            yT = m.sb("yT", [P, 2, S])
            stats = m.sb("stats", [P, TT, 6])
            mv = m.sb("mv", [P, TT, 2])
            ve = m.sb("ve", [P, TT])
            rstd = m.sb("rstd", [P, TT])
            ln = m.sb("ln", [P, TT, D])
            w_in = m.dma_sem("w_in")
            a_exp = m.sem("a_exp")
            zeroed = m.sem("zeroed")
            cur_ready = m.sem("cur_ready")
            xbc_made = m.sem("xbc_made")
            cv_ready = m.sem("cv_ready")
            conv_done = m.sem("conv_done")
            u_ready = m.sem("u_ready")
            z_made = m.sem("z_made")
            sz_ready = m.sem("sz_ready")
            dt_made = m.sem("dt_made")
            dtr_ready = m.sem("dtr_ready")
            sg_ready = m.sem("sg_ready")
            dA_ready = m.sem("dA_ready")
            tok_made = m.sem("tok_made")
            tok_kept = m.sem("tok_kept")
            cum_made = m.sem("cum_made")
            cum_kept = m.sem("cum_kept")
            dif_ready = m.sem("dif_ready")
            ex_ready = m.sem("ex_ready")
            cb_made = m.sem("cb_made")
            cb_read = m.sem("cb_read")
            xdd_ready = m.sem("xdd_ready")
            st_made = m.sem("st_made")
            state_ready = m.sem("state_ready")
            ab_made = m.sem("ab_made")
            min_ready = m.sem("min_ready")
            seg_ready = m.sem("seg_ready")
            mm_ready = m.sem("mm_ready")
            yd_part = m.sem("yd_part")
            y_read = m.sem("y_read")
            y_gated = m.sem("y_gated")
            ms_ready = m.sem("ms_ready")
            ms2_ready = m.sem("ms2_ready")
            rms_ready = m.sem("rms_ready")
            yn_ready = m.sem("yn_ready")
            yT_made = m.sem("yT_made")
            yT_kept = m.sem("yT_kept")
            out_made = m.sem("out_made")
            ve_ready = m.sem("ve_ready")
            rstd_ready = m.sem("rstd_ready")
            x_done = m.sem("x_done")
            dve_step = m.sem("dve_step")
            block = ctx.enter_context(nc.Block())
            NHG = SH5 // HGRP

            def row(k, n):
                return rows[:, k:k + n]
            A_LOG, DT_B, D_SK = row(0, SH5), row(SH5, SH5), row(2 * SH5, SH5)
            NORM_W, LN_W, LN_B = row(3 * SH5, DI), row(3 * SH5 + DI, D), row(3 * SH5 + DI + D, D)

            @block.sync
            def _(sp):
                m.start(sp)
                sp.dma_start(w_x[:, :, :], dram["w_s_x"].rearrange("p (a c) -> p a c", c=P)).then_inc(w_in, 16)
                sp.dma_start(w_z[:, :], dram["w_s_z"]).then_inc(w_in, 16)
                sp.dma_start(w_dt[:, :], dram["w_s_dt"]).then_inc(w_in, 16)
                sp.dma_start(w_o[:, :, :], dram["w_s_o"].rearrange("(a p) d -> p a d", p=P)).then_inc(w_in, 16)
                sp.dma_start(taps[:, :, :], dram["w_s_taps"].rearrange("(a p) k -> p a k", p=P)).then_inc(w_in, 16)
                sp.dma_start(rows[:, :], dram["w_s_rows"].partition_broadcast(P)).then_inc(w_in, 16)
                sp.dma_start(upto[:, :], dram["c_upto"]).then_inc(w_in, 16)
                sp.dma_start(pick[:, :, :], dram["c_pick5"].rearrange("k (a c) -> k a c", c=P)).then_inc(w_in, 16)

            @block.gpsimd
            def _(pool):
                pool.memset(cvin[:, :, 0:KC - 1], 0.0).then_inc(zeroed, 1)
                with pool.Fori(0, NB) as b:
                    pool.wait_ge(out_made, AHEAD + b)
                    pool.tensor_copy(cur[:, :], chip.xT[:, bass.ts(b, S)]).then_inc(cur_ready, 1)
                    pool.wait_ge(ms2_ready, AHEAD + b + 1)
                    pool.tensor_tensor(rms[:, :], ms2[:, :], chip.mhalf[:, 0:TT], ALU.pow).then_inc(rms_ready, 1)
                    pool.wait_ge(ve_ready, AHEAD + b + 1)
                    pool.tensor_tensor(rstd[:, :], ve[:, :], chip.mhalf[:, 0:TT], ALU.pow).then_inc(rstd_ready, 1)

            @block.tensor
            def _(pe):
                pe.wait_ge(w_in, 128)
                with pe.Fori(0, NB) as b:
                    pe.wait_ge(cur_ready, AHEAD + b + 1)
                    pe.wait_ge(x_done, AHEAD + b)
                    for c in range(XC):
                        if c >= 2:
                            pe.wait_ge(cv_ready, AHEAD + b * XC + c - 1)
                        apart(pe, chip)
                        pe.matmul(bank[:, c % 2, :], w_x[:, c, :], cur[:, :], start=True, stop=True).then_inc(xbc_made, 1)
                    for t in range(TT):
                        ins = pe.matmul(bank[:, 2 + t // 2, (t % 2) * DI:(t % 2 + 1) * DI], cur[:, t * P:(t + 1) * P], w_z[:, :],
                                        start=True, stop=True)
                    ins.then_inc(z_made, 1)
                    for t in range(TT):
                        ins = pe.matmul(bank[:, 4, t * SH5:(t + 1) * SH5], cur[:, t * P:(t + 1) * P], w_dt[:, :],
                                        start=True, stop=True)
                    ins.then_inc(dt_made, 1)
                    pe.wait_ge(u_ready, AHEAD + b * XC + 3)
                    apart(pe, chip)
                    for t in range(TT):
                        for c in range(2):
                            pe.transpose(bank[:, 5 + t // 2, (t % 2) * DI + c * P:(t % 2) * DI + (c + 1) * P],
                                         u[:, c, t * P:(t + 1) * P], ident[:, :])
                    for t in range(TT):
                        ins = pe.transpose(bank[:, 7, t * P:(t + 1) * P], u[:, 2, t * P:(t + 1) * P], ident[:, :])
                    ins.then_inc(tok_made, 1)
                    pe.wait_ge(u_ready, AHEAD + b * XC + XC)
                    pe.wait_ge(dA_ready, AHEAD + b + 1)
                    pe.wait_ge(tok_kept, AHEAD + b + 1)
                    apart(pe, chip)
                    for t in range(TT):
                        i = b * TT + t
                        tile = slice(t * P, (t + 1) * P)
                        pe.wait_ge(y_read, AHEAD + i)
                        apart(pe, chip)
                        pe.matmul(bank[:, 4, 0:SH5], upto[:, :], dA[:, t, :], start=True, stop=True)
                        pe.matmul(bank[:, 4, SH5:2 * SH5], chip.ones[:, :], dA[:, t, :], start=True, stop=True)
                        pe.matmul(bank[0:SH5, 4, 2 * SH5:2 * SH5 + P], dA[:, t, :], upto[:, :], start=True, stop=True)\
                            .then_inc(cum_made, 1)
                        pe.matmul(bank[:, 5, 0:P], u[:, 2, tile], u[:, 3, tile], start=True, stop=True).then_inc(cb_made, 1)
                        for g in range(NHG + 2):
                            if g < NHG:
                                if g == 0:
                                    pe.wait_ge(cum_kept, AHEAD + i + 1)
                                pe.wait_ge(min_ready, AHEAD + i * NHG + max(g - 1, 0))
                                apart(pe, chip)
                                for k in range(HGRP):
                                    ins = pe.matmul(bank[:, g % 2, k * P:(k + 1) * P], pick[:, g * HGRP + k, :], acT[:, :],
                                                    start=True, stop=True)
                                ins.then_inc(ab_made, 1)
                            if g == 1:
                                pe.wait_ge(xdd_ready, AHEAD + i + 1)
                                pe.wait_ge(state_ready, AHEAD + b * (TT + 1) + t + 1)
                                apart(pe, chip)
                                pe.matmul(bank[:, 6, 0:DI], bt[:, t, :], xdd[:, :], start=True, stop=True)
                                pe.matmul(bank[:, 6, DI:2 * DI], u[:, 3, tile], state[:, :], start=True, stop=True)\
                                    .then_inc(st_made, 1)
                            if g >= 2:
                                pe.wait_ge(mm_ready, AHEAD + i * NHG + g - 1)
                                apart(pe, chip)
                                for k in range(HGRP):
                                    h = (g - 2) * HGRP + k
                                    ins = pe.matmul(bank[:, 7, h * SP5:(h + 1) * SP5], mm[:, g % 2, k, :],
                                                    xdt[:, h * SP5:(h + 1) * SP5], start=True, stop=True)
                                ins.then_inc(yd_part, 1)
                    pe.wait_ge(yn_ready, AHEAD + b + 1)
                    apart(pe, chip)
                    for t in range(TT):
                        for c in range(2):
                            ins = pe.transpose(bank[:, 2 + c, t * P:(t + 1) * P], y[:, t, c * P:(c + 1) * P], ident[:, :])
                    ins.then_inc(yT_made, 1)
                    pe.wait_ge(yT_kept, AHEAD + b + 1)
                    apart(pe, chip)
                    for t in range(TT):
                        for c in range(2):
                            ins = pe.matmul(bank[:, 5, t * D:(t + 1) * D], yT[:, c, t * P:(t + 1) * P], w_o[:, c, :],
                                            start=(c == 0), stop=(c == 1))
                    ins.then_inc(out_made, 1)

            @block.scalar
            def _(act):
                act.wait_ge(w_in, 128)
                act.activation(acoef[:, :], A_LOG, ACT.Exp).then_inc(a_exp, 1)
                with act.Fori(0, NB) as b:
                    for c in range(XC):
                        act.wait_ge(xbc_made, AHEAD + b * XC + c + 1)
                        act.wait_ge(conv_done, AHEAD + b * XC)
                        act.activation(cvin[:, c, KC - 1:], bank[:, c % 2, :], ACT.Copy).then_inc(cv_ready, 1)
                    act.wait_ge(z_made, AHEAD + b + 1)
                    act.activation(sz[:, 0:2, :], bank[:, 2, :].rearrange("p (t c) -> p t c", c=DI), ACT.Silu)
                    act.activation(sz[:, 2:4, :], bank[:, 3, :].rearrange("p (t c) -> p t c", c=DI), ACT.Silu).then_inc(sz_ready, 1)
                    for c in range(XC):
                        act.wait_ge(conv_done, AHEAD + b * XC + c + 1)
                        act.activation(u[:, c, :], cacc[:, c, :], ACT.Silu).then_inc(u_ready, 1)
                    act.wait_ge(dtr_ready, AHEAD + b + 1)
                    act.activation(sg[:, :, :], dtr[:, :, :], ACT.Sigmoid).then_inc(sg_ready, 1)
                    act.wait_ge(tok_made, AHEAD + b + 1)
                    act.activation(xs[:, 0:2, :], bank[:, 5, :].rearrange("p (t c) -> p t c", c=DI), ACT.Copy)
                    act.activation(xs[:, 2:4, :], bank[:, 6, :].rearrange("p (t c) -> p t c", c=DI), ACT.Copy)
                    act.activation(bt[:, :, :], bank[:, 7, :].rearrange("p (t c) -> p t c", c=NS5), ACT.Copy).then_inc(tok_kept, 1)
                    for t in range(TT):
                        i = b * TT + t
                        act.wait_ge(cum_made, AHEAD + i + 1)
                        act.activation(cum[:, :], bank[:, 4, 0:2 * SH5], ACT.Copy)
                        act.activation(acT[:, :], bank[0:SH5, 4, 2 * SH5:2 * SH5 + P], ACT.Copy).then_inc(cum_kept, 1)
                        act.wait_ge(dif_ready, AHEAD + i + 1)
                        act.activation(ex[:, 0:2, :], cum[:, :].rearrange("p (a h) -> p a h", a=2), ACT.Exp)
                        act.activation(ex[:, 2, :], dif[:, :], ACT.Exp).then_inc(ex_ready, 1)
                        for g in range(NHG):
                            act.wait_ge(min_ready, AHEAD + i * NHG + g + 1)
                            for k in range(HGRP):
                                h = g * HGRP + k
                                ins = act.activation(tmin[:, g % 2, k, :], tmin[:, g % 2, k, :], ACT.Exp, bias=nac[:, h:h + 1])
                            ins.then_inc(seg_ready, 1)
                    for t in range(TT):
                        act.wait_ge(y_gated, AHEAD + b * TT + t + 1)
                        act.activation(ysq[:, :], y[:, t, :], ACT.Square, accum_out=ms[:, t:t + 1]).then_inc(ms_ready, 1)
                        act.wait_ge(ms_ready, AHEAD + b * TT + t + 1)
                    act.wait_ge(yT_made, AHEAD + b + 1)
                    act.activation(yT[:, 0, :], bank[:, 2, :], ACT.Copy)
                    act.activation(yT[:, 1, :], bank[:, 3, :], ACT.Copy).then_inc(yT_kept, 1)

            STEPS = SS_STEPS

            @block.vector
            def _(dve):
                dve.wait_ge(w_in, 128)
                dve.wait_ge(a_exp, AHEAD + 1)
                dve.tensor_scalar(acoef[:, :], acoef[:, :], -1.0, None, ALU.mult).then_inc(a_exp, 1)
                dve.wait_ge(a_exp, AHEAD + 2)
                dve.wait_ge(zeroed, AHEAD + 1)

                def heads(v):
                    return v.rearrange("p (h a) -> p h a", a=1).to_broadcast([P, SH5, SP5])

                def by_head(v):
                    return v.rearrange("p (h c) -> p h c", c=SP5)

                with dve.Fori(0, NB) as b:
                    link = linker(dve, dve_step, b * STEPS, STEPS)
                    for c in range(XC):
                        dve.wait_ge(cv_ready, AHEAD + b * XC + c + 1)
                        dve.wait_ge(u_ready, AHEAD + b * XC)
                        apart(dve, chip)
                        link(dve.tensor_scalar(cacc[:, c, :], cvin[:, c, 0:S], taps[:, c, 0:1], None, ALU.mult))
                        for k in range(1, KC):
                            link(dve.scalar_tensor_tensor(cacc[:, c, :], cvin[:, c, k:k + S], taps[:, c, k:k + 1],
                                                          cacc[:, c, :], ALU.mult, ALU.add))
                        dve.tensor_scalar(cacc[:, c, :], cacc[:, c, :], taps[:, c, KC:KC + 1], None, ALU.add)\
                            .then_inc(conv_done, 1)
                    dve.wait_ge(dt_made, AHEAD + b + 1)
                    dve.tensor_tensor(dtr[:, :, :], bank[:, 4, 0:TT * SH5].rearrange("p (t h) -> p t h", h=SH5),
                                      DT_B.rearrange("p (a h) -> p a h", a=1).to_broadcast([P, TT, SH5]), ALU.add)\
                        .then_inc(dtr_ready, 1)
                    link(dve.memset(state[:, :], 0.0))
                    dve.sem_inc(state_ready, 1)
                    dve.wait_ge(sg_ready, AHEAD + b + 1)
                    apart(dve, chip)
                    link(dve.tensor_scalar(dt[:, :, :], sg[:, :, :], DT_MAX - DT_MIN, DT_MIN, ALU.mult, ALU.add))
                    dve.tensor_tensor(dA[:, :, :], dt[:, :, :],
                                      acoef[:, :].rearrange("p (a h) -> p a h", a=1).to_broadcast([P, TT, SH5]), ALU.mult)\
                        .then_inc(dA_ready, 1)
                    dve.wait_ge(tok_kept, AHEAD + b + 1)
                    for t in range(TT):
                        i = b * TT + t
                        link(dve.tensor_tensor(by_head(xdt[:, :]), by_head(xs[:, t, :]), heads(dt[:, t, :]), ALU.mult))
                        dve.wait_ge(cum_kept, AHEAD + i + 1)
                        apart(dve, chip)
                        dve.tensor_scalar(nac[:, :], cum[:, 0:SH5], -1.0, None, ALU.mult)
                        dve.tensor_tensor(dif[:, :], cum[:, SH5:], cum[:, 0:SH5], ALU.subtract).then_inc(dif_ready, 1)
                        dve.wait_ge(cb_made, AHEAD + i + 1)
                        link(dve.tensor_tensor(cbm[:, :], bank[:, 5, 0:P], upto[:, :], ALU.mult))
                        dve.wait_ge(ex_ready, AHEAD + i + 1)
                        dve.tensor_tensor(by_head(xdd[:, :]), by_head(xdt[:, :]), heads(ex[:, 2, :]), ALU.mult)\
                            .then_inc(xdd_ready, 1)
                        for g in range(NHG + 1):
                            if g < NHG:
                                dve.wait_ge(ab_made, AHEAD + i * NHG + g + 1)
                                dve.wait_ge(mm_ready, AHEAD + i * NHG + max(g - 1, 0))
                                own = cum[:, g * HGRP:(g + 1) * HGRP].rearrange("p (h a) -> p h a", a=1).to_broadcast([P, HGRP, P])
                                dve.tensor_tensor(tmin[:, g % 2, :, :], bank[:, g % 2, :].rearrange("p (h q) -> p h q", q=P),
                                                  own, ALU.min).then_inc(min_ready, 1)
                            if g >= 1:
                                dve.wait_ge(seg_ready, AHEAD + i * NHG + g)
                                dve.wait_ge(yd_part, AHEAD + i * NHG + max(g - 2, 0))
                                dve.tensor_tensor(mm[:, (g - 1) % 2, :, :], tmin[:, (g - 1) % 2, :, :],
                                                  cbm[:, :].rearrange("p (a q) -> p a q", a=1).to_broadcast([P, HGRP, P]),
                                                  ALU.mult).then_inc(mm_ready, 1)
                        dve.wait_ge(st_made, AHEAD + i + 1)
                        link(dve.tensor_tensor(by_head(y[:, t, :]), by_head(bank[:, 6, DI:2 * DI]), heads(ex[:, 0, :]), ALU.mult))
                        link(dve.tensor_tensor(by_head(t1[:, :]), by_head(xs[:, t, :]), heads(D_SK), ALU.mult))
                        link(dve.tensor_tensor(y[:, t, :], y[:, t, :], t1[:, :], ALU.add))
                        link(dve.tensor_tensor(by_head(state[:, :]), by_head(state[:, :]), heads(ex[:, 1, :]), ALU.mult))
                        link(dve.tensor_tensor(state[:, :], state[:, :], bank[:, 6, 0:DI], ALU.add))
                        dve.sem_inc(state_ready, 1)
                        dve.wait_ge(yd_part, AHEAD + (i + 1) * NHG)
                        dve.tensor_tensor(y[:, t, :], y[:, t, :], bank[:, 7, 0:DI], ALU.add).then_inc(y_read, 1)
                        dve.wait_ge(y_read, AHEAD + i + 1)
                        dve.wait_ge(sz_ready, AHEAD + b + 1)
                        dve.tensor_tensor(y[:, t, :], y[:, t, :], sz[:, t, :], ALU.mult).then_inc(y_gated, 1)
                    dve.wait_ge(ms_ready, AHEAD + (b + 1) * TT)
                    apart(dve, chip)
                    dve.tensor_scalar(ms2[:, :], ms[:, :], 1.0 / DI, EPS, ALU.mult, ALU.add).then_inc(ms2_ready, 1)
                    dve.wait_ge(rms_ready, AHEAD + b + 1)
                    apart(dve, chip)
                    for t in range(TT):
                        ins = dve.scalar_tensor_tensor(y[:, t, :], y[:, t, :], rms[:, t:t + 1], NORM_W, ALU.mult, ALU.mult)
                    ins.then_inc(yn_ready, 1)
                    dve.wait_ge(out_made, AHEAD + b + 1)
                    apart(dve, chip)
                    for t in range(TT):
                        ins = dve.bn_stats(stats[:, t, :], bank[:, 5, t * D:(t + 1) * D])
                    link(ins)
                    apart(dve, chip)
                    for t in range(TT):
                        ins = dve.bn_aggr(mv[:, t, :], stats[:, t, :])
                    link(ins)
                    apart(dve, chip)
                    dve.tensor_scalar(ve[:, :], mv[:, :, 1], EPS, None, ALU.add).then_inc(ve_ready, 1)
                    dve.wait_ge(rstd_ready, AHEAD + b + 1)
                    apart(dve, chip)
                    for t in range(TT):
                        ins = dve.tensor_scalar(ln[:, t, :], bank[:, 5, t * D:(t + 1) * D], mv[:, t, 0:1], rstd[:, t:t + 1],
                                                ALU.subtract, ALU.mult)
                    link(ins)
                    wide = lambda v: v.rearrange("p (a d) -> p a d", a=1).to_broadcast([P, TT, D])
                    link(dve.tensor_tensor(ln[:, :, :], ln[:, :, :], wide(LN_W), ALU.mult))
                    link(dve.tensor_tensor(ln[:, :, :], ln[:, :, :], wide(LN_B), ALU.add))
                    link(dve.tensor_tensor(ln[:, :, :], ln[:, :, :], xn_all[:, bass.ts(b, TT), :], ALU.add))
                    xb = chip.x[:, bass.ts(b, TT), :]
                    dve.tensor_tensor(xb, xb, ln[:, :, :], ALU.add).then_inc(x_done, 1)
                    link.check()


SS_STEPS = XC * KC + 2 + TT * 7 + 6


def first_of_top(dve, link, src, top, rev, tmp, top_rev, onehot, shape):
    def along(v):
        return v.rearrange("p (t a) -> p t a", a=1).to_broadcast(shape)

    def across(v):
        return v.rearrange("p (a c) -> p a c", a=1).to_broadcast(shape)

    link(dve.tensor_reduce(top, src, AX.X, ALU.max))
    link(dve.tensor_tensor(tmp, src, along(top), ALU.is_equal))
    link(dve.tensor_tensor(tmp, tmp, across(rev), ALU.mult))
    link(dve.tensor_reduce(top_rev, tmp, AX.X, ALU.max))
    link(dve.tensor_tensor(onehot, across(rev), along(top_rev), ALU.is_equal))


NE6 = 8
CAP = 160
H6 = 512
HC6 = H6 // P
K6 = NE6 + 1


def capacity_experts(chip):
    nc, dram, bank, ident = chip.nc, chip.dram, chip.bank, chip.ident
    norm_stage(chip, "cn")
    with ExitStack() as outer:
        mo = Scope(chip, "c", outer)
        selT = mo.sb("selT", [K6, NB * S])
        with ExitStack() as ctx:
            m = Scope(chip, "cr", ctx)
            rw = m.sb("rw", [P, NE6])
            rb = m.sb("rb", [P, NE6])
            rev = m.sb("rev", [P, D])
            upto = m.sb("upto", [P, P])
            lg = m.sb("lg", [P, NT, NE6])
            pr = m.sb("pr", [P, NT, NE6])
            tmp = m.sb("tmp", [P, NT, NE6])
            oh = m.sb("oh", [P, NT, NE6])
            tot = m.sb("tot", [P, 2, NT, NE6])
            sel = m.sb("sel", [P, NT, K6])
            red = m.sb("red", [P, 4, NT])
            w_in = m.dma_sem("w_in")
            made = m.sem("made")
            dve_step = m.sem("dve_step")
            shifted = m.sem("shifted")
            e_ready = m.sem("e_ready")
            oh_ready = m.sem("oh_ready")
            counted = m.sem("counted")
            sel_ready = m.sem("sel_ready")
            turned = m.sem("turned")
            kept = m.sem("kept")
            block = ctx.enter_context(nc.Block())
            SH = [P, NT, NE6]

            @block.sync
            def _(sp):
                m.start(sp)
                sp.dma_start(rw[:, :], dram["w_c_r"]).then_inc(w_in, 16)
                sp.dma_start(rb[:, :], dram["w_c_rb"].partition_broadcast(P)).then_inc(w_in, 16)
                sp.dma_start(rev[:, :], dram["c_rev"]).then_inc(w_in, 16)
                sp.dma_start(upto[:, :], dram["c_upto"]).then_inc(w_in, 16)

            @block.tensor
            def _(pe):
                pe.wait_ge(w_in, 64)
                for n in range(NT):
                    ins = pe.matmul(bank[:, 0, n * NE6:(n + 1) * NE6], chip.xT[:, n * P:(n + 1) * P], rw[:, :],
                                    start=True, stop=True)
                ins.then_inc(made, 1)
                pe.wait_ge(oh_ready, AHEAD + 1)
                flat = oh[:, :, :].rearrange("p t e -> p (t e)")
                pe.matmul(bank[:, 1, 0:NT * NE6], upto[:, :], flat, start=True, stop=True)
                pe.matmul(bank[:, 2, 0:NT * NE6], chip.ones[:, :], flat, start=True, stop=True).then_inc(counted, 1)
                pe.wait_ge(sel_ready, AHEAD + 1)
                for b in range(NB):
                    if b >= 2:
                        pe.wait_ge(kept, AHEAD + b - 1)
                    for t in range(TT):
                        ins = pe.transpose(bank[0:K6, 3 + b % 2, t * P:(t + 1) * P], sel[:, b * TT + t, :], ident[:, :])
                    ins.then_inc(turned, 1)

            @block.scalar
            def _(act):
                act.wait_ge(shifted, AHEAD + 1)
                act.activation(pr[:, :, :], lg[:, :, :], ACT.Exp).then_inc(e_ready, 1)
                for b in range(NB):
                    act.wait_ge(turned, AHEAD + b + 1)
                    act.activation(selT[:, b * S:(b + 1) * S], bank[0:K6, 3 + b % 2, :], ACT.Copy).then_inc(kept, 1)

            @block.vector
            def _(dve):
                dve.wait_ge(w_in, 64)
                link = linker(dve, dve_step, 0, 19)
                dve.wait_ge(made, AHEAD + 1)
                link(dve.tensor_tensor(lg[:, :, :], bank[:, 0, 0:NT * NE6].rearrange("p (t e) -> p t e", e=NE6),
                                       rb[:, :].rearrange("p (a e) -> p a e", a=1).to_broadcast(SH), ALU.add))
                link(dve.tensor_reduce(red[:, 0, :], lg[:, :, :], AX.X, ALU.max))
                dve.tensor_tensor(lg[:, :, :], lg[:, :, :],
                                  red[:, 0, :].rearrange("p (t a) -> p t a", a=1).to_broadcast(SH), ALU.subtract)\
                    .then_inc(shifted, 1)
                dve.wait_ge(e_ready, AHEAD + 1)
                link(dve.tensor_reduce(red[:, 1, :], pr[:, :, :], AX.X, ALU.add))
                link(dve.reciprocal(red[:, 1, :], red[:, 1, :]))
                link(dve.tensor_tensor(pr[:, :, :], pr[:, :, :],
                                       red[:, 1, :].rearrange("p (t a) -> p t a", a=1).to_broadcast(SH), ALU.mult))
                first_of_top(dve, link, pr[:, :, :], red[:, 2, :], rev[:, 0:NE6], tmp[:, :, :], red[:, 3, :], oh[:, :, :], SH)
                dve.sem_inc(oh_ready, 1)
                dve.wait_ge(counted, AHEAD + 1)
                link(dve.tensor_copy(tot[:, 0, :, :], bank[:, 2, 0:NT * NE6].rearrange("p (t e) -> p t e", e=NE6)))
                src = 0
                step = 1
                while step < NT:
                    dve.tensor_tensor(tot[:, 1 - src, step:, :], tot[:, src, step:, :], tot[:, src, 0:NT - step, :], ALU.add)
                    link(dve.tensor_copy(tot[:, 1 - src, 0:step, :], tot[:, src, 0:step, :]))
                    src, step = 1 - src, 2 * step
                rank = tmp
                dve.tensor_copy(rank[:, 0, :], bank[:, 1, 0:NE6])
                link(dve.tensor_tensor(rank[:, 1:, :], bank[:, 1, NE6:NT * NE6].rearrange("p (t e) -> p t e", e=NE6),
                                       tot[:, src, 0:NT - 1, :], ALU.add))
                link(dve.scalar_tensor_tensor(sel[:, :, 0:NE6], rank[:, :, :], float(CAP), oh[:, :, :], ALU.is_le, ALU.mult))
                link(dve.tensor_reduce(red[:, 0, :], sel[:, :, 0:NE6], AX.X, ALU.add))
                dve.tensor_scalar(sel[:, :, NE6], red[:, 0, :], -1.0, 1.0, ALU.mult, ALU.add).then_inc(sel_ready, 1)
                link.check()

        with ExitStack() as ctx:
            m = Scope(chip, "cx", ctx)
            w1 = m.sb("w1", [P, K6 * HC6, P])
            w2 = m.sb("w2", [P, K6 * HC6, D])
            b1 = m.sb("b1", [P, K6 * HC6])
            b2 = m.sb("b2", [K6, D])
            pick = m.sb("pick", [K6, K6, P])
            rl = m.sb("rl", [P, 2, S])
            hm = m.sb("hm", [P, 2, S])
            w_in = m.dma_sem("w_in")
            spread = m.sem("spread")
            h_made = m.sem("h_made")
            rl_ready = m.sem("rl_ready")
            hm_ready = m.sem("hm_ready")
            used = m.sem("used")
            tail = Tail(m)
            block = ctx.enter_context(nc.Block())
            N = K6 * HC6

            @block.sync
            def _(sp):
                m.start(sp)
                sp.dma_start(w1[:, :, :], dram["w_c_1"].rearrange("p (a c) -> p a c", c=P)).then_inc(w_in, 16)
                sp.dma_start(w2[:, :, :], dram["w_c_2"].rearrange("(a p) d -> p a d", p=P)).then_inc(w_in, 16)
                sp.dma_start(b1[:, :], dram["w_c_b1"]).then_inc(w_in, 16)
                sp.dma_start(b2[:, :], dram["w_c_b2"]).then_inc(w_in, 16)
                sp.dma_start(pick[:, :, :], dram["c_pick6"].rearrange("k (a c) -> k a c", c=P)).then_inc(w_in, 16)

            @block.tensor
            def _(pe):
                pe.wait_ge(w_in, 80)
                with pe.Fori(0, NB) as b:
                    sT = selT[:, bass.ts(b, S)]
                    for n in range(N + 1):
                        e = n // HC6
                        if n < N:
                            if n % HC6 == 0:
                                pe.wait_ge(hm_ready, AHEAD + b * N + max(n - HC6, 0))
                                apart(pe, chip)
                                pe.matmul(bank[:, 4 + e % 2, :], pick[:, e, :], sT, start=True, stop=True).then_inc(spread, 1)
                            pe.wait_ge(rl_ready, AHEAD + b * N + max(n - 1, 0))
                            apart(pe, chip)
                            pe.matmul(bank[:, n % 2, :], w1[:, n, :], chip.xT[:, bass.ts(b, S)], start=True, stop=True)\
                                .then_inc(h_made, 1)
                        if n == 0:
                            pe.wait_ge(tail.yT_ready, AHEAD + b)
                            apart(pe, chip)
                            pe.matmul(bank[:, 7, :], b2[:, :], sT, start=True, stop=False)
                        if n >= 1:
                            pe.wait_ge(hm_ready, AHEAD + b * N + n)
                            apart(pe, chip)
                            pe.matmul(bank[:, 7, :], w2[:, n - 1, :], hm[:, (n - 1) % 2, :], start=False, stop=(n == N))\
                                .then_inc(used, 1)
                    tail.tensor(pe, chip, b)

            @block.scalar
            def _(act):
                with act.Fori(0, NB) as b:
                    for n in range(N):
                        act.wait_ge(h_made, AHEAD + b * N + n + 1)
                        act.wait_ge(hm_ready, AHEAD + b * N + max(n - 1, 0))
                        act.activation(rl[:, n % 2, :], bank[:, n % 2, :], ACT.Relu, bias=b1[:, n:n + 1]).then_inc(rl_ready, 1)
                    act.wait_ge(used, AHEAD + b * N + N)
                    tail.scalar(act, chip, b)

            @block.vector
            def _(dve):
                with dve.Fori(0, NB) as b:
                    for n in range(N):
                        e = n // HC6
                        dve.wait_ge(rl_ready, AHEAD + b * N + n + 1)
                        dve.wait_ge(used, AHEAD + b * N + max(n - 1, 0))
                        dve.wait_ge(spread, AHEAD + b * K6 + e + 1)
                        dve.tensor_tensor(hm[:, n % 2, :], rl[:, n % 2, :], bank[:, 4 + e % 2, :], ALU.mult).then_inc(hm_ready, 1)
                    tail.vector(dve, chip, b)


class Tail:

    def __init__(self, m):
        self.yT = m.sb("yT", [P, S])
        self.yT_ready = m.sem("yT_ready")
        self.y_turned = m.sem("y_turned")
        self.y_added = m.sem("y_added")

    def scalar(self, act, chip, b, bias=None):
        act.wait_ge(self.y_turned, AHEAD + b)
        if bias is None:
            act.activation(self.yT[:, :], chip.bank[:, 7, :], ACT.Copy).then_inc(self.yT_ready, 1)
        else:
            act.activation(self.yT[:, :], chip.bank[:, 7, :], ACT.Identity, bias=bias).then_inc(self.yT_ready, 1)

    def tensor(self, pe, chip, b):
        pe.wait_ge(self.yT_ready, AHEAD + b + 1)
        pe.wait_ge(self.y_added, AHEAD + b)
        apart(pe, chip)
        for t in range(TT):
            ins = pe.transpose(chip.bank[:, 6, t * P:(t + 1) * P], self.yT[:, t * P:(t + 1) * P], chip.ident[:, :])
        ins.then_inc(self.y_turned, 1)

    def vector(self, dve, chip, b):
        dve.wait_ge(self.y_turned, AHEAD + b + 1)
        xb = chip.x[:, bass.ts(b, TT), :]
        dve.tensor_tensor(xb, xb, chip.bank[:, 6, :].rearrange("p (t d) -> p t d", d=D), ALU.add).then_inc(self.y_added, 1)


NE8 = 16
G8 = 4
EG = NE8 // G8
NP8 = NE8 // 2


def grouped_experts(chip):
    nc, dram, bank, ident = chip.nc, chip.dram, chip.bank, chip.ident
    norm_stage(chip, "gn")
    with ExitStack() as outer:
        mo = Scope(chip, "g", outer)
        combT = mo.sb("combT", [NE8, NB * S])
        with ExitStack() as ctx:
            m = Scope(chip, "gr", ctx)
            gw = m.sb("gw", [P, NE8])
            gb = m.sb("gb", [P, NE8])
            rev = m.sb("rev", [P, D])
            SH = [P, NT, NE8]
            lg = m.sb("lg", SH)
            pr = m.sb("pr", SH)
            tmp = m.sb("tmp", SH)
            oh = m.sb("oh", SH)
            oh2 = m.sb("oh2", SH)
            duo = m.sb("duo", [P, NT * G8, 6])
            gs = m.sb("gs", [P, NT, G8])
            gt = m.sb("gt", [P, NT, G8])
            g1 = m.sb("g1", [P, NT, G8])
            g2 = m.sb("g2", [P, NT, G8])
            comb = m.sb("comb", SH)
            red = m.sb("red", [P, 4, NT])
            w_in = m.dma_sem("w_in")
            made = m.sem("made")
            dve_step = m.sem("dve_step")
            shifted = m.sem("shifted")
            e_ready = m.sem("e_ready")
            comb_ready = m.sem("comb_ready")
            turned = m.sem("turned")
            kept = m.sem("kept")
            block = ctx.enter_context(nc.Block())

            @block.sync
            def _(sp):
                m.start(sp)
                sp.dma_start(gw[:, :], dram["w_g_g"]).then_inc(w_in, 16)
                sp.dma_start(gb[:, :], dram["w_g_gb"].partition_broadcast(P)).then_inc(w_in, 16)
                sp.dma_start(rev[:, :], dram["c_rev"]).then_inc(w_in, 16)

            @block.tensor
            def _(pe):
                pe.wait_ge(w_in, 48)
                for n in range(NT):
                    ins = pe.matmul(bank[:, 0, n * NE8:(n + 1) * NE8], chip.xT[:, n * P:(n + 1) * P], gw[:, :],
                                    start=True, stop=True)
                ins.then_inc(made, 1)
                pe.wait_ge(comb_ready, AHEAD + 1)
                for b in range(NB):
                    if b >= 2:
                        pe.wait_ge(kept, AHEAD + b - 1)
                    for t in range(TT):
                        ins = pe.transpose(bank[0:NE8, 3 + b % 2, t * P:(t + 1) * P], comb[:, b * TT + t, :], ident[:, :])
                    ins.then_inc(turned, 1)

            @block.scalar
            def _(act):
                act.wait_ge(shifted, AHEAD + 1)
                act.activation(pr[:, :, :], lg[:, :, :], ACT.Exp).then_inc(e_ready, 1)
                for b in range(NB):
                    act.wait_ge(turned, AHEAD + b + 1)
                    act.activation(combT[:, b * S:(b + 1) * S], bank[0:NE8, 3 + b % 2, :], ACT.Copy).then_inc(kept, 1)

            @block.vector
            def _(dve):
                dve.wait_ge(w_in, 48)
                link = linker(dve, dve_step, 0, 33)

                def along(v, n=NE8):
                    return v.rearrange("p (t a) -> p t a", a=1).to_broadcast([P, NT, n])

                dve.wait_ge(made, AHEAD + 1)
                link(dve.tensor_reduce(red[:, 0, :], bank[:, 0, :].rearrange("p (t e) -> p t e", e=NE8), AX.X, ALU.max))
                dve.tensor_tensor(lg[:, :, :], bank[:, 0, :].rearrange("p (t e) -> p t e", e=NE8), along(red[:, 0, :]),
                                  ALU.subtract).then_inc(shifted, 1)
                dve.wait_ge(e_ready, AHEAD + 1)
                link(dve.tensor_reduce(red[:, 1, :], pr[:, :, :], AX.X, ALU.add))
                link(dve.reciprocal(red[:, 1, :], red[:, 1, :]))
                link(dve.tensor_tensor(pr[:, :, :], pr[:, :, :], along(red[:, 1, :]), ALU.mult))
                link(dve.tensor_tensor(lg[:, :, :], pr[:, :, :],
                                       gb[:, :].rearrange("p (a e) -> p a e", a=1).to_broadcast(SH), ALU.add))
                four = lg[:, :, :].rearrange("p t (g e) -> p (t g) e", e=EG)
                dve.tensor_tensor(duo[:, :, 0:3], four[:, :, 0:3], four[:, :, 1:4], ALU.add)
                dve.tensor_tensor(duo[:, :, 3:5], four[:, :, 0:2], four[:, :, 2:4], ALU.add)
                link(dve.tensor_tensor(duo[:, :, 5:6], four[:, :, 0:1], four[:, :, 3:4], ALU.add))
                link(dve.tensor_reduce(gs[:, :, :].rearrange("p t g -> p (t g)"), duo[:, :, :], AX.X, ALU.max))
                GS = [P, NT, G8]
                first_of_top(dve, link, gs[:, :, :], red[:, 0, :], rev[:, 0:G8], gt[:, :, :], red[:, 1, :], g1[:, :, :], GS)
                link(dve.scalar_tensor_tensor(gs[:, :, :], g1[:, :, :], NEG, gs[:, :, :], ALU.mult, ALU.add))
                first_of_top(dve, link, gs[:, :, :], red[:, 0, :], rev[:, 0:G8], gt[:, :, :], red[:, 1, :], g2[:, :, :], GS)
                link(dve.tensor_tensor(g1[:, :, :], g1[:, :, :], g2[:, :, :], ALU.add))
                link(dve.tensor_scalar(gt[:, :, :], g1[:, :, :], -1.0, -NEG, ALU.add, ALU.mult))

                def over_experts(v):
                    return v.rearrange("p t (g a) -> p (t g) a", a=1).to_broadcast([P, NT * G8, EG])

                link(dve.tensor_tensor(four, four, over_experts(gt[:, :, :]), ALU.add))
                first_of_top(dve, link, lg[:, :, :], red[:, 0, :], rev[:, 0:NE8], tmp[:, :, :], red[:, 1, :], oh[:, :, :], SH)
                link(dve.scalar_tensor_tensor(lg[:, :, :], oh[:, :, :], 2 * NEG, lg[:, :, :], ALU.mult, ALU.add))
                first_of_top(dve, link, lg[:, :, :], red[:, 0, :], rev[:, 0:NE8], tmp[:, :, :], red[:, 1, :], oh2[:, :, :], SH)
                link(dve.tensor_tensor(oh[:, :, :], oh[:, :, :], oh2[:, :, :], ALU.add))
                dve.tensor_tensor(comb[:, :, :], oh[:, :, :], pr[:, :, :], ALU.mult).then_inc(comb_ready, 1)
                link.check()

        with ExitStack() as ctx:
            m = Scope(chip, "gx", ctx)
            N = NP8 + 1
            w1 = m.sb("w1", [P, N, P])
            w3 = m.sb("w3", [P, N, P])
            w2 = m.sb("w2", [P, N, D])
            cols = m.sb("cols", [P, 2 * N + 1])
            b2 = m.sb("b2", [NE8, D])
            pick = m.sb("pick", [NE8, NP8, P])
            si = m.sb("si", [P, 2, S])
            hm = m.sb("hm", [P, 2, S])
            w_in = m.dma_sem("w_in")
            h_made = m.sem("h_made")
            si_ready = m.sem("si_ready")
            dve_step = m.sem("dve_step")
            hm_ready = m.sem("hm_ready")
            used = m.sem("used")
            tail = Tail(m)
            block = ctx.enter_context(nc.Block())

            @block.sync
            def _(sp):
                m.start(sp)
                sp.dma_start(w1[:, :, :], dram["w_g_1"].rearrange("p (a c) -> p a c", c=P)).then_inc(w_in, 16)
                sp.dma_start(w3[:, :, :], dram["w_g_3"].rearrange("p (a c) -> p a c", c=P)).then_inc(w_in, 16)
                sp.dma_start(w2[:, :, :], dram["w_g_2"].rearrange("(a p) d -> p a d", p=P)).then_inc(w_in, 16)
                sp.dma_start(cols[:, :], dram["w_g_cols"]).then_inc(w_in, 16)
                sp.dma_start(b2[:, :], dram["w_g_b2"]).then_inc(w_in, 16)
                sp.dma_start(pick[:, :, :], dram["c_pick8"].rearrange("k (a c) -> k a c", c=P)).then_inc(w_in, 16)

            @block.tensor
            def _(pe):
                pe.wait_ge(w_in, 96)
                with pe.Fori(0, NB) as b:
                    cT = combT[:, bass.ts(b, S)]
                    xb = chip.xT[:, bass.ts(b, S)]
                    for n in range(N + 1):
                        if n < N:
                            o = 3 * (n % 2)
                            pe.wait_ge(hm_ready, AHEAD + b * N + max(n - 1, 0))
                            apart(pe, chip)
                            ins = pe.matmul(bank[:, o, :], w1[:, n, :], xb, start=True, stop=True)
                            ins = pe.matmul(bank[:, o + 1, :], w3[:, n, :], xb, start=True, stop=True)
                            if n < NP8:
                                ins = pe.matmul(bank[:, o + 2, :], pick[:, n, :], cT, start=True, stop=True)
                            ins.then_inc(h_made, 1)
                        if n == 0:
                            pe.wait_ge(tail.yT_ready, AHEAD + b)
                            apart(pe, chip)
                            pe.matmul(bank[:, 7, :], b2[:, :], cT, start=True, stop=False)
                        if n >= 1:
                            pe.wait_ge(hm_ready, AHEAD + b * N + n)
                            apart(pe, chip)
                            pe.matmul(bank[:, 7, :], w2[:, n - 1, :], hm[:, (n - 1) % 2, :], start=False, stop=(n == N))\
                                .then_inc(used, 1)
                    tail.tensor(pe, chip, b)

            @block.scalar
            def _(act):
                with act.Fori(0, NB) as b:
                    for n in range(N):
                        act.wait_ge(h_made, AHEAD + b * N + n + 1)
                        act.wait_ge(hm_ready, AHEAD + b * N + max(n - 1, 0))
                        act.activation(si[:, n % 2, :], bank[:, 3 * (n % 2), :], ACT.Silu, bias=cols[:, n:n + 1]).then_inc(si_ready, 1)
                    act.wait_ge(used, AHEAD + b * N + N)
                    tail.scalar(act, chip, b, bias=cols[:, 2 * N:2 * N + 1])

            @block.vector
            def _(dve):
                with dve.Fori(0, NB) as b:
                    for n in range(N):
                        o = 3 * (n % 2)
                        dve.wait_ge(si_ready, AHEAD + b * N + n + 1)
                        dve.wait_ge(used, AHEAD + b * N + max(n - 1, 0))
                        ins = dve.scalar_tensor_tensor(hm[:, n % 2, :], bank[:, o + 1, :], cols[:, N + n:N + n + 1],
                                                       si[:, n % 2, :], ALU.add, ALU.mult)
                        if n < NP8:
                            ins.then_inc(dve_step, 1)
                            dve.wait_ge(dve_step, AHEAD + b * NP8 + n + 1)
                            ins = dve.tensor_tensor(hm[:, n % 2, :], hm[:, n % 2, :], bank[:, o + 2, :], ALU.mult)
                        ins.then_inc(hm_ready, 1)
                    tail.vector(dve, chip, b)


def program(nc, dram):
    with ExitStack() as ctx:
        chip = Chip(nc, dram, ctx)
        load_x(chip)
        small_head_attention(chip, "m0", dram["w_m0_qk"], dram["w_m0_v"], dram["w_m0_o"], dram["c_alibi"],
                           rope=dram["c_rope"], ob=dram["L0_attn_out_b"])
        local_layers(chip)
        batch_softmax_attention(chip)
        argmax_experts(chip)
        state_space(chip)
        capacity_experts(chip)
        small_head_attention(chip, "m3", dram["w_m3_qk"], dram["w_m3_v"], dram["w_m3_o"], None)
        grouped_experts(chip)
        store_x(chip)


def shape_constants():
    f = np.float32
    c = {}
    c["c_ident"] = np.eye(P, dtype=f)
    p = np.arange(P, dtype=f)[:, None]
    y = np.arange(S, dtype=f)[None, :]
    dist = p + (S - P) - y
    slopes = np.array([2.0 ** (-8.0 * (h + 1) / NH) for h in range(NH)], f)
    al = np.where(dist[None] < 0, f(NEG), -slopes[:, None, None] * dist[None] / f(ISQ)).astype(f)
    c["c_alibi"] = np.ascontiguousarray(al.reshape(G, HPG, P, S).transpose(0, 2, 1, 3)).reshape(G, P, HPG * S)
    half = D // 2
    freqs = (1.0 / f(10000.0) ** (np.arange(half, dtype=f) / f(half))).astype(f)
    ang = (np.arange(S, dtype=f)[None, :] * freqs[:, None]).astype(f)
    cos = np.concatenate([np.cos(ang), np.cos(ang)]).astype(f)
    sin = np.concatenate([-np.sin(ang), np.sin(ang)]).astype(f)
    rope = np.zeros((G, P, 2, S), f)
    for g in range(G):
        for j in range(HPG):
            for a, tab in enumerate((cos, sin)):
                rope[g, 32 * j:32 * j + HD, a] = tab[(g * HPG + j) * HD:(g * HPG + j + 1) * HD]
    c["c_rope"] = rope.reshape(G, P, 2 * S)
    c["c_log1p_dist"] = np.log1p(np.maximum(dist, 0)).astype(f)
    c["c_causal"] = np.where(dist < 0, f(NEG), f(0)).astype(f)
    ch = np.arange(0, LD, 2, dtype=f)
    inv_freq = (1.0 / f(10000.0) ** (ch / f(LD))).astype(f)
    t = np.arange(S, dtype=f)
    fr = (t[:, None] * inv_freq[None, :]).astype(f)
    bs = ((ch + f(0.4 * LD)) / f(1.4 * LD)).astype(f)
    power = ((t - S // 2) / f(WIN // 2)).astype(f)
    sc = (bs[None, :] ** power[:, None]).astype(f)
    two = lambda a: np.concatenate([a, a], 1)
    sgn = np.concatenate([-np.ones(LD // 2, f), np.ones(LD // 2, f)])[None, :]
    co, si, sc = two(np.cos(fr)), two(np.sin(fr)) * sgn, two(sc)
    inv = (f(1) / sc).astype(f)
    c["c_lrot"] = np.concatenate([np.concatenate([a.T, a.T]) for a in (co * sc, si * sc, co * inv, si * inv)], 1).astype(f)
    i_, y_ = np.arange(P)[:, None], np.arange(NK)[None, :]
    back = i_ - (y_ - WIN)
    ok = (back >= 0) & (back <= WIN)
    c["c_lmask"] = np.concatenate([np.where(ok & (y_ >= WIN), 0, NEG), np.where(ok, 0, NEG)], 1).astype(f)
    c["c_pair"] = np.repeat(np.eye(2, dtype=f), LD, 0)
    c["c_rev"] = np.repeat((D - np.arange(D, dtype=f))[None, :], P, 0)
    k_, q_ = np.arange(P)[:, None], np.arange(P)[None, :]
    c["c_upto"] = (k_ <= q_).astype(f)
    c["c_pick6"] = np.repeat(np.eye(K6, dtype=f), P, 1)
    c["c_pick8"] = np.repeat(np.eye(NE8, dtype=f), P // 2, 1)
    c["c_pick5"] = np.repeat(np.eye(SH5, dtype=f), P, 1)
    return c


def padded_heads(w):
    out = np.zeros((G, D, P), w.dtype)
    for g in range(G):
        for j in range(HPG):
            h = g * HPG + j
            out[g, :, 32 * j:32 * j + HD] = w[:, h * HD:(h + 1) * HD]
    return out


def lay_out(inp):
    a = {}
    a["x"] = inp["L0_attn_x"].reshape(NB * S, D)
    half = np.concatenate([np.arange(D // 2, D), np.arange(0, D // 2)])
    wq, wk = inp["L0_attn_wq"].T, inp["L0_attn_wk"].T
    a["w_m0_qk"] = np.concatenate([padded_heads(wq), padded_heads(wq[:, half]),
                                   padded_heads(wk), padded_heads(wk[:, half])], axis=2)
    a["w_m0_v"] = inp["L0_attn_wv"].T
    a["w_m0_o"] = inp["L0_attn_out_w"].T
    a["L0_attn_out_b"] = inp["L0_attn_out_b"]
    W = inp["L0_ffn_Wqkv"]
    inner = LH * LD
    sw = np.concatenate([np.arange(LD // 2, LD), np.arange(0, LD // 2)])
    swap = (np.arange(LH)[:, None] * LD + sw[None, :]).reshape(-1)
    q, k, v = W[:, :, :inner], W[:, :, inner:2 * inner], W[:, :, 2 * inner:]
    grp = lambda w: w.reshape(DEPTH, D, NG, P)
    a["w_l_qk"] = np.stack([grp(q), grp(q[:, :, swap]), grp(k), grp(k[:, :, swap])], 3).reshape(DEPTH, D, NG * 4 * P)
    a["w_l_v"] = v
    a["w_l_o"] = inp["L0_ffn_Wo"]
    pad = HC * P - HID
    halves = lambda w: np.concatenate([np.pad(w[..., :HID], [(0, 0)] * (w.ndim - 1) + [(0, pad)]),
                                       np.pad(w[..., HID:], [(0, 0)] * (w.ndim - 1) + [(0, pad)])], -1)
    a["w_l_1"] = halves(inp["L0_ffn_W1"])
    a["w_l_2"] = np.pad(inp["L0_ffn_W2"], ((0, 0), (0, pad), (0, 0)))
    qs, ks = inp["L0_ffn_q_scale"], inp["L0_ffn_k_scale"]
    col = lambda w: w.reshape(DEPTH, -1, P).transpose(0, 2, 1)
    dup = lambda w: np.concatenate([w, w], 1)
    a["w_l_cols"] = np.concatenate([col(dup(qs)), col(dup(qs[:, sw])), col(dup(ks)), col(dup(ks[:, sw])),
                                    col(inp["L0_ffn_ln_g"]), col(inp["L0_ffn_ln_b"]), col(inp["L0_ffn_b2"]),
                                    col(inp["L0_ffn_b2"]), col(halves(inp["L0_ffn_b1"]))], 2)
    a["w_b_v"] = inp["L1_attn_Wv"].T
    a["w_b_qk"] = np.concatenate([inp["L1_attn_Wq"].T, inp["L1_attn_Wk"].T], 1)
    a["w_e_g"] = inp["L1_ffn_Wg"]
    a["w_e_e"] = inp["L1_ffn_We"].transpose(1, 0, 2).reshape(D, -1)
    a["w_e_be"] = inp["L1_ffn_be"].reshape(1, -1)
    a["w_e_bg"] = inp["L1_ffn_bg"]
    wa = inp["L3_attn_w_attn"]
    a["w_m3_qk"] = np.concatenate([padded_heads(wa[:, :D]), padded_heads(wa[:, D:2 * D])], axis=2)
    a["w_m3_v"] = wa[:, 2 * D:]
    a["w_m3_o"] = inp["L3_attn_w_proj"]
    a["L3_attn_decay_raw"] = inp["L3_attn_decay_raw"]
    w1 = np.concatenate([inp["L2_ffn_w1"], inp["L2_ffn_ow1"][None]])
    w2 = np.concatenate([inp["L2_ffn_w2"], inp["L2_ffn_ow2"][None]])
    a["w_c_1"] = w1.transpose(1, 0, 2).reshape(D, K6 * H6)
    a["w_c_2"] = w2.reshape(K6 * H6, D)
    a["w_c_b1"] = np.concatenate([inp["L2_ffn_b1"], inp["L2_ffn_ob1"][None]]).reshape(K6 * HC6, P).T
    a["w_c_b2"] = np.concatenate([inp["L2_ffn_b2"], inp["L2_ffn_ob2"][None]])
    a["w_c_r"] = inp["L2_ffn_router_w"]
    a["w_c_rb"] = inp["L2_ffn_router_b"]
    pairs = lambda w, s: np.concatenate([w.transpose(1, 0, 2).reshape(D, NE8 * (P // 2)), s], 1)
    a["w_g_1"] = pairs(inp["L3_ffn_We1"], inp["L3_ffn_ws1"])
    a["w_g_3"] = pairs(inp["L3_ffn_We3"], inp["L3_ffn_ws3"])
    a["w_g_2"] = np.concatenate([inp["L3_ffn_We2"].reshape(-1, D), inp["L3_ffn_ws2"]])
    rows = lambda e, s: np.concatenate([e.reshape(-1), s]).reshape(-1, P).T
    a["w_g_cols"] = np.concatenate([rows(inp["L3_ffn_be1"], inp["L3_ffn_bs1"]), rows(inp["L3_ffn_be3"], inp["L3_ffn_bs3"]),
                                    inp["L3_ffn_bs2"][:, None]], 1)
    a["w_g_b2"] = inp["L3_ffn_be2"]
    a["w_g_g"] = inp["L3_ffn_gate_w"].T
    a["w_g_gb"] = inp["L3_ffn_gate_b"]
    wi = inp["L2_attn_in_proj_w"].T
    a["w_s_z"] = wi[:, :DI]
    a["w_s_x"] = wi[:, DI:DI + XC * P]
    a["w_s_dt"] = wi[:, DI + XC * P:]
    a["w_s_o"] = inp["L2_attn_out_proj_w"].T
    a["w_s_taps"] = np.concatenate([inp["L2_attn_conv_w"], inp["L2_attn_conv_b"][:, None]], 1)
    a["w_s_rows"] = np.concatenate([inp["L2_attn_" + n] for n in ("A_log", "dt_bias", "D_skip", "norm_w", "ln_w", "ln_b")])
    return a


def kernel(**inputs):
    import concourse.bacc as _bacc
    from concourse.bass_utils import run_bass_kernel_spmd as _run

    nc = _bacc.Bacc("TRN2", target_bir_lowering=False, num_devices=1)
    arrays, dram = {}, {}
    inputs = {k: np.asarray(v) for k, v in inputs.items()}
    for name, a in {**lay_out(inputs), **shape_constants()}.items():
        a = np.ascontiguousarray(a)
        arrays[f"in_{name}"] = a
        dram[name] = nc.dram_tensor(f"in_{name}", a.shape, mybir.dt.from_np(a.dtype), kind="ExternalInput").ap()
    dram["out"] = nc.dram_tensor("out_x", (NB * S, D), F32, kind="ExternalOutput").ap()
    program(nc, dram)
    r = _run(nc, [arrays], core_ids=[0])
    return r.results[0]["out_x"].reshape(NB, S, D)
```
